# Optimizing a Trainium2 kernel written in Bass

```python
import numpy as np
import jax
import jax.numpy as jnp

def _softmax(x, axis=-1):
    return jax.nn.softmax(x, axis=axis)

def _gelu(x):
    return jax.nn.gelu(x, approximate=True)

def _silu(x):
    return jax.nn.silu(x)

def _sigmoid(x):
    return jax.nn.sigmoid(x)

def _layernorm(x, axis=-1, eps=1e-05):
    m = jnp.mean(x, axis=axis, keepdims=True)
    v = jnp.var(x, axis=axis, keepdims=True)
    return (x - m) / jnp.sqrt(v + eps)

def _scatter_add(tgt, idx, src, axis=0):
    return tgt.at[idx].add(src)

def _segment_sum(src, seg, n):
    return jax.ops.segment_sum(src, seg, n)
kernel_name = 'mk_seq_preln_d1_jaxref_r8_1b1e2f'

def setup_inputs(seed: int=0):
    np.random.seed(seed)
    _w = jnp.asarray

    def _L0_attn_setup():
        import jax, jax.numpy as jnp
        import numpy as np
        B, T, D = (2, 256, 128)
        H = 16
        HD = D // H
        key = jax.random.key(seed)
        ks = jax.random.split(key, 6)
        s = D ** (-0.5)
        x = jax.random.normal(ks[0], (B, T, D), dtype=jnp.float32)
        Wq = jax.random.normal(ks[1], (D, D), dtype=jnp.float32) * s
        Wk = jax.random.normal(ks[2], (D, D), dtype=jnp.float32) * s
        Wv = jax.random.normal(ks[3], (D, D), dtype=jnp.float32) * s
        Wo = jax.random.normal(ks[4], (D, D), dtype=jnp.float32) * s
        bo = jnp.zeros((D,), dtype=jnp.float32)
        return {'x': x, 'Wq': Wq, 'Wk': Wk, 'Wv': Wv, 'Wo': Wo, 'bo': bo}
    _L0_attn_in = _L0_attn_setup()

    def _L0_ffn_setup():
        import jax, jax.numpy as jnp
        import numpy as np
        TEMPERATURE = 1.0
        TOPK = 2
        key = jax.random.key(seed)
        ks = jax.random.split(key, 6)
        S, B, H, F, E = (256, 4, 128, 512, 8)
        x = jax.random.normal(ks[0], (S, B, H), dtype=jnp.float32)
        gate_w = jax.random.normal(ks[1], (E, H), dtype=jnp.float32) * (1.0 / np.sqrt(H))
        w1 = jax.random.normal(ks[2], (E, H, F), dtype=jnp.float32) * (1.0 / np.sqrt(H))
        b1 = jnp.zeros((E, F), dtype=jnp.float32)
        w2 = jax.random.normal(ks[3], (E, F, H), dtype=jnp.float32) * (1.0 / np.sqrt(F))
        b2 = jnp.zeros((E, H), dtype=jnp.float32)
        return {'x': x, 'gate_w': gate_w, 'w1': w1, 'b1': b1, 'w2': w2, 'b2': b2}
    _L0_ffn_in = _L0_ffn_setup()
    _d = {'L0_attn_x': _L0_attn_in['x'], 'L0_attn_Wq': _L0_attn_in['Wq'], 'L0_attn_Wk': _L0_attn_in['Wk'], 'L0_attn_Wv': _L0_attn_in['Wv'], 'L0_attn_Wo': _L0_attn_in['Wo'], 'L0_attn_bo': _L0_attn_in['bo'], 'L0_ffn_gate_w': _L0_ffn_in['gate_w'], 'L0_ffn_w1': _L0_ffn_in['w1'], 'L0_ffn_b1': _L0_ffn_in['b1'], 'L0_ffn_w2': _L0_ffn_in['w2'], 'L0_ffn_b2': _L0_ffn_in['b2']}
    _x0 = _d['L0_attn_x']
    _d['L0_attn_x'] = jax.random.normal(jax.random.fold_in(jax.random.key(seed), 1), (8, 512, 128), dtype=_x0.dtype)
    del _x0
    return _d

def reference(L0_attn_x, L0_attn_Wq, L0_attn_Wk, L0_attn_Wv, L0_attn_Wo, L0_attn_bo, L0_ffn_gate_w, L0_ffn_w1, L0_ffn_b1, L0_ffn_w2, L0_ffn_b2):

    def _L0_attn_ref(x, Wq, Wk, Wv, Wo, bo):
        import jax, jax.numpy as jnp
        import numpy as np
        B, T, D = (2, 256, 128)
        H = 16
        HD = D // H
        b, t, _ = x.shape
        scale = HD ** (-0.5)
        q = (x @ Wq).reshape(b, t, H, HD)
        k = (x @ Wk).reshape(b, t, H, HD)
        v = (x @ Wv).reshape(b, t, H, HD)
        s = jnp.einsum('bqhd,bkhd->bhqk', q * scale, k)
        causal = jnp.tril(jnp.ones((t, t), dtype=bool))
        s = jnp.where(causal[None, None], s, -jnp.inf)
        p = jax.nn.softmax(s, axis=-1)
        o = jnp.einsum('bhqk,bkhd->bqhd', p, v).reshape(b, t, H * HD)
        return o @ Wo + bo

    def _L0_ffn_ref(x, gate_w, w1, b1, w2, b2):
        import jax, jax.numpy as jnp
        import numpy as np
        TEMPERATURE = 1.0
        TOPK = 2
        s, b, h = x.shape
        x_flat = x.reshape(s * b, h)
        logits = x_flat @ gate_w.T
        probs = jax.nn.softmax(logits / TEMPERATURE, axis=-1)
        topk_probs, topk_idx = jax.lax.top_k(probs, TOPK)
        hidden = jax.nn.relu(jnp.einsum('th,ehf->tef', x_flat, w1) + b1[None])
        all_out = jnp.einsum('tef,efh->teh', hidden, w2) + b2[None]
        gathered = jnp.take_along_axis(all_out, topk_idx[:, :, None], axis=1)
        y_flat = jnp.sum(gathered * topk_probs[:, :, None], axis=1)
        return y_flat.reshape(s, b, h)
    x = L0_attn_x
    x = x + _L0_attn_ref(_layernorm(x, axis=-1), L0_attn_Wq, L0_attn_Wk, L0_attn_Wv, L0_attn_Wo, L0_attn_bo)
    x = x + _L0_ffn_ref(_layernorm(x, axis=-1), L0_ffn_gate_w, L0_ffn_w1, L0_ffn_b1, L0_ffn_w2, L0_ffn_b2)
    return x

_drawn_inputs = setup_inputs


def setup_inputs(seed=0):
    import zlib

    import numpy as np

    out = dict(_drawn_inputs(seed))
    spreads = {'L0_attn_bo': (0.0, 0.1), 'L0_ffn_b1': (0.0, 0.274), 'L0_ffn_b2': (0.0, 0.1)}
    factors = {}
    for name, (base, spread) in spreads.items():
        noise = np.random.default_rng([zlib.crc32(name.encode()), seed]).standard_normal(out[name].shape)
        drawn = base * np.exp(spread * noise) if base else spread * noise
        out[name] = jnp.asarray(drawn.astype(out[name].dtype))
    for name, factor in factors.items():
        out[name] = (out[name] * factor).astype(out[name].dtype)
    return out
```

```python
from contextlib import ExitStack

import concourse.bass as bass
from concourse import mybir

F32 = mybir.dt.float32
BF16 = mybir.dt.bfloat16
U32 = mybir.dt.uint32
I32 = mybir.dt.int32
ALU = mybir.AluOpType
ACT = mybir.ActivationFunctionType
AX_X = mybir.AxisListType.X

P = 128
BATCH, T, D = 8, 512, 128
HEADS = 16
HD = D // HEADS
CH = T // P
TILES = BATCH * CH
GROUPS = 4
GH = HEADS // GROUPS
STEPS = BATCH * GROUPS
PARTS = 3
PAIRS = PARTS * PARTS
QK_ROWS = 96
SHIFT0 = 96
SHIFTS = PARTS * GH
ST_ROWS = SHIFT0 + SHIFTS
VW = 32
SCALE = float(HD) ** -0.5
EPS = 1e-5
NEG = -3.0e38
E, F, TOPK = 8, 512, 2
FC = F // P
HALVES = 2
HTILES = TILES // HALVES
HPAIRS = BATCH // HALVES // 2
SLOTS = (HTILES * P * TOPK + E * (P - 1)) // P
EVEN, ODD = (SLOTS + 1) // 2, SLOTS // 2

SCORE_TASKS = (
    [[(3, h, 0)] for h in range(GH)]
    + [[(2, h, 0), (0, h, 3 * P)] for h in range(GH)]
    + [[(1, h, 0), (1, h + 1, 2 * P)] for h in range(0, GH, 2)]
)
NSCORE = len(SCORE_TASKS)
PROB_TASKS = [(0, 0, 2), (0, 2, 2), (1, 0, 2), (1, 2, 2), (2, 0, 4), (3, 0, 4)]
NPROB = len(PROB_TASKS)
PT0 = [0, GH * 4 * P, GH * 7 * P, GH * 9 * P]
PT_COLS = GH * 10 * P


def at_least(eng, sem, n):
    if not isinstance(n, int) or n > 0:
        eng.wait_ge(sem, n)


def repeat(eng, n, body):
    body(0)
    with eng.Fori(1, n) as i:
        body(i)


def layer(nc, x, wq, wk, wv, wo, bo, gate_w, w1, b1, w2, b2, out):
    with ExitStack() as ctx:
        def sb(name, shape, dt=F32):
            return ctx.enter_context(nc.sbuf_tensor(name, shape, dt))

        def ps(name, shape):
            return ctx.enter_context(nc.psum_tensor(name, shape, F32))

        def sem(name):
            return ctx.enter_context(nc.semaphore(name))

        def sems(name, n):
            return [sem(f"{name}{i}") for i in range(n)]

        x_all = sb("x_all", [P, TILES, D])
        stats = sb("stats", [P, TILES, 6])
        mean = sb("mean", [P, TILES])
        rstd = sb("rstd", [P, TILES])
        lnt = sb("lnt", [P, 4, TILES])
        wq_sb = sb("wq_sb", [P, D])
        wk_sb = sb("wk_sb", [P, D])
        wv_sb = sb("wv_sb", [P, D])
        wo_sb = sb("wo_sb", [P, D])
        wqp = sb("wqp", [P, D])
        wkp = sb("wkp", [P, D])
        bo_b = sb("bo_b", [P, D])
        identf = sb("identf", [P, P])
        identb = sb("identb", [P, P], BF16)
        mask_qk = sb("mask_qk", [P, P], BF16)
        mask_kq = sb("mask_kq", [P, P], BF16)
        own = sb("own", [P, GH], BF16)
        xn = sb("xn", [P, 2, CH, D])
        xnT = sb("xnT", [P, 2, T])
        qf = sb("qf", [P, 2, T])
        kf = sb("kf", [P, 2, T])
        qrest = sb("qrest", [P, T])
        krest = sb("krest", [P, T])
        qparts = sb("qparts", [P, 2, PARTS, T], BF16)
        kparts = sb("kparts", [P, 2, PARTS, T], BF16)
        v_all = sb("v_all", [P, TILES, D])
        Qs = sb("Qs", [P, GROUPS, GH, T], BF16)
        Ks = sb("Ks", [P, GROUPS, GH, T], BF16)
        Vs = sb("Vs", [P, GROUPS, CH, GH, VW])
        PT = sb("PT", [P, PT_COLS])
        nmax = sb("nmax", [P, 2, CH, GH])
        nrest = sb("nrest", [P, 2, CH, GH])
        nparts = sb("nparts", [P, 2, CH, PARTS, GH], BF16)
        shiftT = sb("shiftT", [SHIFTS, 2, T], BF16)
        Os = sb("Os", [P, 2, T])
        rsum = sb("rsum", [P, CH, GH])
        attn = sb("attn", [P, TILES, D])
        w1_sb = sb("w1_sb", [P, E, F])
        w2_sb = sb("w2_sb", [P, E, FC, D])
        b2_b = sb("b2_b", [P, E * D])
        gate_rows = sb("gate_rows", [E, D])
        gateT = sb("gateT", [P, E])
        b1_rows = sb("b1_rows", [E * FC, P])
        b1T = sb("b1T", [P, E * FC])
        xn2 = sb("xn2", [P, HTILES, D])
        zeros = attn[:, 0:8, :].rearrange("p t d -> p (t d)")
        tri = sb("tri", [P, P], BF16)
        onesb = sb("onesb", [P, P], BF16)
        ints = sb("ints", [P, E + HTILES + SLOTS], I32)
        cst = sb("cst", [P, E + HTILES + SLOTS])
        back = cst[:, 0:E]
        starts = cst[:, E:E + HTILES]
        slot_no = cst[:, E + HTILES:]
        resets = sb("resets", [P, E, HTILES])
        ones_e = sb("ones_e", [P, E])
        lg, pr, oh1, oh2, rt = (sb(n, [P, HTILES, E]) for n in ("lg", "pr", "oh1", "oh2", "rt"))
        rmax, rz = sb("rmax", [P, HTILES]), sb("rz", [P, HTILES])
        picks = sb("picks", [P, E, HTILES], BF16)
        tot, inc, pos = (sb(n, [P, E, HTILES]) for n in ("tot", "inc", "pos"))
        need = sb("need", [P, E, HTILES])
        nt, ends, base = (sb(n, [P, E]) for n in ("nt", "ends", "base"))
        past = sb("past", [P, SLOTS, E])
        eidf = sb("eidf", [P, SLOTS])
        eid = sb("eid", [P, HALVES, SLOTS], I32)
        dstf = sb("dstf", [P, HTILES])
        place = sb("place", [P, HALVES, TOPK, HTILES], I32)
        wgt = sb("wgt", [P, HALVES, TOPK, HTILES])
        xs_t = Os[:, 0, 0:2 * D].rearrange("p (u d) -> p u d", u=2)
        xsT = Os[:, 0, 2 * D:4 * D].rearrange("p (u d) -> p u d", u=2)
        y_t = Os[:, 1, 0:2 * D].rearrange("p (u d) -> p u d", u=2)
        h_sb = qf
        hT = kf
        yg = [attn, v_all]
        xs_dram = [nc.dram_tensor(f"sorted_x{i}", [SLOTS * P, D], F32, kind="Internal").ap() for i in range(HALVES)]
        ys_dram = [nc.dram_tensor(f"sorted_y{i}", [SLOTS * P, D], F32, kind="Internal").ap() for i in range(HALVES)]
        q_dram = nc.dram_tensor("q_parts", [BATCH, GROUPS, PARTS, HD * GH, T], BF16, kind="Internal").ap()
        k_dram = nc.dram_tensor("k_parts", [BATCH, GROUPS, PARTS, HD * GH, T], BF16, kind="Internal").ap()

        psS = ps("psS", [P, 2, 512])
        psT = ps("psT", [P, 4, 512])
        psO = ps("psO", [P, 512])
        psM = ps("psM", [P, 512])
        ps_v = [psO, psM]

        x_in, w_in = sem("x_in"), sem("w_in")
        wperm, consts, const_step = sem("wperm"), sem("consts"), sem("const_step")
        slots_set = sem("slots_set")
        ln = sem("ln")
        var_done, std_done = sem("var_done"), sem("std_done")
        xn_ready, xT_ready, xT_copied = sems("xn_ready", 2), sems("xT_ready", 2), sems("xT_copied", 2)
        qkv_ready, q_copied, k_copied, v_copied = (sems(n, 2) for n in ("qkv_ready", "q_copied", "k_copied", "v_copied"))
        qsplit, ksplit = sem("qsplit"), sem("ksplit")
        qsplit_done, ksplit_done = sems("qsplit_done", 2), sems("ksplit_done", 2)
        q_stored, k_stored = sems("q_stored", 2), sems("k_stored", 2)
        xb_done = sem("xb_done")
        qk_loaded, shift_loaded = sems("qk_loaded", GROUPS), sems("shift_loaded", GROUPS)
        v_loaded = sem("v_loaded")
        scores_ready, scores_used = sems("scores_ready", 2), sems("scores_used", 2)
        shift_step, shift_split = sem("shift_step"), sems("shift_split", 2)
        shiftT_ready, shiftT_copied = sem("shiftT_ready"), sem("shiftT_copied")
        prob_ready, prob_done = sems("prob_ready", 2), sems("prob_done", 2)
        pv_done = sems("pv_done", CH)
        heads_copied, headsT_ready, rsum_done, normed = (sem(n) for n in ("heads_copied", "headsT_ready", "rsum_done", "normed"))
        stage_done, aT_ready, aT_copied, o_ready, x2_done = (sems(n, 2) for n in ("stage_done", "aT_ready", "aT_copied", "o_ready", "x2_done"))
        out_done, pool_turn = sem("out_done"), sem("pool_turn")
        moe_in, smallT, smallT_copied = sem("moe_in"), sem("smallT"), sem("smallT_copied")
        zeros_set, xs_cleared = sem("zeros_set"), sem("xs_cleared")
        iotas, cst_done, sort_consts = sem("iotas"), sem("cst_done"), sem("sort_consts")
        xn2_ready, xn2_kept, xn2T_ready, xn2T_copied, logits_ready = (
            sems(n, 2) for n in ("xn2_ready", "xn2_kept", "xn2T_ready", "xn2T_copied", "logits_ready"))
        stats_done = sem("stats_done")
        lg_done, exp_done, picks_done, ranks_ready, routed = (
            sem(n) for n in ("lg_done", "exp_done", "picks_done", "ranks_ready", "routed"))
        scattered, gathered, combined = sems("scattered", HALVES), sems("gathered", HALVES), sems("combined", HALVES)
        xs_loaded, xs_turned, xsT_copied, h_ready, h_copied, hT_ready, relu_act, relu_dve, y_ready, y_copied, y_stored = (
            sems(n, 2) for n in ("xs_loaded", "xs_turned", "xsT_copied", "h_ready", "h_copied", "hT_ready",
                                 "relu_act", "relu_dve", "y_ready", "y_copied", "y_stored"))

        QK_LOADS = (PARTS + PAIRS) * 16
        STORES = GROUPS * 16
        CONSTS = 6

        block = ctx.enter_context(nc.Block())

        @block.sync
        def _(sp):
            x_v = x.rearrange("b (c p) d -> b p c d", p=P)
            for b in range(BATCH):
                sp.dma_start(x_all[:, b * CH:(b + 1) * CH, :], x_v[b]).then_inc(x_in, 16)
            for dst, src in ((wq_sb, wq), (wk_sb, wk), (wv_sb, wv), (wo_sb, wo)):
                sp.dma_start(dst[:, :], src).then_inc(w_in, 16)
            sp.dma_start(bo_b[:, :], bo.partition_broadcast(P)).then_inc(w_in, 16)

            sp.dma_start(gate_rows[:, :], gate_w).then_inc(moe_in, 16)
            sp.dma_start(b1_rows[:, :], b1.rearrange("e (c p) -> (e c) p", p=P)).then_inc(moe_in, 16)
            sp.dma_start(b2_b[:, :], b2.rearrange("e d -> (e d)").partition_broadcast(P)).then_inc(moe_in, 16)
            sp.dma_start(w1_sb[:, :, :], w1.rearrange("e h f -> h e f")).then_inc(moe_in, 16)
            sp.dma_start(w2_sb[:, :, :, :].rearrange("p e c d -> p (e c) d"),
                         w2.rearrange("e (c p) d -> p (e c) d", p=P)).then_inc(moe_in, 16)
            sp.wait_ge(zeros_set, 1)
            for half in range(HALVES):
                xs_v = xs_dram[half].rearrange("(p n) d -> p (n d)", p=P)
                for c0 in range(0, SLOTS, 8):
                    n = min(8, SLOTS - c0)
                    sp.dma_start(xs_v[:, c0 * D:(c0 + n) * D], zeros[:, 0:n * D]).then_inc(xs_cleared, 16)

            def body(pair):
                for u in range(2):
                    b = pair * 2 + u
                    for parts, dram, ready, stored in ((qparts, q_dram, qsplit_done, q_stored),
                                                       (kparts, k_dram, ksplit_done, k_stored)):
                        at_least(sp, ready[u], pair + 1)
                        for g in range(GROUPS):
                            sp.dma_start(dram[b, g].rearrange("i r t -> r i t"),
                                         parts[g * 32:(g + 1) * 32, u, :, :]).then_inc(stored[u], 16)

            repeat(sp, BATCH // 2, body)
            for s in q_stored + k_stored:
                sp.wait_ge(s, STORES * BATCH // 2)
            sp.wait_ge(slots_set, 1 + 2 * GROUPS)

            def load_qk(b, g):
                for a in range(PARTS):
                    sp.dma_start(Qs[a * 24:(a + 1) * 24, g, :, :].rearrange("r h t -> r (h t)"),
                                 q_dram[b, g].rearrange("i (d h) t -> (i d) (h t)", h=GH)).then_inc(qk_loaded[g], 16)
                    for i in range(PARTS):
                        r = (a * PARTS + i) * HD
                        sp.dma_start(Ks[r:r + HD, g, :, :].rearrange("r h t -> r (h t)"),
                                     k_dram[b, g, a].rearrange("(d h) t -> d (h t)", h=GH)).then_inc(qk_loaded[g], 16)

            def load_shift(s, g):
                sp.wait_ge(shiftT_copied, s + 1)
                for h in range(GH):
                    sp.dma_start(Qs[SHIFT0:SHIFT0 + SHIFTS, g, h, :], shiftT[:, g % 2, :]).then_inc(shift_loaded[g], 16)

            def step(b, g, last):
                s = b * GROUPS + g
                if not (last and g == GROUPS - 1):
                    load_shift(s + 1, (g + 1) % GROUPS)
                if not last:
                    sp.wait_ge(prob_ready[1], (s + 1) * (NPROB // 2))
                    load_qk(b + 1, g)

            for g in range(GROUPS):
                load_qk(0, g)
            load_shift(0, 0)
            with sp.Fori(0, BATCH - 1) as b:
                for g in range(GROUPS):
                    step(b, g, False)
            for g in range(GROUPS):
                step(BATCH - 1, g, True)

            def moe(half):
                def load(i, k, u):
                    at_least(sp, xs_turned[u], half * (EVEN, ODD)[u] + k)
                    sp.dma_start(xs_t[:, u, :], xs_dram[half][bass.ts(i, P), :]).then_inc(xs_loaded[u], 16)

                def store(i, k, u):
                    sp.wait_ge(y_copied[u], half * (EVEN, ODD)[u] + k + 1)
                    sp.dma_start(ys_dram[half][bass.ts(i, P), :], y_t[:, u, :]).then_inc(y_stored[u], 16)

                sp.wait_ge(scattered[half], TOPK * HTILES * 16)
                for i in range(4):
                    load(i, i // 2, i % 2)
                def body(k):
                    for u in range(2):
                        load(k * 2 + u + 4, k + 2, u)
                        store(k * 2 + u, k, u)

                repeat(sp, (SLOTS - 4) // 2, body)
                for i in range((SLOTS - 4) // 2 * 2, SLOTS):
                    if i + 4 < SLOTS:
                        load(i + 4, (i + 4) // 2, i % 2)
                    store(i, i // 2, i % 2)

            for half in range(HALVES):
                moe(half)
            o_v = out.rearrange("b (c p) d -> b p c d", p=P)
            for half in range(HALVES):
                for b in range(BATCH // HALVES):
                    sp.wait_ge(combined[half], (b + 1) * CH)
                    bb = half * (BATCH // HALVES) + b
                    sp.dma_start(o_v[bb], x_all[:, bb * CH:(bb + 1) * CH, :]).then_inc(out_done, 16)
            sp.wait_ge(out_done, 16 * BATCH)

        @block.gpsimd
        def _(pool):
            def own_wait():
                pool.sem_inc(pool_turn, 1)

            pool.memset(identf[:, :], 0.0).then_inc(const_step, 1)
            pool.memset(identb[:, :], 0.0).then_inc(const_step, 1)
            pool.memset(mask_qk[:, :], 0.0).then_inc(const_step, 1)
            pool.memset(mask_kq[:, :], 0.0).then_inc(const_step, 1)
            pool.memset(own[:, :], 0.0).then_inc(const_step, 1)
            pool.wait_ge(const_step, 5)
            for m in (identf, identb):
                pool.affine_select(out=m[:, :], in_=m[:, :], compare_op=ALU.not_equal, fill=1.0, base=0,
                                   pattern=[[-1, P]], channel_multiplier=1).then_inc(consts, 1)
            pool.affine_select(out=mask_qk[:, :], in_=mask_qk[:, :], compare_op=ALU.is_ge, fill=NEG, base=0,
                               pattern=[[-1, P]], channel_multiplier=1).then_inc(consts, 1)
            pool.affine_select(out=mask_kq[:, :], in_=mask_kq[:, :], compare_op=ALU.is_ge, fill=NEG, base=0,
                               pattern=[[1, P]], channel_multiplier=-1).then_inc(consts, 1)
            for i in range(PARTS):
                pool.affine_select(out=own[:, :], in_=own[:, :], compare_op=ALU.not_equal, fill=1.0,
                                   base=-(SHIFT0 + i * GH), pattern=[[-1, GH]], channel_multiplier=1)\
                    .then_inc(const_step, 1)
                pool.wait_ge(const_step, 6 + i)
            pool.memset(Vs[:, :, :, :, :], 0.0).then_inc(const_step, 1)
            pool.wait_ge(const_step, 9)
            pool.memset(Vs[:, :, :, :, HD:HD + 1], 1.0).then_inc(const_step, 1)

            pool.memset(zeros, 0.0).then_inc(zeros_set, 1)
            pool.memset(tri[:, :], 0.0).then_inc(const_step, 1)
            pool.memset(resets[:, :, :], 1.0).then_inc(sort_consts, 1)
            pool.wait_ge(sort_consts, 1)
            pool.memset(resets[:, :, 0:1], 0.0).then_inc(sort_consts, 1)
            pool.memset(onesb[:, :], 1.0).then_inc(sort_consts, 1)
            pool.memset(ones_e[:, :], 1.0).then_inc(sort_consts, 1)
            pool.wait_ge(const_step, 11)
            pool.affine_select(out=tri[:, :], in_=tri[:, :], compare_op=ALU.is_ge, fill=1.0, base=0,
                               pattern=[[-1, P]], channel_multiplier=1).then_inc(sort_consts, 1)
            pool.iota(ints[:, 0:E], pattern=[[1, E]], base=-E, channel_multiplier=0).then_inc(iotas, 1)
            pool.iota(ints[:, E:E + HTILES], pattern=[[P, HTILES]], base=0, channel_multiplier=0).then_inc(iotas, 1)
            pool.iota(ints[:, E + HTILES:], pattern=[[1, SLOTS]], base=0, channel_multiplier=0).then_inc(iotas, 1)

            def body(pair):
                for u in range(2):
                    b = pair * 2 + u
                    if True:
                        at_least(pool, w_in, 5 * 16)
                        at_least(pool, xn_ready[u], pair + 1)
                        xs = x_all[:, bass.ts(b, CH), :]
                        pool.tensor_tensor(xs, xs, bo_b[:, :].unsqueeze(1).to_broadcast([P, CH, D]), ALU.add)\
                            .then_inc(xb_done, 1)
                    at_least(pool, k_copied[u], pair + 1)
                    at_least(pool, k_stored[u], pair * STORES)
                    own_wait()
                    pool.tensor_copy(kparts[:, u, 0, :], kf[:, u, :]).then_inc(ksplit, 1)
                    at_least(pool, ksplit, b * 3 + 1)
                    pool.tensor_tensor(krest[:, :], kf[:, u, :], kparts[:, u, 0, :], ALU.subtract).then_inc(ksplit, 1)
                    at_least(pool, ksplit, b * 3 + 2)
                    own_wait()
                    pool.tensor_copy(kparts[:, u, 1, :], krest[:, :]).then_inc(ksplit, 1)
                    at_least(pool, ksplit, b * 3 + 3)
                    pool.tensor_tensor(kparts[:, u, 2, :], krest[:, :], kparts[:, u, 1, :], ALU.subtract)\
                        .then_inc(ksplit_done[u], 1)

            repeat(pool, BATCH // 2, body)

            def load_v(b, g):
                own_wait()
                for c in range(CH):
                    last = pool.tensor_copy(Vs[:, g, c, :, 0:HD],
                                            v_all[:, b * CH + c, g * 32:(g + 1) * 32].rearrange("p (h d) -> p h d", d=HD))
                last.then_inc(v_loaded, 1)

            def split_shift(s, g):
                par = g % 2
                pool.wait_ge(scores_used[(NSCORE - 1) % 2], (s + 1) * (NSCORE // 2))
                at_least(pool, shiftT_ready, s - 1)
                own_wait()
                pool.tensor_copy(nparts[:, par, :, 0, :], nmax[:, par, :, :]).then_inc(shift_step, 1)
                pool.wait_ge(shift_step, s * 3 + 1)
                pool.tensor_tensor(nrest[:, par, :, :], nmax[:, par, :, :], nparts[:, par, :, 0, :], ALU.subtract)\
                    .then_inc(shift_step, 1)
                pool.wait_ge(shift_step, s * 3 + 2)
                own_wait()
                pool.tensor_copy(nparts[:, par, :, 1, :], nrest[:, par, :, :]).then_inc(shift_step, 1)
                pool.wait_ge(shift_step, s * 3 + 3)
                pool.tensor_tensor(nparts[:, par, :, 2, :], nrest[:, par, :, :], nparts[:, par, :, 1, :], ALU.subtract)\
                    .then_inc(shift_split[par], 1)

            def step(b, g, first, last):
                s = b * GROUPS + g
                if not (first and g == 0) and not (last and g > 0):
                    pool.wait_ge(pv_done[CH - 1], s)
                    load_v(b + (g + 3) // GROUPS, (g + 3) % GROUPS)
                if not (last and g >= 2):
                    split_shift(s + 2, (g + 2) % GROUPS)

            pool.wait_ge(const_step, 10)
            for u in range(2):
                pool.wait_ge(v_copied[u], BATCH // 2)
            for g in range(GROUPS):
                load_v(0, g)
            split_shift(0, 0)
            split_shift(1, 1)
            for g in range(GROUPS):
                step(0, g, True, False)
            with pool.Fori(1, BATCH - 1) as b:
                for g in range(GROUPS):
                    step(b, g, False, False)
            for g in range(GROUPS):
                step(BATCH - 1, g, False, True)

            def scatter(half):
                pool.wait_ge(routed, half + 1)
                for u in range(2):
                    pool.wait_ge(xn2_kept[u], (half + 1) * HPAIRS)
                pool.wait_ge(xs_cleared, HALVES * -(-SLOTS // 8) * 16)
                for t in range(HTILES):
                    for k in range(TOPK):
                        pool.indirect_dma_start(
                            out=xs_dram[half], out_offset=bass.IndirectOffsetOnAxis(ap=place[:, half, k, t:t + 1], axis=0),
                            in_=xn2[:, t, :], in_offset=None).then_inc(scattered[half], 16)

            def gather(half):
                for u in range(2):
                    pool.wait_ge(y_stored[u], (half + 1) * (EVEN, ODD)[u] * 16)
                for t in range(HTILES):
                    for k in range(TOPK):
                        pool.indirect_dma_start(
                            out=yg[half][:, k * HTILES + t, :], out_offset=None, in_=ys_dram[half],
                            in_offset=bass.IndirectOffsetOnAxis(ap=place[:, half, k, t:t + 1], axis=0))\
                            .then_inc(gathered[half], 16)

            for half in range(HALVES):
                scatter(half)
            for half in range(HALVES):
                gather(half)


        @block.scalar
        def _(act):
            act.wait_ge(var_done, 1)
            act.activation(rstd[:, :], lnt[:, 3, :], ACT.Sqrt).then_inc(std_done, 1)

            def body(pair):
                for u in range(2):
                    b = pair * 2 + u
                    at_least(act, xT_ready[u], pair + 1)
                    at_least(act, qkv_ready[u], pair)
                    act.activation(xnT[:, u, :], psS[:, u, :], ACT.Copy).then_inc(xT_copied[u], 1)
                    at_least(act, qkv_ready[u], pair + 1)
                    at_least(act, qsplit_done[u], pair)
                    act.activation(qf[:, u, :], psT[:, 2 * u, :], ACT.Copy, scale=SCALE).then_inc(q_copied[u], 1)
                    at_least(act, ksplit_done[u], pair)
                    act.activation(kf[:, u, :], psT[:, 2 * u + 1, :], ACT.Copy).then_inc(k_copied[u], 1)
                    act.activation(v_all[:, bass.ts(b, CH), :].rearrange("p c d -> p (c d)"), ps_v[u][:, :], ACT.Copy)\
                        .then_inc(v_copied[u], 1)

            repeat(act, BATCH // 2, body)

            def exps(s, n):
                i, h0, nh = PROB_TASKS[n]
                slot, cols = n % 2, T - i * P
                act.wait_ge(prob_ready[slot], s * (NPROB // 2) + n // 2 + 1)
                at_least(act, pv_done[i], s)
                src = psT[:, 2 * slot:2 * slot + 2, 0:cols] if i < 2 else \
                    psT[:, 2 * slot:2 * slot + 2, :].rearrange("p a n -> p (a n)")[:, 0:nh * cols]
                dst = PT[:, PT0[i] + h0 * cols:PT0[i] + (h0 + nh) * cols]
                if i == 1:
                    dst = dst.rearrange("p (a n) -> p a n", a=nh)
                elif i == 0:
                    src = src.rearrange("p a n -> p (a n)")
                act.activation(dst, src, ACT.Exp).then_inc(prob_done[slot], 1)

            def copy_heads(s, g):
                act.wait_ge(pv_done[CH - 1], s + 1)
                at_least(act, headsT_ready, s - 1)
                act.activation(Os[:, g % 2, :], psO[:, :], ACT.Copy).then_inc(heads_copied, 1)

            def copy_shift(s, b, g):
                act.wait_ge(shiftT_ready, s + 1)
                if b is not None:
                    act.wait_ge(shift_loaded[(g + 2) % GROUPS], (b + 1) * GH * 16)
                act.activation(shiftT[:, g % 2, :], psM[0:SHIFTS, 0:T // 2].bitcast(BF16), ACT.Copy)\
                    .then_inc(shiftT_copied, 1)

            def step(b, g, first, last):
                s = b * GROUPS + g
                exps(s, 0)
                exps(s, 1)
                if not (first and g == 0):
                    copy_heads(s - 1, (g + 3) % GROUPS)
                if not (last and g == GROUPS - 1):
                    before = None if first and g == 0 else b - (1 if g == 0 else 0)
                    copy_shift(s + 1, before, (g + 1) % GROUPS)
                for n in range(2, NPROB):
                    exps(s, n)

            copy_shift(0, None, 0)
            for g in range(GROUPS):
                step(0, g, True, False)
            with act.Fori(1, BATCH - 1) as b:
                for g in range(GROUPS):
                    step(b, g, False, False)
            for g in range(GROUPS):
                step(BATCH - 1, g, False, True)
            copy_heads(STEPS - 1, GROUPS - 1)

            def finish_attention(half):
                def body(pair):
                    for u in range(2):
                        b = half * (BATCH // HALVES) + pair * 2 + u
                        k = half * HPAIRS + pair
                        at_least(act, aT_ready[u], k)
                        act.activation(xn[:, u, :, :], attn[:, bass.ts(b, CH), :], ACT.Copy).then_inc(stage_done[u], 1)
                        at_least(act, aT_ready[u], k + 1)
                        at_least(act, o_ready[u], k)
                        act.activation(xnT[:, u, :], psS[:, u, :], ACT.Copy).then_inc(aT_copied[u], 1)

                repeat(act, HPAIRS, body)
                act.wait_ge(var_done, half + 2)
                sl = slice(half * HTILES, (half + 1) * HTILES)
                act.activation(rstd[:, sl], lnt[:, 3, sl], ACT.Sqrt).then_inc(std_done, 1)
                def body(pair):
                    for u in range(2):
                        b = half * (BATCH // HALVES) + pair * 2 + u
                        k = half * HPAIRS + pair
                        at_least(act, xn2T_ready[u], k + 1)
                        at_least(act, logits_ready[u], k)
                        act.activation(xnT[:, u, :], psS[:, u, :], ACT.Copy).then_inc(xn2T_copied[u], 1)
                        at_least(act, xn2_ready[u], k + 1)
                        if half:
                            at_least(act, scattered[half - 1], TOPK * HTILES * 16)
                        act.activation(xn2[:, bass.ts(pair * 2 + u, CH), :], xn[:, u, :, :], ACT.Copy)\
                            .then_inc(xn2_kept[u], 1)

                repeat(act, HPAIRS, body)
                act.wait_ge(lg_done, half + 1)
                act.activation(pr[:, :, :], lg[:, :, :], ACT.Exp).then_inc(exp_done, 1)

            act.wait_ge(smallT, 2)
            act.activation(gateT[:, :], psS[:, 0, 0:E], ACT.Copy).then_inc(smallT_copied, 1)
            act.activation(b1T[:, :], psS[:, 0, E:E + E * FC], ACT.Copy).then_inc(smallT_copied, 1)
            act.wait_ge(normed, STEPS)
            for half in range(HALVES):
                finish_attention(half)

            def moe(half):
                def copy_xs(i, k, u):
                    k = half * (EVEN, ODD)[u] + k
                    act.wait_ge(xs_turned[u], k + 1)
                    at_least(act, h_ready[u], k)
                    act.activation(xsT[:, u, :], psS[:, u, 0:P], ACT.Copy).then_inc(xsT_copied[u], 1)

                def relu(i, k, u):
                    e = act.value_load(eid[0:1, half, bass.ds(i, 1)], min_val=0, max_val=E - 1)
                    k = half * (EVEN, ODD)[u] + k
                    act.wait_ge(hT_ready[u], k + 1)
                    at_least(act, y_ready[u], k)
                    for c in range(FC // 2):
                        last = act.activation(hT[:, u, c * P:(c + 1) * P], psT[:, 2 + u, c * P:(c + 1) * P], ACT.Relu,
                                              bias=b1T[:, bass.ds(e * FC + c, 1)])
                    last.then_inc(relu_act[u], 1)

                copy_xs(0, 0, 0)
                copy_xs(1, 0, 1)
                relu(0, 0, 0)
                def body(k):
                    for u in range(2):
                        relu(k * 2 + u + 1, k + (u + 1) // 2, (u + 1) % 2)
                        copy_xs(k * 2 + u + 2, k + 1, u)

                repeat(act, (SLOTS - 2) // 2, body)
                for i in range((SLOTS - 2) // 2 * 2, SLOTS):
                    if i + 1 < SLOTS:
                        relu(i + 1, (i + 1) // 2, (i + 1) % 2)
                    if i + 2 < SLOTS:
                        copy_xs(i + 2, (i + 2) // 2, i % 2)

            for half in range(HALVES):
                moe(half)

        @block.tensor
        def _(pe):
            pe.wait_ge(consts, 4)
            pe.wait_ge(wperm, 2)
            pe.wait_ge(w_in, 5 * 16)
            def body(pair):
                for u in range(2):
                    at_least(pe, xn_ready[u], pair + 1)
                    at_least(pe, xT_copied[u], pair)
                    for c in range(CH):
                        last = pe.transpose(psS[:, u, c * P:(c + 1) * P], xn[:, u, c, :], identf[:, :])
                    last.then_inc(xT_ready[u], 1)
                    at_least(pe, xT_copied[u], pair + 1)
                    at_least(pe, v_copied[u], pair)
                    pe.matmul(psT[:, 2 * u, :], wqp[:, :], xnT[:, u, :], start=True, stop=True)
                    pe.matmul(psT[:, 2 * u + 1, :], wkp[:, :], xnT[:, u, :], start=True, stop=True)
                    for c in range(CH):
                        last = pe.matmul(ps_v[u][:, c * P:(c + 1) * P], xnT[:, u, c * P:(c + 1) * P], wv_sb[:, :],
                                         start=True, stop=True)
                    last.then_inc(qkv_ready[u], 1)

            repeat(pe, BATCH // 2, body)

            def scores(s, b, g, a):
                slot = a % 2
                at_least(pe, scores_used[slot], s * (NSCORE // 2) + a // 2)
                if a == 0:
                    pe.wait_ge(qk_loaded[g], (b + 1) * QK_LOADS)
                for j, h, c0 in SCORE_TASKS[a]:
                    n = (j + 1) * P
                    pe.matmul(psS[:, slot, c0:c0 + n], Qs[0:QK_ROWS, g, h, j * P:n], Ks[0:QK_ROWS, g, h, 0:n],
                              start=True, stop=False)
                    last = pe.matmul(psS[:, slot, c0 + n - P:c0 + n], identb[:, :], mask_qk[:, :], start=False, stop=True)
                last.then_inc(scores_ready[slot], 1)

            def probs(s, b, g, n):
                i, h0, nh = PROB_TASKS[n]
                slot, cols = n % 2, T - i * P
                at_least(pe, prob_done[slot], s * (NPROB // 2) + n // 2)
                if n == 0:
                    pe.wait_ge(shift_loaded[g], (b + 1) * GH * 16)
                for k in range(nh):
                    h = h0 + k
                    bank, c0 = (k, 0) if i < 2 else (k * cols // 512, k * cols % 512)
                    reg = psT[:, 2 * slot + bank, c0:c0 + cols]
                    pe.matmul(reg, Ks[0:ST_ROWS, g, h, i * P:(i + 1) * P], Qs[0:ST_ROWS, g, h, i * P:T],
                              start=True, stop=False)
                    last = pe.matmul(reg[:, 0:P], identb[:, :], mask_kq[:, :], start=False, stop=True)
                last.then_inc(prob_ready[slot], 1)

            def weigh(s, g, i):
                for slot in {n % 2 for n, task in enumerate(PROB_TASKS) if task[0] == i}:
                    done = max(n // 2 for n, task in enumerate(PROB_TASKS) if task[0] == i and n % 2 == slot) + 1
                    pe.wait_ge(prob_done[slot], s * (NPROB // 2) + done)
                if i == 0:
                    at_least(pe, heads_copied, s)
                    pe.wait_ge(v_loaded, s + 1)
                cols = T - i * P
                for h in range(GH):
                    c0 = PT0[i] + h * cols
                    last = pe.matmul(psO[h * VW:(h + 1) * VW, i * P:T], Vs[:, g, i, h, :], PT[:, c0:c0 + cols],
                                     start=(i == 0), stop=(i == CH - 1))
                last.then_inc(pv_done[i], 1)

            def turn_shift(s, b, g):
                pe.wait_ge(shift_split[g % 2], b * 2 + g // 2 + 1)
                at_least(pe, normed, s - 2)
                for j in range(CH):
                    last = pe.transpose(psM[0:SHIFTS, j * P // 2:(j + 1) * P // 2].bitcast(BF16),
                                        nparts[:, g % 2, j, :, :].rearrange("p i h -> p (i h)"), identb[:, :])
                last.then_inc(shiftT_ready, 1)

            def turn_heads(s, g, copied):
                pe.wait_ge(heads_copied, s + 1)
                at_least(pe, normed, s)
                pe.wait_ge(shiftT_copied, copied)
                for j in range(CH):
                    last = pe.transpose(psM[:, j * P:(j + 1) * P], Os[:, g % 2, j * P:(j + 1) * P], identf[:, :])
                last.then_inc(headsT_ready, 1)

            def step(b, g, first, last):
                s = b * GROUPS + g
                ahead = (s + 2, b + (g + 2) // GROUPS, (g + 2) % GROUPS)
                more = not (last and g >= 2)
                before = not (first and g == 0)
                nxt = not (last and g == GROUPS - 1)

                def sc(*tasks):
                    if more:
                        for a in tasks:
                            scores(*ahead, a)

                probs(s, b, g, 0)
                sc(0)
                if before:
                    weigh(s - 1, (g + 3) % GROUPS, 3)
                probs(s, b, g, 1)
                sc(1, 2)
                if nxt:
                    turn_shift(s + 1, b + (g + 1) // GROUPS, (g + 1) % GROUPS)
                probs(s, b, g, 2)
                sc(3)
                weigh(s, g, 0)
                if before:
                    turn_heads(s - 1, (g + 3) % GROUPS, s + 2 if nxt else s + 1)
                probs(s, b, g, 3)
                sc(4, 5)
                probs(s, b, g, 4)
                weigh(s, g, 1)
                sc(6, 7)
                probs(s, b, g, 5)
                sc(8)
                weigh(s, g, 2)
                sc(9)

            for u in range(2):
                pe.wait_ge(v_copied[u], BATCH // 2)
            for a in range(NSCORE):
                scores(0, 0, 0, a)
            for a in range(NSCORE):
                scores(1, 0, 1, a)
            turn_shift(0, 0, 0)
            for g in range(GROUPS):
                step(0, g, True, False)
            with pe.Fori(1, BATCH - 1) as b:
                for g in range(GROUPS):
                    step(b, g, False, False)
            for g in range(GROUPS):
                step(BATCH - 1, g, False, True)
            weigh(STEPS - 1, GROUPS - 1, 3)
            turn_heads(STEPS - 1, GROUPS - 1, STEPS)

            def finish_attention(half):
                def body(pair):
                    for u in range(2):
                        k = half * HPAIRS + pair
                        at_least(pe, stage_done[u], k + 1)
                        at_least(pe, aT_copied[u], k)
                        for c in range(CH):
                            last = pe.transpose(psS[:, u, c * P:(c + 1) * P], xn[:, u, c, :], identf[:, :])
                        last.then_inc(aT_ready[u], 1)
                        at_least(pe, aT_copied[u], k + 1)
                        at_least(pe, x2_done[u], k)
                        for c in range(CH):
                            last = pe.matmul(psT[:, u, c * P:(c + 1) * P], xnT[:, u, c * P:(c + 1) * P], wo_sb[:, :],
                                             start=True, stop=True)
                        last.then_inc(o_ready[u], 1)

                repeat(pe, HPAIRS, body)
                def body(pair):
                    for u in range(2):
                        k = half * HPAIRS + pair
                        at_least(pe, xn2_ready[u], k + 1)
                        at_least(pe, xn2T_copied[u], k)
                        for c in range(CH):
                            last = pe.transpose(psS[:, u, c * P:(c + 1) * P], xn[:, u, c, :], identf[:, :])
                        last.then_inc(xn2T_ready[u], 1)
                        at_least(pe, xn2T_copied[u], k + 1)
                        for c in range(CH):
                            last = pe.matmul(psM[:, bass.ts((pair * 2 + u) * CH + c, E)],
                                             xnT[:, u, c * P:(c + 1) * P], gateT[:, :], start=True, stop=True)
                        last.then_inc(logits_ready[u], 1)

                repeat(pe, HPAIRS, body)
                pe.wait_ge(picks_done, half + 1)
                pk = picks[:, :, :].rearrange("p e t -> p (e t)")
                pe.matmul(psM[:, 0:E * HTILES], tri[:, :], pk, start=True, stop=True)
                pe.matmul(psM[:, E * HTILES:2 * E * HTILES], onesb[:, :], pk, start=True, stop=True).then_inc(ranks_ready, 1)

            pe.wait_ge(moe_in, 5 * 16)
            pe.wait_ge(sort_consts, 5)
            pe.transpose(psS[:, 0, 0:E], gate_rows[:, :], identf[0:E, 0:E]).then_inc(smallT, 1)
            pe.transpose(psS[:, 0, E:E + E * FC], b1_rows[:, :], identf[0:E * FC, 0:E * FC]).then_inc(smallT, 1)
            pe.wait_ge(smallT_copied, 2)
            for half in range(HALVES):
                finish_attention(half)
                pe.wait_ge(routed, half + 1)

            def moe(half):
                def turn_xs(i, k, u):
                    k = half * (EVEN, ODD)[u] + k
                    pe.wait_ge(xs_loaded[u], (k + 1) * 16)
                    at_least(pe, xsT_copied[u], k)
                    pe.transpose(psS[:, u, 0:P], xs_t[:, u, :], identf[:, :]).then_inc(xs_turned[u], 1)

                def expand(i, k, u):
                    e = pe.value_load(eid[0:1, half, bass.ds(i, 1)], min_val=0, max_val=E - 1)
                    k = half * (EVEN, ODD)[u] + k
                    pe.wait_ge(xsT_copied[u], k + 1)
                    at_least(pe, h_copied[u], k)
                    pe.matmul(psT[:, u, :], xsT[:, u, :], w1_sb[:, bass.ds(e, 1), :].rearrange("p a f -> p (a f)"),
                              start=True, stop=True).then_inc(h_ready[u], 1)

                def turn_hidden(i, k, u):
                    k = half * (EVEN, ODD)[u] + k
                    pe.wait_ge(h_copied[u], k + 1)
                    at_least(pe, relu_act[u], k)
                    at_least(pe, relu_dve[u], k)
                    for c in range(FC):
                        last = pe.transpose(psT[:, 2 + u, c * P:(c + 1) * P], h_sb[:, u, c * P:(c + 1) * P], identf[:, :])
                    last.then_inc(hT_ready[u], 1)

                def contract(i, k, u):
                    e = pe.value_load(eid[0:1, half, bass.ds(i, 1)], min_val=0, max_val=E - 1)
                    k = half * (EVEN, ODD)[u] + k
                    pe.wait_ge(relu_act[u], k + 1)
                    pe.wait_ge(relu_dve[u], k + 1)
                    at_least(pe, y_copied[u], k)
                    for c in range(FC):
                        last = pe.matmul(ps_v[u][:, 0:D], hT[:, u, c * P:(c + 1) * P],
                                         w2_sb[:, bass.ds(e, 1), c, :].rearrange("p a d -> p (a d)"),
                                         start=(c == 0), stop=(c == FC - 1))
                    last.then_inc(y_ready[u], 1)

                turn_xs(0, 0, 0)
                turn_xs(1, 0, 1)
                expand(0, 0, 0)
                turn_hidden(0, 0, 0)
                def body(k):
                    for u in range(2):
                        nxt = (k * 2 + u + 1, k + (u + 1) // 2, (u + 1) % 2)
                        expand(*nxt)
                        contract(k * 2 + u, k, u)
                        turn_hidden(*nxt)
                        turn_xs(k * 2 + u + 2, k + 1, u)

                repeat(pe, (SLOTS - 2) // 2, body)
                for i in range((SLOTS - 2) // 2 * 2, SLOTS):
                    nxt = (i + 1, (i + 1) // 2, (i + 1) % 2)
                    if i + 1 < SLOTS:
                        expand(*nxt)
                    contract(i, i // 2, i % 2)
                    if i + 1 < SLOTS:
                        turn_hidden(*nxt)
                    if i + 2 < SLOTS:
                        turn_xs(i + 2, (i + 2) // 2, i % 2)

            for half in range(HALVES):
                moe(half)

        @block.vector
        def _(dve):
            links = [0]

            def link(ins):
                links[0] += 1
                ins.then_inc(ln, 1)
                dve.wait_ge(ln, links[0])

            def row_stats(t0, t1):
                st, m = stats[:, t0:t1, :], mean[:, t0:t1]
                diff, sq, both, var = (lnt[:, i, t0:t1] for i in range(4))
                link(dve.tensor_tensor(diff, st[:, :, 1], st[:, :, 4], ALU.subtract))
                dve.tensor_tensor(m, st[:, :, 1], st[:, :, 4], ALU.add)
                link(dve.tensor_tensor(sq, diff, diff, ALU.mult))
                link(dve.tensor_tensor(both, st[:, :, 2], st[:, :, 5], ALU.add))
                link(dve.tensor_scalar(sq, sq, 0.25, EPS, ALU.mult, ALU.add))
                link(dve.tensor_scalar(m, m, 0.5, None, ALU.mult))
                dve.scalar_tensor_tensor(var, both, 1.0 / D, sq, ALU.mult, ALU.add).then_inc(var_done, 1)

            dve.memset(Qs[64:96, :, :, :].rearrange("p g h t -> p (g h t)").bitcast(U32), 0).then_inc(slots_set, 1)
            for g in range(GROUPS):
                dve.memset(Ks[64:96, g, :, :].rearrange("p h t -> p (h t)").bitcast(U32), 0).then_inc(slots_set, 1)
            dve.wait_ge(const_step, 8)
            for g in range(GROUPS):
                dve.tensor_copy(Ks[96:128, g, :, :], own[96:128, :].unsqueeze(2).to_broadcast([32, GH, T])).then_inc(slots_set, 1)

            dve.wait_ge(w_in, 5 * 16)
            for dst, src in ((wqp, wq_sb), (wkp, wk_sb)):
                dve.tensor_copy(dst[:, :].rearrange("p (g d h) -> p g d h", g=GROUPS, h=GH),
                                src[:, :].rearrange("p (g h d) -> p g d h", g=GROUPS, h=GH)).then_inc(wperm, 1)

            dve.wait_ge(x_in, 16 * BATCH)
            for t in range(TILES):
                last = dve.bn_stats(stats[:, t, :], x_all[:, t, :])
            link(last)
            row_stats(0, TILES)
            dve.wait_ge(std_done, 1)
            link(dve.reciprocal(rstd[:, :], rstd[:, :]))
            def body(pair):
                for u in range(2):
                    b = pair * 2 + u
                    at_least(dve, xT_ready[u], pair)
                    for c in range(CH):
                        t = b * CH + c
                        last = dve.tensor_scalar(xn[:, u, c, :], x_all[:, t, :], mean[:, bass.ds(t, 1)],
                                                 rstd[:, bass.ds(t, 1)], ALU.subtract, ALU.mult)
                    last.then_inc(xn_ready[u], 1)
                for u in range(2):
                    b = pair * 2 + u
                    at_least(dve, q_copied[u], pair + 1)
                    at_least(dve, q_stored[u], pair * STORES)
                    dve.tensor_copy(qparts[:, u, 0, :], qf[:, u, :]).then_inc(qsplit, 1)
                    at_least(dve, qsplit, b * 3 + 1)
                    dve.tensor_tensor(qrest[:, :], qf[:, u, :], qparts[:, u, 0, :], ALU.subtract).then_inc(qsplit, 1)
                    at_least(dve, qsplit, b * 3 + 2)
                    dve.tensor_copy(qparts[:, u, 1, :], qrest[:, :]).then_inc(qsplit, 1)
                    at_least(dve, qsplit, b * 3 + 3)
                    dve.tensor_tensor(qparts[:, u, 2, :], qrest[:, :], qparts[:, u, 1, :], ALU.subtract)\
                        .then_inc(qsplit_done[u], 1)

            repeat(dve, BATCH // 2, body)

            def maxima(s, b, g, tasks):
                par = g % 2
                for a in tasks:
                    slot = a % 2
                    if a == 0:
                        at_least(dve, shift_split[par], b * 2 + g // 2)
                    dve.wait_ge(scores_ready[slot], s * (NSCORE // 2) + a // 2 + 1)
                    if SCORE_TASKS[a][0][0] == 1:
                        h = SCORE_TASKS[a][0][1]
                        last = dve.tensor_reduce(nmax[:, par, 1, h:h + 2],
                                                 psS[:, slot, :].rearrange("p (h n) -> p h n", h=2),
                                                 AX_X, ALU.max, negate=True)
                    else:
                        for j, h, c0 in SCORE_TASKS[a]:
                            last = dve.tensor_reduce(nmax[:, par, j, h:h + 1], psS[:, slot, c0:c0 + (j + 1) * P],
                                                     AX_X, ALU.max, negate=True)
                    last.then_inc(scores_used[slot], 1)

            def norm(s, b, g):
                dve.wait_ge(headsT_ready, s + 1)
                o = psM[:, :].rearrange("p (j h v) -> p j h v", j=CH, h=GH)
                dve.reciprocal(rsum[:, :, :], o[:, :, :, HD]).then_inc(rsum_done, 1)
                dve.wait_ge(rsum_done, s + 1)
                dst = attn[:, bass.ts(b, CH), g * 32:(g + 1) * 32].rearrange("p j (h d) -> p j h d", h=GH)
                dve.tensor_tensor(dst, o[:, :, :, 0:HD], rsum[:, :, :].unsqueeze(3).to_broadcast([P, CH, GH, HD]),
                                  ALU.mult).then_inc(normed, 1)

            def step(b, g, first, last):
                s = b * GROUPS + g
                ahead = (s + 2, b + (g + 2) // GROUPS, (g + 2) % GROUPS)
                more = not (last and g >= 2)
                if more:
                    maxima(*ahead, range(5))
                if not (first and g == 0):
                    norm(s - 1, b - (1 if g == 0 else 0), (g + 3) % GROUPS)
                if more:
                    maxima(*ahead, range(5, NSCORE))

            dve.wait_ge(xs_cleared, HALVES * -(-SLOTS // 8) * 16)
            maxima(0, 0, 0, range(NSCORE))
            maxima(1, 0, 1, range(NSCORE))
            for g in range(GROUPS):
                step(0, g, True, False)
            with dve.Fori(1, BATCH - 1) as b:
                for g in range(GROUPS):
                    step(b, g, False, False)
            for g in range(GROUPS):
                step(BATCH - 1, g, False, True)
            norm(STEPS - 1, BATCH - 1, GROUPS - 1)

            def finish_attention(half):
                def body(pair):
                    for u in range(2):
                        b = half * (BATCH // HALVES) + pair * 2 + u
                        at_least(dve, o_ready[u], half * HPAIRS + pair + 1)
                        xs = x_all[:, bass.ts(b, CH), :]
                        dve.tensor_tensor(xs, psT[:, u, :].rearrange("p (c d) -> p c d", c=CH), xs, ALU.add)\
                            .then_inc(x2_done[u], 1)
                        at_least(dve, x2_done[u], half * HPAIRS + pair + 1)
                        for c in range(CH):
                            t = b * CH + c
                            last = dve.bn_stats(stats[:, bass.ds(t, 1), :].rearrange("p a s -> p (a s)"), x_all[:, t, :])
                        last.then_inc(stats_done, 1)

                repeat(dve, HPAIRS, body)
                dve.wait_ge(stats_done, (half + 1) * HPAIRS * 2)
                t0, t1 = half * HTILES, (half + 1) * HTILES
                row_stats(t0, t1)
                dve.wait_ge(std_done, half + 2)
                link(dve.reciprocal(rstd[:, t0:t1], rstd[:, t0:t1]))
                def body(pair):
                    for u in range(2):
                        b = half * (BATCH // HALVES) + pair * 2 + u
                        k = half * HPAIRS + pair
                        at_least(dve, xn2T_ready[u], k)
                        at_least(dve, xn2_kept[u], k)
                        for c in range(CH):
                            t = b * CH + c
                            last = dve.tensor_scalar(xn[:, u, c, :], x_all[:, t, :], mean[:, bass.ds(t, 1)],
                                                     rstd[:, bass.ds(t, 1)], ALU.subtract, ALU.mult)
                        last.then_inc(xn2_ready[u], 1)

                repeat(dve, HPAIRS, body)
                route(half)

            def route(half):
                def wide(v, n=E):
                    return v.unsqueeze(2).to_broadcast([P, v.shape[1], n])

                def across(v, n=HTILES):
                    return v.unsqueeze(1).to_broadcast([P, n, v.shape[1]])

                for u in range(2):
                    dve.wait_ge(logits_ready[u], (half + 1) * HPAIRS)
                logits = psM[:, 0:HTILES * E].rearrange("p (t e) -> p t e", e=E)
                link(dve.tensor_reduce(rmax[:, :], logits, AX_X, ALU.max))
                dve.tensor_tensor(lg[:, :, :], logits, wide(rmax[:, :]), ALU.subtract).then_inc(lg_done, 1)
                dve.wait_ge(lg_done, half + 1)
                left = lg
                for k, oh in enumerate((oh1, oh2)):
                    if k:
                        link(dve.scalar_tensor_tensor(left[:, :, :], oh1[:, :, :], NEG, left[:, :, :], ALU.mult, ALU.add))
                        link(dve.tensor_reduce(rmax[:, :], left[:, :, :], AX_X, ALU.max))
                        link(dve.tensor_tensor(rt[:, :, :], left[:, :, :], wide(rmax[:, :]), ALU.is_equal))
                    else:
                        link(dve.tensor_scalar(rt[:, :, :], left[:, :, :], 0.0, None, ALU.is_equal))
                    link(dve.tensor_tensor(rt[:, :, :], rt[:, :, :], across(back), ALU.mult))
                    link(dve.tensor_reduce(rz[:, :], rt[:, :, :], AX_X, ALU.min))
                    if not k:
                        dve.wait_ge(exp_done, half + 1)
                    link(dve.tensor_tensor(oh[:, :, :], across(back), wide(rz[:, :]), ALU.is_equal))
                dve.tensor_tensor(picks[:, :, :].rearrange("p e t -> p t e"), oh1[:, :, :], oh2[:, :, :], ALU.add)\
                    .then_inc(picks_done, 1)
                link(dve.tensor_reduce(rz[:, :], pr[:, :, :], AX_X, ALU.add))
                link(dve.reciprocal(rz[:, :], rz[:, :]))
                for k, oh in enumerate((oh1, oh2)):
                    link(dve.tensor_tensor(rt[:, :, :], oh[:, :, :], pr[:, :, :], ALU.mult))
                    link(dve.tensor_reduce(rmax[:, :], rt[:, :, :], AX_X, ALU.add))
                    link(dve.tensor_tensor(wgt[:, half, k, :], rmax[:, :], rz[:, :], ALU.mult))
                dve.wait_ge(ranks_ready, half + 1)
                flat = [v[:, :, :].rearrange("p e t -> p (e t)") for v in (tot, inc, resets)]
                link(dve.tensor_copy(flat[0], psM[:, E * HTILES:2 * E * HTILES]))
                link(dve.tensor_tensor_scan(flat[1], flat[2], flat[0], 0.0, ALU.mult, ALU.add))
                link(dve.tensor_tensor(need[:, :, :], wide(inc[:, :, HTILES - 1], HTILES), across(starts, E), ALU.is_gt))
                link(dve.tensor_reduce(nt[:, :], need[:, :, :], AX_X, ALU.add))
                link(dve.tensor_tensor_scan(ends[:, :], ones_e[:, :], nt[:, :], 0.0, ALU.mult, ALU.add))
                link(dve.tensor_tensor(base[:, :], ends[:, :], nt[:, :], ALU.subtract))
                link(dve.tensor_scalar(base[:, :], base[:, :], float(P), None, ALU.mult))
                link(dve.tensor_tensor(inc[:, :, :], inc[:, :, :], tot[:, :, :], ALU.subtract))
                link(dve.tensor_tensor(pos[:, :, :], psM[:, 0:E * HTILES].rearrange("p (e t) -> p e t", e=E),
                                       inc[:, :, :], ALU.add))
                link(dve.tensor_tensor(pos[:, :, :], pos[:, :, :], wide(base[:, :], HTILES), ALU.add))
                for k, oh in enumerate((oh1, oh2)):
                    link(dve.tensor_tensor(rt[:, :, :], oh[:, :, :], pos[:, :, :].rearrange("p e t -> p t e"), ALU.mult))
                    link(dve.tensor_reduce(dstf[:, :], rt[:, :, :], AX_X, ALU.add))
                    link(dve.tensor_copy(place[:, half, k, :], dstf[:, :]))
                link(dve.tensor_tensor(past[:, :, :], wide(slot_no), across(ends[:, :], SLOTS), ALU.is_ge))
                link(dve.tensor_reduce(eidf[:, :], past[:, :, :], AX_X, ALU.add))
                link(dve.tensor_scalar(eidf[:, :], eidf[:, :], float(E - 1), None, ALU.min))
                dve.tensor_copy(eid[:, half, :], eidf[:, :]).then_inc(routed, 1)

            dve.wait_ge(xb_done, BATCH)
            dve.wait_ge(iotas, 3)
            dve.wait_ge(sort_consts, 5)
            link(dve.tensor_copy(cst[:, :], ints[:, :]))
            for half in range(HALVES):
                finish_attention(half)

            def moe(half):
                def copy_hidden(i, k, u):
                    k = half * (EVEN, ODD)[u] + k
                    dve.wait_ge(h_ready[u], k + 1)
                    at_least(dve, hT_ready[u], k)
                    dve.tensor_copy(h_sb[:, u, :], psT[:, u, :]).then_inc(h_copied[u], 1)

                def relu(i, k, u):
                    e = dve.value_load(eid[0:1, half, bass.ds(i, 1)], min_val=0, max_val=E - 1)
                    k = half * (EVEN, ODD)[u] + k
                    dve.wait_ge(relu_act[u], k + 1)
                    for c in range(FC // 2, FC):
                        last = dve.tensor_scalar(hT[:, u, c * P:(c + 1) * P], psT[:, 2 + u, c * P:(c + 1) * P],
                                                 b1T[:, bass.ds(e * FC + c, 1)], 0.0, ALU.add, ALU.max)
                    last.then_inc(relu_dve[u], 1)

                def copy_y(i, k, u):
                    e = dve.value_load(eid[0:1, half, bass.ds(i, 1)], min_val=0, max_val=E - 1)
                    k = half * (EVEN, ODD)[u] + k
                    dve.wait_ge(y_ready[u], k + 1)
                    at_least(dve, y_stored[u], k * 16)
                    dve.tensor_tensor(y_t[:, u, :], ps_v[u][:, 0:D], b2_b[:, bass.ts(e, D)], ALU.add)\
                        .then_inc(y_copied[u], 1)

                copy_hidden(0, 0, 0)
                relu(0, 0, 0)
                def body(k):
                    for u in range(2):
                        nxt = (k * 2 + u + 1, k + (u + 1) // 2, (u + 1) % 2)
                        copy_hidden(*nxt)
                        copy_y(k * 2 + u, k, u)
                        relu(*nxt)

                repeat(dve, (SLOTS - 2) // 2, body)
                for i in range((SLOTS - 2) // 2 * 2, SLOTS):
                    nxt = (i + 1, (i + 1) // 2, (i + 1) % 2)
                    if i + 1 < SLOTS:
                        copy_hidden(*nxt)
                    copy_y(i, i // 2, i % 2)
                    if i + 1 < SLOTS:
                        relu(*nxt)

            def combine(half):
                dve.wait_ge(gathered[half], TOPK * HTILES * 16)
                for t in range(HTILES):
                    xt = x_all[:, half * HTILES + t, :]
                    link(dve.scalar_tensor_tensor(xt, yg[half][:, t, :], wgt[:, half, 0, t:t + 1], xt, ALU.mult, ALU.add))
                    dve.scalar_tensor_tensor(xt, yg[half][:, HTILES + t, :], wgt[:, half, 1, t:t + 1], xt,
                                             ALU.mult, ALU.add).then_inc(combined[half], 1)

            for half in range(HALVES):
                moe(half)
            for half in range(HALVES):
                combine(half)


_INS = ["L0_attn_x", "L0_attn_Wq", "L0_attn_Wk", "L0_attn_Wv", "L0_attn_Wo", "L0_attn_bo",
        "L0_ffn_gate_w", "L0_ffn_w1", "L0_ffn_b1", "L0_ffn_w2", "L0_ffn_b2"]
_OUTS = [((BATCH, T, D), "float32")]


def kernel(**inputs):
    import numpy as np
    import concourse.bacc as bacc
    from concourse.bass_utils import run_bass_kernel_spmd

    nc = bacc.Bacc("TRN2", target_bir_lowering=False, num_devices=1)
    arrays, args = {}, []
    for name in _INS:
        a = np.ascontiguousarray(inputs[name])
        arrays[f"in_{name}"] = a
        args.append(nc.dram_tensor(f"in_{name}", a.shape, mybir.dt.from_np(a.dtype), kind="ExternalInput").ap())
    for i, (shape, dtype) in enumerate(_OUTS):
        args.append(nc.dram_tensor(f"out_{i}", shape, mybir.dt.from_np(np.dtype(dtype)), kind="ExternalOutput").ap())
    layer(nc, *args)
    r = run_bass_kernel_spmd(nc, [arrays], core_ids=[0])
    return r.results[0]["out_0"]
```

```python
from contextlib import ExitStack

import concourse.bass as bass
from concourse import mybir

F32 = mybir.dt.float32
BF16 = mybir.dt.bfloat16
U32 = mybir.dt.uint32
I32 = mybir.dt.int32
ALU = mybir.AluOpType
ACT = mybir.ActivationFunctionType
AX_X = mybir.AxisListType.X

P = 128
BATCH, T, D = 8, 512, 128
HEADS = 16
HD = D // HEADS
CH = T // P
TILES = BATCH * CH
GROUPS = 4
GH = HEADS // GROUPS
STEPS = BATCH * GROUPS
PARTS = 3
PAIRS = PARTS * PARTS
QK_ROWS = 96
SHIFT0 = 96
SHIFTS = PARTS * GH
ST_ROWS = SHIFT0 + SHIFTS
VW = 32
SCALE = float(HD) ** -0.5
EPS = 1e-5
NEG = -3.0e38
E, F, TOPK = 8, 512, 2
FC = F // P
HALVES = 2
HTILES = TILES // HALVES
HPAIRS = BATCH // HALVES // 2
SLOTS = (HTILES * P * TOPK + E * (P - 1)) // P
EVEN, ODD = (SLOTS + 1) // 2, SLOTS // 2
TOKEN, BEST = D, D + 1
XW = D + 2
YROWS = HTILES * P * 2
ROUND = 4
ROUNDS = -(-SLOTS // ROUND)
FULL = (SLOTS - 5) // ROUND
DIGITS = ROUND + 3
SLOTS_UP = ROUNDS * ROUND + DIGITS

STATIC0 = BATCH // 2 + 1
STATS = (STATIC0, 0)
RSTD = (STATIC0, 1)
TURN = {(STATIC0, 2): (0, 1), (STATIC0, 3): (2, 3)}
GATE = (STATIC0 + 1, 1)
PICK = (STATIC0 + 1, 2)
COUNT = (STATIC0 + 1, 2)
ROUTE = ((STATIC0 + 1, 3), (STATIC0 + 2, 0))
WEIGHTS = (STATIC0 + 2, 2)
SCATTER = {(STATIC0 + 2, 2): 3, (STATIC0 + 2, 3): 3}
EARLY = (BATCH - 1) * CH

SCORE_TASKS = (
    [[(3, h, 0)] for h in range(GH)]
    + [[(2, h, 0), (0, h, 3 * P)] for h in range(GH)]
    + [[(1, h, 0), (1, h + 1, 2 * P)] for h in range(0, GH, 2)]
)
NSCORE = len(SCORE_TASKS)
PROB_TASKS = [(0, 0, 2), (0, 2, 2), (1, 0, 2), (1, 2, 2), (2, 0, 4), (3, 0, 4)]
NPROB = len(PROB_TASKS)
PT0 = [0, GH * 4 * P, GH * 7 * P, GH * 9 * P]
PT_COLS = GH * 10 * P


def at_least(eng, sem, n):
    if not isinstance(n, int) or n > 0:
        eng.wait_ge(sem, n)


def there(i):
    return not isinstance(i, int) or i < SLOTS


def at(b, g, step):
    return isinstance(b, int) and divmod(b * GROUPS + g, GROUPS) == step


def near(pair, u, distance):
    return pair + (u + distance) // 2, (u + distance) % 2


def is_batch(pair, u):
    return not isinstance(pair, int) or 0 <= pair * 2 + u < BATCH


def over_pairs(eng, body):
    body(0)
    with eng.Fori(1, BATCH // 2 - 1) as pair:
        body(pair)
    body(BATCH // 2 - 1)


def repeat(eng, n, body):
    body(0)
    with eng.Fori(1, n) as i:
        body(i)


def layer(nc, x, wq, wk, wv, wo, bo, gate_w, w1, b1, w2, b2, out):
    with ExitStack() as ctx:
        def sb(name, shape, dt=F32):
            return ctx.enter_context(nc.sbuf_tensor(name, shape, dt))

        def ps(name, shape):
            return ctx.enter_context(nc.psum_tensor(name, shape, F32))

        def sem(name):
            return ctx.enter_context(nc.semaphore(name))

        def sems(name, n):
            return [sem(f"{name}{i}") for i in range(n)]

        x_all = sb("x_all", [P, TILES, D])
        stats = sb("stats", [P, TILES, 6])
        mean = sb("mean", [P, TILES])
        rstd = sb("rstd", [P, TILES])
        lnt = sb("lnt", [P, 4, TILES])
        wq_sb = sb("wq_sb", [P, D])
        wk_sb = sb("wk_sb", [P, D])
        wv_sb = sb("wv_sb", [P, D])
        wo_sb = sb("wo_sb", [P, D])
        wqp = sb("wqp", [P, D])
        wkp = sb("wkp", [P, D])
        bo_b = sb("bo_b", [P, D])
        identf = sb("identf", [P, P])
        identb = sb("identb", [P, P], BF16)
        mask_qk = sb("mask_qk", [P, P], BF16)
        own = sb("own", [P, GH], BF16)
        xn = sb("xn", [P, 2, CH, D])
        xnT = sb("xnT", [P, 2, T])
        qrest = sb("qrest", [P, 2, T])
        krest = sb("krest", [P, 2, T])
        rows3T = sb("rows3T", [P, T])
        scoresT = sb("scoresT", [P, T])
        pad_row = sb("pad_row", [P, XW])
        qparts = sb("qparts", [P, 2, PARTS, T], BF16)
        kparts = sb("kparts", [P, 2, PARTS, T], BF16)
        v_all = sb("v_all", [P, TILES, D])
        Qs = sb("Qs", [P, GROUPS, GH, T], BF16)
        Ks = sb("Ks", [P, GROUPS, GH, T], BF16)
        Vs = sb("Vs", [P, GROUPS, CH, GH, VW])
        PT = sb("PT", [P, PT_COLS])
        nmax = sb("nmax", [P, 2, CH, GH])
        nrest = sb("nrest", [P, 2, CH, GH])
        nparts = sb("nparts", [P, 2, CH, PARTS, GH], BF16)
        shiftT = sb("shiftT", [SHIFTS, 2, T], BF16)
        Os = sb("Os", [P, 2, T])
        rsum = sb("rsum", [P, CH, GH])
        attn = sb("attn", [P, CH, D])
        w1_sb = sb("w1_sb", [P, E, F])
        w2_sb = sb("w2_sb", [P, E, FC, D])
        b2_b = sb("b2_b", [P, E * D])
        gate_rows = sb("gate_rows", [E, D])
        gateT = sb("gateT", [P, P // CH])
        b1_rows = sb("b1_rows", [E * FC, P])
        b1T = sb("b1T", [P, E * FC])
        xn2 = sb("xn2", [P, TILES, XW])
        tri = sb("tri", [P, P], BF16)
        onesb = sb("onesb", [P, P], BF16)
        ints = sb("ints", [P, E + HTILES + SLOTS_UP], I32)
        cst = sb("cst", [P, E + HTILES + SLOTS_UP])
        back = cst[:, 0:E]
        starts = cst[:, E:E + HTILES]
        slot_no = cst[:, E + HTILES:]
        resets = sb("resets", [P, E, HTILES])
        ones_e = sb("ones_e", [P, E])
        lg, rest, pr, oh1, oh2, rt = (sb(n, [P, HTILES, E]) for n in ("lg", "rest", "pr", "oh1", "oh2", "rt"))
        rmax, rz = sb("rmax", [P, HTILES]), sb("rz", [P, HTILES])
        picks = sb("picks", [P, E, HTILES], BF16)
        tot, inc, pos, rank = (sb(n, [P, E, HTILES]) for n in ("tot", "inc", "pos", "rank"))
        need = sb("need", [P, E, HTILES])
        nt, ends, base = (sb(n, [P, E]) for n in ("nt", "ends", "base"))
        past = sb("past", [P, SLOTS_UP, E])
        eidf = sb("eidf", [P, SLOTS_UP])
        slot_expert = sb("slot_expert", [P, HALVES, SLOTS_UP])
        packed = sb("packed", [P, ROUNDS])
        token2i = sb("token2i", [P, TILES + 1], I32)
        xs_t = sb("xs_t", [P, ROUND, XW])
        y_row = sb("y_row", [P, ROUND], I32)
        turns = sb("turns", [P, HALVES, ROUNDS], I32)
        dstf = sb("dstf", [P, HTILES])
        place = sb("place", [P, HALVES, TOPK, HTILES], I32)
        wgt = sb("wgt", [P, HALVES, TOPK, HTILES])
        xsT = Os[:, 0, 2 * D:4 * D].rearrange("p (u d) -> p u d", u=2)
        y_t = Os[:, 1, 0:2 * D].rearrange("p (u d) -> p u d", u=2)
        rowsT = [xn[:, 0, :, :].rearrange("p c d -> p (c d)"), xn[:, 1, :, :].rearrange("p c d -> p (c d)"),
                 xnT[:, 1, :], rows3T[:, :]]
        w1_t = qrest
        hT = krest
        yg = [v.rearrange("p (t k d) -> p t k d", t=HTILES, k=TOPK)
              for v in (v_all[:, :, :].rearrange("p t d -> p (t d)"), PT[:, 0:TILES * D])]
        xs_dram = [nc.dram_tensor(f"sorted_x{i}", [SLOTS * P, XW], F32, kind="Internal").ap() for i in range(HALVES)]
        ys_dram = [nc.dram_tensor(f"rows_y{i}", [YROWS, D], F32, kind="Internal").ap() for i in range(HALVES)]
        q_dram = nc.dram_tensor("q_parts", [BATCH, GROUPS, PARTS, HD * GH, T], BF16, kind="Internal").ap()
        k_dram = nc.dram_tensor("k_parts", [BATCH, PARTS, GROUPS, HD * GH, T], BF16, kind="Internal").ap()

        psS = ps("psS", [P, 2, 512])
        psT = ps("psT", [P, 4, 512])
        psO = ps("psO", [P, 512])
        psM = ps("psM", [P, 512])
        ps_v = [psO, psM]

        x_in, w_in, wo_in, gate_in = sems("x_in", BATCH), sem("w_in"), sem("wo_in"), sem("gate_in")
        wperm, consts, const_step = sem("wperm"), sem("consts"), sem("const_step")
        slots_set, rows_cleared = sem("slots_set"), sem("rows_cleared")
        ln = sem("ln")
        var_done, std_done = sem("var_done"), sem("std_done")
        xn_ready, xT_ready, xT_copied = sems("xn_ready", 2), sems("xT_ready", 2), sems("xT_copied", 2)
        qkv_ready, first_parts, rests, second_parts, v_copied = (
            sems(n, 2) for n in ("qkv_ready", "first_parts", "rests", "second_parts", "v_copied"))
        qsplit_done, ksplit_done = sems("qsplit_done", 2), sems("ksplit_done", 2)
        q_stored, k_stored = sems("q_stored", 2), sems("k_stored", 2)
        xb_done = sem("xb_done")
        qk_loaded, shift_loaded = sems("qk_loaded", GROUPS), sems("shift_loaded", GROUPS)
        v_loaded = sem("v_loaded")
        scores_ready, scores_used = sems("scores_ready", 2), sems("scores_used", 2)
        shift_step, shift_split = sem("shift_step"), sems("shift_split", 2)
        shiftT_ready, shiftT_copied = sem("shiftT_ready"), sem("shiftT_copied")
        prob_ready, prob_done, masked = sems("prob_ready", 2), sems("prob_done", 2), sem("masked")
        pv_done = sems("pv_done", CH)
        heads_copied, headsT_ready, rsum_done, normed = (sem(n) for n in ("heads_copied", "headsT_ready", "rsum_done", "normed"))
        attnT_ready, attnT_copied, o_ready, x2_done = (sem(n) for n in ("attnT_ready", "attnT_copied", "o_ready", "x2_done"))
        gate_padded = sem("gate_padded")
        out_done, pool_turn, sp_turn = sem("out_done"), sem("pool_turn"), sem("sp_turn")
        moe_in, smallT, smallT_copied = sem("moe_in"), sem("smallT"), sem("smallT_copied")
        zeros_set, xs_cleared = sem("zeros_set"), sem("xs_cleared")
        iotas, cst_done, sort_consts = sem("iotas"), sem("cst_done"), sem("sort_consts")
        xn2_ready, xn2T_ready, xn2T_copied, scoresT_ready, scoresT_copied, logits_ready, logits_kept = (
            sem(n) for n in ("xn2_ready", "xn2T_ready", "xn2T_copied", "scoresT_ready", "scoresT_copied",
                             "logits_ready", "logits_kept"))
        stats_done = sem("stats_done")
        lg_done, exp_done, picks_done, ranks_ready, ranks_kept, routed = (
            sem(n) for n in ("lg_done", "exp_done", "picks_done", "ranks_ready", "ranks_kept", "routed"))
        scattered, combined = sems("scattered", HALVES), sem("combined")
        results_loaded, best_added = sems("results_loaded", BATCH), sem("best_added")
        tokens_set, row_found = sem("tokens_set"), sem("row_found")
        xs_loaded = sems("xs_loaded", ROUND)
        xs_turned, xsT_copied, w1_copied, h_ready, relu_act, relu_dve, y_ready, y_copied, y_stored = (
            sems(n, 2) for n in ("xs_turned", "xsT_copied", "w1_copied", "h_ready",
                                 "relu_act", "relu_dve", "y_ready", "y_copied", "y_stored"))

        QK_LOADS = (1 + PARTS) * 16
        Q_STORES, K_STORES = GROUPS * 16, 16
        CLEAR = 5
        CLEARS = HALVES * BATCH * 16

        def experts(eng, half, k):
            digits = eng.value_load(turns[0:1, half, bass.ds(k, 1)], min_val=0, max_val=E ** DIGITS - 1)
            return [digits // E ** n % E for n in range(DIGITS)]

        def turns_of(eng, body):
            repeat(eng, FULL, body)
            for k in range(FULL, ROUNDS):
                body(k)

        block = ctx.enter_context(nc.Block())

        @block.sync
        def _(sp):
            x_v = x.rearrange("b (c p) d -> b p c d", p=P)
            sp.dma_start(x_all[:, 0:CH, :], x_v[0]).then_inc(x_in[0], 16)
            for dst, src in ((wq_sb, wq), (wk_sb, wk), (wv_sb, wv)):
                sp.dma_start(dst[:, :], src).then_inc(w_in, 16)
            for b in range(1, BATCH):
                sp.dma_start(x_all[:, b * CH:(b + 1) * CH, :], x_v[b]).then_inc(x_in[b], 16)
            sp.dma_start(wo_sb[:, :], wo).then_inc(wo_in, 16)
            sp.dma_start(bo_b[:, :], bo.partition_broadcast(P)).then_inc(wo_in, 16)
            sp.dma_start(gate_rows[:, :], gate_w).then_inc(gate_in, 16)
            sp.dma_start(b1_rows[:, :], b1.rearrange("e (c p) -> (e c) p", p=P)).then_inc(gate_in, 16)
            sp.dma_start(b2_b[:, :], b2.rearrange("e d -> (e d)").partition_broadcast(P)).then_inc(moe_in, 16)

            def load_qk(b, g):
                sp.dma_start(Qs[0:PAIRS * HD, g, :, :].rearrange("r h t -> r (h t)"),
                             q_dram[b, g].rearrange("i (d h) t -> (i d) (h t)", h=GH).unsqueeze(0)
                             .to_broadcast([PARTS, PARTS * HD, GH * T])).then_inc(qk_loaded[g], 16)
                for a in range(PARTS):
                    sp.dma_start(Ks[a * PARTS * HD:(a + 1) * PARTS * HD, g, :, :].rearrange("r h t -> r (h t)"),
                                 k_dram[b, a, g].rearrange("(d h) t -> d (h t)", h=GH).unsqueeze(0)
                                 .to_broadcast([PARTS, HD, GH * T])).then_inc(qk_loaded[g], 16)

            def store_parts(pair, u):
                b = pair * 2 + u
                sp.wait_ge(qsplit_done[u], pair + 1)
                for g in range(GROUPS):
                    sp.dma_start(q_dram[b, g].rearrange("i r t -> r i t"),
                                 qparts[g * 32:(g + 1) * 32, u, :, :]).then_inc(q_stored[u], 16)
                sp.wait_ge(ksplit_done[u], pair + 1)
                sp.dma_start(k_dram[b].rearrange("i g r t -> (g r) i t"), kparts[:, u, :, :]).then_inc(k_stored[u], 16)

            store_parts(0, 0)
            store_parts(0, 1)
            sp.wait_ge(q_stored[0], Q_STORES)
            sp.wait_ge(k_stored[0], K_STORES)
            sp.wait_ge(slots_set, GROUPS)
            sp.wait_ge(rows_cleared, 2)
            for b in range(2, BATCH):
                if b - 2 < GROUPS:
                    load_qk(0, b - 2)
                store_parts(b // 2, b % 2)
            for u in range(2):
                sp.wait_ge(q_stored[u], Q_STORES * BATCH // 2)
                sp.wait_ge(k_stored[u], K_STORES * BATCH // 2)

            def clear(half, slot, n):
                sp.dma_start(xs_dram[half].rearrange("(n p) d -> p n d", p=P)[:, bass.ds(slot, n), :],
                             pad_row[:, :].unsqueeze(1).to_broadcast([P, n, XW])).then_inc(xs_cleared, 16)

            sp.wait_ge(zeros_set, 1)
            sp.wait_ge(tokens_set, 1)
            for half in range(HALVES):
                clear(half, (BATCH - 1) * CLEAR, SLOTS - (BATCH - 1) * CLEAR)

            def load_shift(s, g):
                sp.wait_ge(shiftT_copied, s + 1)
                sp.dma_start(Qs[SHIFT0:SHIFT0 + SHIFTS, g, :, :],
                             shiftT[:, g % 2, :].unsqueeze(1).to_broadcast([SHIFTS, GH, T])).then_inc(shift_loaded[g], 16)

            def step(b, g, last):
                s = b * GROUPS + g
                if not (last and g == GROUPS - 1):
                    load_shift(s + 1, (g + 1) % GROUPS)
                if g == 0:
                    sp.dma_start(w1_sb[:, bass.ds(b, 1), :].rearrange("p a f -> p (a f)"), w1[b]).then_inc(moe_in, 16)
                if g == 1:
                    sp.dma_start(w2_sb[:, bass.ds(b, 1), :, :].rearrange("p a c d -> p (a c) d"),
                                 w2[b].rearrange("(c p) d -> p c d", p=P)).then_inc(moe_in, 16)
                if g >= 2 and not last:
                    clear(g - 2, b * CLEAR, CLEAR)
                if not last:
                    sp.wait_ge(prob_ready[1], (s + 1) * (NPROB // 2))
                    load_qk(b + 1, g)

            load_shift(0, 0)
            with sp.Fori(0, BATCH - 1) as b:
                for g in range(GROUPS):
                    step(b, g, False)
            for g in range(GROUPS):
                step(BATCH - 1, g, True)

            def load_results(half):
                for u in range(2):
                    sp.wait_ge(y_stored[u], (half + 1) * (EVEN, ODD)[u] * 16)
                for b in range(BATCH // HALVES):
                    rows = ys_dram[half][b * CH * P * 2:(b + 1) * CH * P * 2, :].rearrange("(t p k) d -> p t (k d)", p=P, k=TOPK)
                    sp.dma_start(yg[half][:, b * CH:(b + 1) * CH, :, :].rearrange("p t k d -> p t (k d)"), rows)\
                        .then_inc(results_loaded[half * (BATCH // HALVES) + b], 16)

            def moe(half):
                before = [-(-(SLOTS - n) // ROUND) * half for n in range(ROUND)]

                def load(i, k, n):
                    u = n % 2
                    tiles = half * (EVEN, ODD)[u] + k * 2 + n // 2 - 1
                    if isinstance(k, int) and k == 0:
                        tiles = half * (EVEN, ODD)[u]
                    at_least(sp, xs_turned[u], tiles)
                    sp.sem_inc(sp_turn, 1)
                    at_least(sp, row_found, half * SLOTS + (k * ROUND + n - ROUND + 1 if not (isinstance(k, int) and k == 0) else 0))
                    sp.sem_inc(sp_turn, 1)
                    sp.dma_start(xs_t[:, n, :], xs_dram[half][bass.ts(i, P), :]).then_inc(xs_loaded[n], 16)

                sp.wait_ge(scattered[half], TOPK * HTILES * 16)
                def body(k):
                    for n in range(ROUND):
                        if there(k * ROUND + n):
                            load(k * ROUND + n, k, n)

                turns_of(sp, body)

            moe(0)
            load_results(0)
            moe(1)
            load_results(1)
            o_v = out.rearrange("b (c p) d -> b p c d", p=P)
            for b in range(BATCH):
                sp.wait_ge(combined, (b + 1) * CH)
                sp.dma_start(o_v[b], x_all[:, b * CH:(b + 1) * CH, :]).then_inc(out_done, 16)
            sp.wait_ge(out_done, 16 * BATCH)

        @block.gpsimd
        def _(pool):
            def own_wait():
                pool.sem_inc(pool_turn, 1)

            pool.memset(identf[:, :], 0.0).then_inc(const_step, 1)
            pool.memset(identb[:, :], 0.0).then_inc(const_step, 1)
            pool.memset(mask_qk[:, :], 0.0).then_inc(const_step, 1)
            pool.memset(own[:, :], 0.0).then_inc(const_step, 1)
            pool.wait_ge(const_step, 4)
            for m in (identf, identb):
                pool.affine_select(out=m[:, :], in_=m[:, :], compare_op=ALU.not_equal, fill=1.0, base=0,
                                   pattern=[[-1, P]], channel_multiplier=1).then_inc(consts, 1)
            pool.affine_select(out=mask_qk[:, :], in_=mask_qk[:, :], compare_op=ALU.is_ge, fill=NEG, base=0,
                               pattern=[[-1, P]], channel_multiplier=1).then_inc(consts, 1)
            for i in range(PARTS):
                pool.affine_select(out=own[:, :], in_=own[:, :], compare_op=ALU.not_equal, fill=1.0,
                                   base=-(SHIFT0 + i * GH), pattern=[[-1, GH]], channel_multiplier=1)\
                    .then_inc(const_step, 1)
                pool.wait_ge(const_step, 5 + i)
            pool.memset(Qs[64:96, :, :, :].rearrange("p g h t -> p (g h t)").bitcast(U32), 0).then_inc(rows_cleared, 1)
            pool.memset(Ks[64:96, :, :, :].rearrange("p g h t -> p (g h t)").bitcast(U32), 0).then_inc(rows_cleared, 1)
            pool.wait_ge(rows_cleared, 2)
            pool.memset(Vs[:, :, :, :, :], 0.0).then_inc(const_step, 1)
            pool.wait_ge(const_step, 8)
            pool.memset(Vs[:, :, :, :, HD:HD + 1], 1.0).then_inc(const_step, 1)

            pool.memset(gateT[:, :], 0.0).then_inc(gate_padded, 1)

            pool.memset(pad_row[:, 0:D], 0.0).then_inc(zeros_set, 1)
            pool.memset(tri[:, :], 0.0).then_inc(const_step, 1)
            pool.memset(resets[:, :, :], 1.0).then_inc(sort_consts, 1)
            pool.wait_ge(sort_consts, 1)
            pool.memset(resets[:, :, 0:1], 0.0).then_inc(sort_consts, 1)
            pool.memset(onesb[:, :], 1.0).then_inc(sort_consts, 1)
            pool.memset(ones_e[:, :], 1.0).then_inc(sort_consts, 1)
            pool.wait_ge(const_step, 10)
            pool.affine_select(out=tri[:, :], in_=tri[:, :], compare_op=ALU.is_ge, fill=1.0, base=0,
                               pattern=[[-1, P]], channel_multiplier=1).then_inc(sort_consts, 1)
            pool.iota(token2i[:, 0:TILES], pattern=[[0, HALVES], [2 * P, HTILES]], base=0, channel_multiplier=2).then_inc(iotas, 1)
            pool.iota(token2i[:, TILES:], pattern=[[0, 1]], base=2 * P * HTILES, channel_multiplier=2).then_inc(iotas, 1)
            pool.iota(ints[:, 0:E], pattern=[[1, E]], base=-E, channel_multiplier=0).then_inc(iotas, 1)
            pool.iota(ints[:, E:E + HTILES], pattern=[[P, HTILES]], base=0, channel_multiplier=0).then_inc(iotas, 1)
            pool.iota(ints[:, E + HTILES:], pattern=[[1, SLOTS_UP]], base=0, channel_multiplier=0).then_inc(iotas, 1)

            def third_k(pair, u):
                pool.wait_ge(second_parts[u], pair + 1)
                pool.tensor_tensor(kparts[:, u, 2, :], krest[:, u, :], kparts[:, u, 1, :], ALU.subtract)\
                    .then_inc(ksplit_done[u], 1)

            pool.wait_ge(wo_in, 2 * 16)
            def body(pair):
                for u in range(2):
                    if is_batch(*near(pair, u, -1)):
                        third_k(*near(pair, u, -1))
                    pool.wait_ge(xn_ready[u], pair + 1)
                    xs = x_all[:, bass.ts(pair * 2 + u, CH), :]
                    pool.tensor_tensor(xs, xs, bo_b[:, :].unsqueeze(1).to_broadcast([P, CH, D]), ALU.add)\
                        .then_inc(xb_done, 1)

            over_pairs(pool, body)
            third_k(BATCH // 2 - 1, 1)

            def load_v(b, g):
                own_wait()
                for c in range(CH):
                    last = pool.tensor_copy(Vs[:, g, c, :, 0:HD],
                                            v_all[:, b * CH + c, g * 32:(g + 1) * 32].rearrange("p (h d) -> p h d", d=HD))
                last.then_inc(v_loaded, 1)

            def mask(s, i):
                for slot in sorted({n % 2 for n, task in enumerate(PROB_TASKS) if task[0] == i}):
                    done = max(n // 2 for n, task in enumerate(PROB_TASKS) if task[0] == i and n % 2 == slot) + 1
                    pool.wait_ge(prob_done[slot], s * (NPROB // 2) + done)
                own_wait()
                cols = T - i * P
                square = PT[:, PT0[i]:PT0[i] + GH * cols].rearrange("p (h n) -> p h n", h=GH)[:, :, 0:P]
                pool.affine_select(out=square, in_=square, compare_op=ALU.is_ge, fill=0.0, base=0,
                                   pattern=[[0, GH], [1, P]], channel_multiplier=-1).then_inc(masked, 1)

            def split_shift(s, g):
                par = g % 2
                pool.wait_ge(scores_used[(NSCORE - 1) % 2], (s + 1) * (NSCORE // 2))
                at_least(pool, shiftT_ready, s - 1)
                own_wait()
                pool.tensor_copy(nparts[:, par, :, 0, :], nmax[:, par, :, :]).then_inc(shift_step, 1)
                pool.wait_ge(shift_step, s * 3 + 1)
                pool.tensor_tensor(nrest[:, par, :, :], nmax[:, par, :, :], nparts[:, par, :, 0, :], ALU.subtract)\
                    .then_inc(shift_step, 1)
                pool.wait_ge(shift_step, s * 3 + 2)
                own_wait()
                pool.tensor_copy(nparts[:, par, :, 1, :], nrest[:, par, :, :]).then_inc(shift_step, 1)
                pool.wait_ge(shift_step, s * 3 + 3)
                pool.tensor_tensor(nparts[:, par, :, 2, :], nrest[:, par, :, :], nparts[:, par, :, 1, :], ALU.subtract)\
                    .then_inc(shift_split[par], 1)

            def scatter(half, number):
                t, k = number // TOPK, number % TOPK
                pool.indirect_dma_start(
                    out=xs_dram[half], out_offset=bass.IndirectOffsetOnAxis(ap=place[:, half, k, t:t + 1], axis=0),
                    in_=xn2[:, half * HTILES + t, :], in_offset=None).then_inc(scattered[half], 16)

            sent = [0]
            def step(b, g, first, last):
                s = b * GROUPS + g
                early = SCATTER.get((b, g), 0) if isinstance(b, int) else 0
                if early and not sent[0]:
                    pool.wait_ge(routed, 1)
                    pool.wait_ge(xs_cleared, CLEARS)
                mask(s, 0)
                if not (first and g == 0) and not (last and g > 0):
                    pool.wait_ge(pv_done[CH - 1], s)
                    load_v(b + (g + 3) // GROUPS, (g + 3) % GROUPS)
                for i in range(1, CH):
                    for _ in range(early // (CH - 1) + (i <= early % (CH - 1))):
                        scatter(0, sent[0])
                        sent[0] += 1
                    mask(s, i)
                if not (last and g >= 2):
                    split_shift(s + 2, (g + 2) % GROUPS)

            pool.wait_ge(const_step, 9)
            pool.wait_ge(v_copied[0], 1)
            for g in range(GROUPS):
                load_v(0, g)
            for u in range(2):
                pool.wait_ge(v_copied[u], BATCH // 2)
            split_shift(0, 0)
            split_shift(1, 1)
            for g in range(GROUPS):
                step(0, g, True, False)
            with pool.Fori(1, BATCH - 1) as b:
                for g in range(GROUPS):
                    step(b, g, False, False)
            for g in range(GROUPS):
                step(BATCH - 1, g, False, True)

            def store_y(half, k, n):
                u = n % 2
                pool.wait_ge(y_copied[u], half * (EVEN, ODD)[u] + k * 2 + n // 2 + 1)
                own_wait()
                pool.indirect_dma_start(
                    out=ys_dram[half], out_offset=bass.IndirectOffsetOnAxis(ap=y_row[:, n:n + 1], axis=0),
                    in_=y_t[:, u, :], in_offset=None, bounds_check=HTILES * P * 2 - 1, oob_is_err=False)\
                    .then_inc(y_stored[u], 16)

            for number in range(sent[0], TOPK * HTILES):
                scatter(0, number)
            for k in range(ROUNDS):
                for n in range(ROUND):
                    if there(k * ROUND + n):
                        store_y(0, k, n)
                    number = (k - 1) * ROUND + n
                    if 0 <= number < TOPK * HTILES:
                        if number == 0:
                            pool.wait_ge(routed, 2)
                        scatter(1, number)
            def body(k):
                for n in range(ROUND):
                    if there(k * ROUND + n):
                        store_y(1, k, n)

            turns_of(pool, body)

        @block.scalar
        def _(act):
            act.wait_ge(const_step, 7)
            for g in range(GROUPS // 2):
                act.activation(Ks[96:128, g, :, :], own[96:128, :].unsqueeze(2).to_broadcast([32, GH, T]), ACT.Copy)\
                    .then_inc(slots_set, 1)

            def root(t0, t1, n):
                act.wait_ge(var_done, n)
                act.activation(rstd[:, t0:t1], lnt[:, 3, t0:t1], ACT.Sqrt).then_inc(std_done, 1)

            def copy_xn(pair, u):
                act.wait_ge(xT_ready[u], pair + 1)
                at_least(act, qkv_ready[u], pair)
                act.activation(xnT[:, u, :], psS[:, u, :], ACT.Copy).then_inc(xT_copied[u], 1)

            def round_rests(pair, u):
                act.wait_ge(rests[u], pair + 1)
                act.activation(qparts[:, u, 1, :], qrest[:, u, :], ACT.Copy)
                act.activation(kparts[:, u, 1, :], krest[:, u, :], ACT.Copy).then_inc(second_parts[u], 1)

            root(0, 2 * CH, 1)
            copy_xn(0, 0)
            def body(pair):
                for u in range(2):
                    if isinstance(pair, int) and (pair, u) == (0, 1):
                        root(2 * CH, TILES, 2)
                    if is_batch(*near(pair, u, 1)):
                        copy_xn(*near(pair, u, 1))
                    if is_batch(*near(pair, u, -1)):
                        round_rests(*near(pair, u, -1))
                    act.wait_ge(qkv_ready[u], pair + 1)
                    at_least(act, q_stored[u], pair * Q_STORES)
                    at_least(act, k_stored[u], pair * K_STORES)
                    act.activation(qparts[:, u, 0, :], psT[:, 2 * u, :], ACT.Copy, scale=SCALE)
                    act.activation(kparts[:, u, 0, :], psT[:, 2 * u + 1, :], ACT.Copy).then_inc(first_parts[u], 1)
                    act.activation(v_all[:, bass.ts(pair * 2 + u, CH), :].rearrange("p c d -> p (c d)"), ps_v[u][:, :], ACT.Copy)\
                        .then_inc(v_copied[u], 1)

            over_pairs(act, body)
            round_rests(BATCH // 2 - 1, 1)
            act.wait_ge(smallT, 2)
            act.wait_ge(gate_padded, 1)
            act.activation(gateT[:, 0:E], psS[:, 0, 0:E], ACT.Copy).then_inc(smallT_copied, 1)
            act.activation(b1T[:, :], psS[:, 0, E:E + E * FC], ACT.Copy).then_inc(smallT_copied, 1)

            def exps(s, n):
                i, h0, nh = PROB_TASKS[n]
                slot, cols = n % 2, T - i * P
                act.wait_ge(prob_ready[slot], s * (NPROB // 2) + n // 2 + 1)
                at_least(act, pv_done[i], s)
                src = psT[:, 2 * slot:2 * slot + 2, 0:cols] if i < 2 else \
                    psT[:, 2 * slot:2 * slot + 2, :].rearrange("p a n -> p (a n)")[:, 0:nh * cols]
                dst = PT[:, PT0[i] + h0 * cols:PT0[i] + (h0 + nh) * cols]
                if i == 1:
                    dst = dst.rearrange("p (a n) -> p a n", a=nh)
                elif i == 0:
                    src = src.rearrange("p a n -> p (a n)")
                act.activation(dst, src, ACT.Exp).then_inc(prob_done[slot], 1)

            def copy_heads(s, g):
                act.wait_ge(pv_done[CH - 1], s + 1)
                at_least(act, headsT_ready, s - 1)
                act.activation(Os[:, g % 2, :], psO[:, :], ACT.Copy).then_inc(heads_copied, 1)

            def copy_shift(s, b, g):
                act.wait_ge(shiftT_ready, s + 1)
                if b is not None:
                    act.wait_ge(shift_loaded[(g + 2) % GROUPS], (b + 1) * 16)
                act.activation(shiftT[:, g % 2, :], psM[0:SHIFTS, 0:T // 2].bitcast(BF16), ACT.Copy)\
                    .then_inc(shiftT_copied, 1)

            def copy_attention(b):
                act.wait_ge(attnT_ready, b + 1)
                at_least(act, o_ready, b)
                act.activation(xnT[:, 0, :], psM[:, :], ACT.Copy).then_inc(attnT_copied, 1)

            def copy_rows(b, bank):
                act.wait_ge(xn2T_ready, b + 1)
                at_least(act, scoresT_ready, b // (BATCH // HALVES))
                act.activation(rowsT[b % (BATCH // HALVES)], bank, ACT.Copy).then_inc(xn2T_copied, 1)

            def copy_scores(half, bank):
                act.wait_ge(scoresT_ready, half + 1)
                at_least(act, logits_ready, half)
                act.activation(scoresT[:, :], bank, ACT.Copy).then_inc(scoresT_copied, 1)

            def exp_logits(half):
                act.wait_ge(lg_done, half + 1)
                act.activation(pr[:, :, :], lg[:, :, :], ACT.Exp).then_inc(exp_done, 1)

            def step(b, g, first, last):
                s = b * GROUPS + g
                exps(s, 0)
                exps(s, 1)
                if not (first and g == 0):
                    copy_heads(s - 1, (g + 3) % GROUPS)
                if not (last and g == GROUPS - 1):
                    before = None if first and g == 0 else b - (1 if g == 0 else 0)
                    copy_shift(s + 1, before, (g + 1) % GROUPS)
                if at(b, g, RSTD):
                    root(0, HTILES, 3)
                if at(b, g, WEIGHTS):
                    exp_logits(0)
                for n in range(2, NPROB - 1):
                    exps(s, n)
                turned = isinstance(b, int) and TURN.get((b, g))
                if g == 0 and not first:
                    copy_attention(b - 1)
                if turned:
                    copy_rows(turned[0], psM[:, :])
                if at(b, g, GATE):
                    copy_scores(0, psM[:, :])
                exps(s, NPROB - 1)
                if turned:
                    copy_rows(turned[1], psM[:, :])

            copy_shift(0, None, 0)
            for g in range(GROUPS):
                step(0, g, True, False)
            with act.Fori(1, STATIC0) as b:
                for g in range(GROUPS):
                    step(b, g, False, False)
            for b in range(STATIC0, BATCH):
                for g in range(GROUPS):
                    step(b, g, False, b == BATCH - 1)
            copy_heads(STEPS - 1, GROUPS - 1)
            copy_attention(BATCH - 1)
            root(HTILES, EARLY, 4)
            copy_rows(4, psT[:, 0, :])
            copy_rows(5, psT[:, 1, :])
            root(EARLY, TILES, 5)
            copy_rows(6, psT[:, 2, :])
            copy_rows(7, psT[:, 3, :])
            copy_scores(1, psS[:, 0, :])
            exp_logits(1)

            def moe(half):
                def copy_xs(k, u):
                    k = half * (EVEN, ODD)[u] + k
                    act.wait_ge(xs_turned[u], k + 1)
                    at_least(act, h_ready[u], k)
                    act.activation(xsT[:, u, :], psS[:, u, 0:P], ACT.Copy).then_inc(xsT_copied[u], 1)

                def relu(k, u, e):
                    k = half * (EVEN, ODD)[u] + k
                    act.wait_ge(h_ready[u], k + 1)
                    at_least(act, y_ready[u], k)
                    for c in range(FC // 2):
                        last = act.activation(hT[:, u, c * P:(c + 1) * P], psT[:, 2 * u, c * P:(c + 1) * P], ACT.Relu,
                                              bias=b1T[:, bass.ds(e * FC + c, 1)])
                    last.then_inc(relu_act[u], 1)

                for i in range(3):
                    copy_xs(i // 2, i % 2)
                relu(0, 0, experts(act, half, 0)[0])
                def body(k):
                    es = experts(act, half, k)
                    for n in range(ROUND):
                        i = k * ROUND + n
                        if there(i + 1):
                            relu(k * 2 + (n + 1) // 2, (n + 1) % 2, es[n + 1])
                        if there(i + 3):
                            copy_xs(k * 2 + (n + 3) // 2, (n + 3) % 2)

                turns_of(act, body)

            for half in range(HALVES):
                moe(half)

        @block.tensor
        def _(pe):
            def turn_xn(pair, u):
                pe.wait_ge(xn_ready[u], pair + 1)
                at_least(pe, xT_copied[u], pair)
                for c in range(CH):
                    last = pe.transpose(psS[:, u, c * P:(c + 1) * P], xn[:, u, c, :], identf[:, :])
                last.then_inc(xT_ready[u], 1)

            pe.wait_ge(consts, 3)
            turn_xn(0, 0)
            pe.wait_ge(wperm, 2)
            pe.wait_ge(w_in, 3 * 16)
            def body(pair):
                for u in range(2):
                    if is_batch(*near(pair, u, 1)):
                        turn_xn(*near(pair, u, 1))
                    pe.wait_ge(xT_copied[u], pair + 1)
                    at_least(pe, rests[u], pair)
                    at_least(pe, v_copied[u], pair)
                    pe.matmul(psT[:, 2 * u, :], wqp[:, :], xnT[:, u, :], start=True, stop=True)
                    pe.matmul(psT[:, 2 * u + 1, :], wkp[:, :], xnT[:, u, :], start=True, stop=True)
                    for c in range(CH):
                        last = pe.matmul(ps_v[u][:, c * P:(c + 1) * P], xnT[:, u, c * P:(c + 1) * P], wv_sb[:, :],
                                         start=True, stop=True)
                    last.then_inc(qkv_ready[u], 1)

            over_pairs(pe, body)

            for u in range(2):
                pe.wait_ge(v_copied[u], BATCH // 2)
                pe.wait_ge(rests[u], BATCH // 2)
            pe.wait_ge(gate_in, 2 * 16)
            pe.wait_ge(wo_in, 2 * 16)
            pe.wait_ge(sort_consts, 5)
            pe.transpose(psS[:, 0, 0:E], gate_rows[:, :], identf[0:E, 0:E]).then_inc(smallT, 1)
            pe.transpose(psS[:, 0, E:E + E * FC], b1_rows[:, :], identf[0:E * FC, 0:E * FC]).then_inc(smallT, 1)
            pe.wait_ge(smallT_copied, 2)

            def scores(s, b, g, a):
                slot = a % 2
                at_least(pe, scores_used[slot], s * (NSCORE // 2) + a // 2)
                if a == 0:
                    pe.wait_ge(qk_loaded[g], (b + 1) * QK_LOADS)
                for j, h, c0 in SCORE_TASKS[a]:
                    n = (j + 1) * P
                    pe.matmul(psS[:, slot, c0:c0 + n], Qs[0:QK_ROWS, g, h, j * P:n], Ks[0:QK_ROWS, g, h, 0:n],
                              start=True, stop=False)
                    last = pe.matmul(psS[:, slot, c0 + n - P:c0 + n], identb[:, :], mask_qk[:, :], start=False, stop=True)
                last.then_inc(scores_ready[slot], 1)

            def probs(s, b, g, n):
                i, h0, nh = PROB_TASKS[n]
                slot, cols = n % 2, T - i * P
                at_least(pe, prob_done[slot], s * (NPROB // 2) + n // 2)
                if n == 0:
                    pe.wait_ge(shift_loaded[g], (b + 1) * 16)
                for k in range(nh):
                    h = h0 + k
                    bank, c0 = (k, 0) if i < 2 else (k * cols // 512, k * cols % 512)
                    reg = psT[:, 2 * slot + bank, c0:c0 + cols]
                    last = pe.matmul(reg, Ks[0:ST_ROWS, g, h, i * P:(i + 1) * P], Qs[0:ST_ROWS, g, h, i * P:T],
                                     start=True, stop=True)
                last.then_inc(prob_ready[slot], 1)

            def weigh(s, g, i):
                pe.wait_ge(masked, s * CH + i + 1)
                if i == 0:
                    at_least(pe, heads_copied, s)
                    pe.wait_ge(v_loaded, s + 1)
                cols = T - i * P
                for h in range(GH):
                    c0 = PT0[i] + h * cols
                    last = pe.matmul(psO[h * VW:(h + 1) * VW, i * P:T], Vs[:, g, i, h, :], PT[:, c0:c0 + cols],
                                     start=(i == 0), stop=(i == CH - 1))
                last.then_inc(pv_done[i], 1)

            def turn_shift(s, b, g):
                pe.wait_ge(shift_split[g % 2], b * 2 + g // 2 + 1)
                at_least(pe, normed, s - 2)
                for j in range(CH):
                    last = pe.transpose(psM[0:SHIFTS, j * P // 2:(j + 1) * P // 2].bitcast(BF16),
                                        nparts[:, g % 2, j, :, :].rearrange("p i h -> p (i h)"), identb[:, :])
                last.then_inc(shiftT_ready, 1)

            def turn_heads(s, g, copied):
                pe.wait_ge(heads_copied, s + 1)
                at_least(pe, normed, s)
                pe.wait_ge(shiftT_copied, copied)
                for j in range(CH):
                    last = pe.transpose(psM[:, j * P:(j + 1) * P], Os[:, g % 2, j * P:(j + 1) * P], identf[:, :])
                last.then_inc(headsT_ready, 1)

            def turn_attention(b):
                pe.wait_ge(normed, (b + 1) * GROUPS)
                for c in range(CH):
                    last = pe.transpose(psM[:, c * P:(c + 1) * P], attn[:, c, :], identf[:, :])
                last.then_inc(attnT_ready, 1)

            def project(b):
                pe.wait_ge(attnT_copied, b + 1)
                for c in range(CH):
                    last = pe.matmul(psM[:, c * P:(c + 1) * P], xnT[:, 0, c * P:(c + 1) * P], wo_sb[:, :],
                                     start=True, stop=True)
                last.then_inc(o_ready, 1)

            def turn_rows(b, bank):
                pe.wait_ge(xn2_ready, b + 1)
                for c in range(CH):
                    last = pe.transpose(bank[:, c * P:(c + 1) * P], xn2[:, b * CH + c, 0:D], identf[:, :])
                last.then_inc(xn2T_ready, 1)

            def score_experts(half, bank):
                pe.wait_ge(xn2T_copied, (half + 1) * (BATCH // HALVES))
                for i, rows in enumerate(rowsT):
                    last = pe.matmul(bank[i * 32:(i + 1) * 32, :], gateT[:, :], rows, start=True, stop=True)
                last.then_inc(scoresT_ready, 1)

            def turn_scores(half):
                pe.wait_ge(scoresT_copied, half + 1)
                for c in range(CH):
                    last = pe.transpose(psM[:, c * P:(c + 1) * P], scoresT[:, c * P:(c + 1) * P], identf[:, :])
                last.then_inc(logits_ready, 1)

            def count_rows(half):
                pe.wait_ge(picks_done, half + 1)
                pk = picks[:, :, :].rearrange("p e t -> p (e t)")
                pe.matmul(psM[:, 0:E * HTILES], tri[:, :], pk, start=True, stop=True)
                pe.matmul(psM[:, E * HTILES:2 * E * HTILES], onesb[:, :], pk, start=True, stop=True).then_inc(ranks_ready, 1)

            def step(b, g, first, last):
                s = b * GROUPS + g
                ahead = (s + 2, b + (g + 2) // GROUPS, (g + 2) % GROUPS)
                more = not (last and g >= 2)
                before = not (first and g == 0)
                nxt = not (last and g == GROUPS - 1)
                turned = isinstance(b, int) and TURN.get((b, g))

                def sc(*tasks):
                    if more:
                        for a in tasks:
                            scores(*ahead, a)

                probs(s, b, g, 0)
                sc(0)
                if before:
                    weigh(s - 1, (g + 3) % GROUPS, 3)
                sc(1)
                probs(s, b, g, 1)
                if g == 1 and not first:
                    pe.wait_ge(x2_done, b)
                for step_before, batches in TURN.items():
                    if at(b, g - 1, step_before):
                        pe.wait_ge(xn2T_copied, batches[1] + 1)
                if at(b, g - 1, GATE):
                    pe.wait_ge(logits_kept, 1)
                if at(b, g - 1, COUNT):
                    pe.wait_ge(ranks_kept, 1)
                if nxt:
                    turn_shift(s + 1, b + (g + 1) // GROUPS, (g + 1) % GROUPS)
                sc(2)
                probs(s, b, g, 2)
                sc(3)
                probs(s, b, g, 3)
                weigh(s, g, 0)
                sc(4)
                if before:
                    turn_heads(s - 1, (g + 3) % GROUPS, s + 2 if nxt else s + 1)
                sc(5)
                probs(s, b, g, 4)
                weigh(s, g, 1)
                if g == 0 and not first:
                    turn_attention(b - 1)
                if turned:
                    pe.wait_ge(normed, s)
                    turn_rows(turned[0], psM[:, :])
                if at(b, g, GATE):
                    pe.wait_ge(normed, s)
                    score_experts(0, psM[:, :])
                sc(6)
                probs(s, b, g, 5)
                sc(7)
                sc(8)
                weigh(s, g, 2)
                if g == 0 and not first:
                    project(b - 1)
                if turned:
                    pe.wait_ge(xn2T_copied, turned[0] + 1)
                    turn_rows(turned[1], psM[:, :])
                if at(b, g, GATE):
                    turn_scores(0)
                if at(b, g, COUNT):
                    pe.wait_ge(normed, s)
                    count_rows(0)
                sc(9)

            for a in range(NSCORE):
                scores(0, 0, 0, a)
            for a in range(NSCORE):
                scores(1, 0, 1, a)
            turn_shift(0, 0, 0)
            for g in range(GROUPS):
                step(0, g, True, False)
            with pe.Fori(1, STATIC0) as b:
                for g in range(GROUPS):
                    step(b, g, False, False)
            for b in range(STATIC0, BATCH):
                for g in range(GROUPS):
                    step(b, g, False, b == BATCH - 1)
            weigh(STEPS - 1, GROUPS - 1, 3)
            turn_heads(STEPS - 1, GROUPS - 1, STEPS)
            turn_attention(BATCH - 1)
            project(BATCH - 1)
            for b in range(BATCH // 2, BATCH):
                turn_rows(b, psT[:, b % CH, :])
            score_experts(1, psS[:, 0, :])
            pe.wait_ge(x2_done, BATCH)
            turn_scores(1)
            pe.wait_ge(logits_kept, 2)
            count_rows(1)
            pe.wait_ge(ranks_kept, HALVES)

            def moe(half):
                def turn_xs(k, n):
                    u = n % 2
                    pe.wait_ge(xs_loaded[n], (-(-(SLOTS - n) // ROUND) * half + k + 1) * 16)
                    at_least(pe, xsT_copied[u], half * (EVEN, ODD)[u] + k * 2 + n // 2)
                    pe.transpose(psS[:, u, 0:P], xs_t[:, n, 0:D], identf[:, :]).then_inc(xs_turned[u], 1)

                def expand(k, u):
                    k = half * (EVEN, ODD)[u] + k
                    pe.wait_ge(xsT_copied[u], k + 1)
                    pe.wait_ge(w1_copied[u], k + 1)
                    at_least(pe, relu_act[u], k)
                    at_least(pe, relu_dve[u], k)
                    for c in range(FC):
                        bank, c0 = 2 * u + c // (FC // 2), c % (FC // 2) * P
                        last = pe.matmul(psT[:, bank, c0:c0 + P], w1_t[:, u, c * P:(c + 1) * P], xsT[:, u, :],
                                         start=True, stop=True)
                    last.then_inc(h_ready[u], 1)

                def contract(k, u, e):
                    k = half * (EVEN, ODD)[u] + k
                    pe.wait_ge(relu_act[u], k + 1)
                    pe.wait_ge(relu_dve[u], k + 1)
                    at_least(pe, y_copied[u], k)
                    for c in range(FC):
                        last = pe.matmul(ps_v[u][:, 0:D], hT[:, u, c * P:(c + 1) * P],
                                         w2_sb[:, bass.ds(e, 1), c, :].rearrange("p a d -> p (a d)"),
                                         start=(c == 0), stop=(c == FC - 1))
                    last.then_inc(y_ready[u], 1)

                for i in range(3):
                    turn_xs(0, i)
                expand(0, 0)
                def body(k):
                    es = experts(pe, half, k)
                    for n in range(ROUND):
                        i = k * ROUND + n
                        if there(i + 1):
                            expand(k * 2 + (n + 1) // 2, (n + 1) % 2)
                        if there(i):
                            contract(k * 2 + n // 2, n % 2, es[n])
                        if there(i + 3):
                            turn_xs(k + (n + 3) // ROUND, (n + 3) % ROUND)

                turns_of(pe, body)

            pe.wait_ge(moe_in, (1 + 2 * E) * 16)
            for half in range(HALVES):
                moe(half)

        @block.vector
        def _(dve):
            links = [0]

            def link(ins):
                links[0] += 1
                ins.then_inc(ln, 1)
                dve.wait_ge(ln, links[0])

            def row_stats(t0, t1):
                st, m = stats[:, t0:t1, :], mean[:, t0:t1]
                diff, sq, both, var = (lnt[:, i, t0:t1] for i in range(4))
                link(dve.tensor_tensor(diff, st[:, :, 1], st[:, :, 4], ALU.subtract))
                dve.tensor_tensor(m, st[:, :, 1], st[:, :, 4], ALU.add)
                link(dve.tensor_tensor(sq, diff, diff, ALU.mult))
                link(dve.tensor_tensor(both, st[:, :, 2], st[:, :, 5], ALU.add))
                link(dve.tensor_scalar(sq, sq, 0.25, EPS, ALU.mult, ALU.add))
                link(dve.tensor_scalar(m, m, 0.5, None, ALU.mult))
                dve.scalar_tensor_tensor(var, both, 1.0 / D, sq, ALU.mult, ALU.add).then_inc(var_done, 1)

            def invert(t0, t1, n):
                dve.wait_ge(std_done, n)
                link(dve.reciprocal(rstd[:, t0:t1], rstd[:, t0:t1]))

            dve.wait_ge(const_step, 7)
            for g in range(GROUPS // 2, GROUPS):
                dve.tensor_copy(Ks[96:128, g, :, :], own[96:128, :].unsqueeze(2).to_broadcast([32, GH, T])).then_inc(slots_set, 1)

            def x_stats(batches):
                for b in batches:
                    dve.wait_ge(x_in[b], 16)
                    for t in range(b * CH, (b + 1) * CH):
                        last = dve.bn_stats(stats[:, t, :], x_all[:, t, :])
                link(last)
                row_stats(batches[0] * CH, (batches[-1] + 1) * CH)

            def first_norm(pair, u):
                b = pair * 2 + u
                at_least(dve, xT_ready[u], pair)
                for c in range(CH):
                    t = b * CH + c
                    last = dve.tensor_scalar(xn[:, u, c, :], x_all[:, t, :], mean[:, bass.ds(t, 1)],
                                             rstd[:, bass.ds(t, 1)], ALU.subtract, ALU.mult)
                last.then_inc(xn_ready[u], 1)

            def third_q(pair, u):
                dve.wait_ge(second_parts[u], pair + 1)
                dve.tensor_tensor(qparts[:, u, 2, :], qrest[:, u, :], qparts[:, u, 1, :], ALU.subtract)\
                    .then_inc(qsplit_done[u], 1)

            x_stats([0, 1])
            invert(0, 2 * CH, 1)
            first_norm(0, 0)
            dve.wait_ge(w_in, 3 * 16)
            for dst, src in ((wqp, wq_sb), (wkp, wk_sb)):
                dve.tensor_copy(dst[:, :].rearrange("p (g d h) -> p g d h", g=GROUPS, h=GH),
                                src[:, :].rearrange("p (g h d) -> p g d h", g=GROUPS, h=GH)).then_inc(wperm, 1)
            first_norm(0, 1)
            x_stats(range(2, BATCH))

            def body(pair):
                for u in range(2):
                    start = isinstance(pair, int) and (pair, u) == (0, 0)
                    if is_batch(*near(pair, u, 2)) and not start:
                        first_norm(*near(pair, u, 2))
                    if is_batch(*near(pair, u, -1)):
                        third_q(*near(pair, u, -1))
                    dve.wait_ge(first_parts[u], pair + 1)
                    at_least(dve, ksplit_done[u], pair)
                    dve.scalar_tensor_tensor(qrest[:, u, :], psT[:, 2 * u, :], SCALE, qparts[:, u, 0, :], ALU.mult, ALU.subtract)
                    dve.tensor_tensor(krest[:, u, :], psT[:, 2 * u + 1, :], kparts[:, u, 0, :], ALU.subtract)\
                        .then_inc(rests[u], 1)
                    if start:
                        invert(2 * CH, TILES, 2)
                        first_norm(1, 0)

            over_pairs(dve, body)
            third_q(BATCH // 2 - 1, 1)
            dve.wait_ge(xb_done, BATCH)
            dve.wait_ge(iotas, 5)
            dve.wait_ge(sort_consts, 5)
            link(dve.tensor_copy(cst[:, :], ints[:, :]))
            dve.tensor_copy(xn2[:, :, TOKEN], token2i[:, 0:TILES])
            dve.memset(pad_row[:, BEST:], 1.0)
            dve.tensor_copy(pad_row[:, TOKEN:BEST], token2i[:, TILES:]).then_inc(tokens_set, 1)

            def maxima(s, b, g, tasks):
                par = g % 2
                for a in tasks:
                    slot = a % 2
                    if a == 0:
                        at_least(dve, shift_split[par], b * 2 + g // 2)
                    dve.wait_ge(scores_ready[slot], s * (NSCORE // 2) + a // 2 + 1)
                    if SCORE_TASKS[a][0][0] == 1:
                        h = SCORE_TASKS[a][0][1]
                        last = dve.tensor_reduce(nmax[:, par, 1, h:h + 2],
                                                 psS[:, slot, :].rearrange("p (h n) -> p h n", h=2),
                                                 AX_X, ALU.max, negate=True)
                    else:
                        for j, h, c0 in SCORE_TASKS[a]:
                            last = dve.tensor_reduce(nmax[:, par, j, h:h + 1], psS[:, slot, c0:c0 + (j + 1) * P],
                                                     AX_X, ALU.max, negate=True)
                    last.then_inc(scores_used[slot], 1)

            def norm(s, b, g):
                dve.wait_ge(headsT_ready, s + 1)
                o = psM[:, :].rearrange("p (j h v) -> p j h v", j=CH, h=GH)
                dve.reciprocal(rsum[:, :, :], o[:, :, :, HD]).then_inc(rsum_done, 1)
                dve.wait_ge(rsum_done, s + 1)
                if g == 0:
                    at_least(dve, attnT_ready, b)
                dst = attn[:, :, g * 32:(g + 1) * 32].rearrange("p j (h d) -> p j h d", h=GH)
                dve.tensor_tensor(dst, o[:, :, :, 0:HD], rsum[:, :, :].unsqueeze(3).to_broadcast([P, CH, GH, HD]),
                                  ALU.mult).then_inc(normed, 1)

            def add_attention(b):
                dve.wait_ge(o_ready, b + 1)
                xs = x_all[:, bass.ts(b, CH), :]
                dve.tensor_tensor(xs, psM[:, :].rearrange("p (c d) -> p c d", c=CH), xs, ALU.add).then_inc(x2_done, 1)

            def batch_stats(b):
                dve.wait_ge(x2_done, b + 1)
                for c in range(CH):
                    t = b * CH + c
                    last = dve.bn_stats(stats[:, bass.ds(t, 1), :].rearrange("p a s -> p (a s)"), x_all[:, t, :])
                last.then_inc(stats_done, 1)

            def normalise(b):
                for t in range(b * CH, (b + 1) * CH):
                    last = dve.tensor_scalar(xn2[:, t, 0:D], x_all[:, t, :], mean[:, t:t + 1], rstd[:, t:t + 1],
                                             ALU.subtract, ALU.mult)
                last.then_inc(xn2_ready, 1)

            def keep_logits(half):
                dve.wait_ge(logits_ready, half + 1)
                dve.tensor_copy(lg[:, :, :].rearrange("p (b c) e -> p b c e", c=CH),
                                psM[:, :].rearrange("p (c b e) -> p b c e", c=CH, b=BATCH // HALVES)[:, :, :, 0:E])\
                    .then_inc(logits_kept, 1)
                dve.wait_ge(logits_kept, half + 1)

            def wide(v, n=E):
                return v.unsqueeze(2).to_broadcast([P, v.shape[1], n])

            def across(v, n=HTILES):
                return v.unsqueeze(1).to_broadcast([P, n, v.shape[1]])

            def pick_best(half):
                keep_logits(half)
                link(dve.tensor_reduce(rmax[:, :], lg[:, :, :], AX_X, ALU.max))
                dve.tensor_tensor(lg[:, :, :], lg[:, :, :], wide(rmax[:, :]), ALU.subtract).then_inc(lg_done, 1)
                dve.wait_ge(lg_done, half + 1)
                link(dve.tensor_scalar(rt[:, :, :], lg[:, :, :], 0.0, None, ALU.is_equal))
                pick_first(oh1)
                dve.tensor_copy(xn2[:, half * HTILES:(half + 1) * HTILES, BEST], rz[:, :])

            def pick_second(half):
                link(dve.scalar_tensor_tensor(rest[:, :, :], oh1[:, :, :], NEG, lg[:, :, :], ALU.mult, ALU.add))
                link(dve.tensor_reduce(rmax[:, :], rest[:, :, :], AX_X, ALU.max))
                link(dve.tensor_tensor(rt[:, :, :], rest[:, :, :], wide(rmax[:, :]), ALU.is_equal))
                pick_first(oh2)
                dve.tensor_tensor(picks[:, :, :].rearrange("p e t -> p t e"), oh1[:, :, :], oh2[:, :, :], ALU.add)\
                    .then_inc(picks_done, 1)

            def pick_first(oh):
                link(dve.tensor_tensor(rt[:, :, :], rt[:, :, :], across(back), ALU.mult))
                link(dve.tensor_reduce(rz[:, :], rt[:, :, :], AX_X, ALU.min))
                link(dve.tensor_tensor(oh[:, :, :], across(back), wide(rz[:, :]), ALU.is_equal))

            def keep_ranks(half):
                dve.wait_ge(ranks_ready, half + 1)
                dve.tensor_copy(rank[:, :, :].rearrange("p e t -> p (e t)"), psM[:, 0:E * HTILES])
                last = dve.tensor_copy(tot[:, :, :].rearrange("p e t -> p (e t)"), psM[:, E * HTILES:2 * E * HTILES])
                last.then_inc(ranks_kept, 1)
                dve.wait_ge(ranks_kept, half + 1)

            def weights(half):
                dve.wait_ge(exp_done, half + 1)
                link(dve.tensor_reduce(rz[:, :], pr[:, :, :], AX_X, ALU.add))
                link(dve.reciprocal(rz[:, :], rz[:, :]))
                for k, oh in enumerate((oh1, oh2)):
                    link(dve.tensor_tensor(rt[:, :, :], oh[:, :, :], pr[:, :, :], ALU.mult))
                    link(dve.tensor_reduce(rmax[:, :], rt[:, :, :], AX_X, ALU.add))
                    link(dve.tensor_tensor(wgt[:, half, k, :], rmax[:, :], rz[:, :], ALU.mult))

            def rank_rows(half):
                flat = [v[:, :, :].rearrange("p e t -> p (e t)") for v in (tot, inc, resets)]
                link(dve.tensor_tensor_scan(flat[1], flat[2], flat[0], 0.0, ALU.mult, ALU.add))
                link(dve.tensor_tensor(need[:, :, :], wide(inc[:, :, HTILES - 1], HTILES), across(starts, E), ALU.is_gt))
                link(dve.tensor_reduce(nt[:, :], need[:, :, :], AX_X, ALU.add))
                link(dve.tensor_tensor_scan(ends[:, :], ones_e[:, :], nt[:, :], 0.0, ALU.mult, ALU.add))
                link(dve.tensor_tensor(base[:, :], ends[:, :], nt[:, :], ALU.subtract))
                link(dve.tensor_scalar(base[:, :], base[:, :], float(P), None, ALU.mult))
                link(dve.tensor_tensor(inc[:, :, :], inc[:, :, :], tot[:, :, :], ALU.subtract))
                link(dve.tensor_tensor(pos[:, :, :], rank[:, :, :], inc[:, :, :], ALU.add))
                link(dve.tensor_tensor(pos[:, :, :], pos[:, :, :], wide(base[:, :], HTILES), ALU.add))

            def place_rows(half):
                for k, oh in enumerate((oh1, oh2)):
                    link(dve.tensor_tensor(rt[:, :, :], oh[:, :, :], pos[:, :, :].rearrange("p e t -> p t e"), ALU.mult))
                    link(dve.tensor_reduce(dstf[:, :], rt[:, :, :], AX_X, ALU.add))
                    link(dve.tensor_copy(place[:, half, k, :], dstf[:, :]))
                link(dve.tensor_tensor(past[:, :, :], wide(slot_no), across(ends[:, :], SLOTS_UP), ALU.is_ge))
                link(dve.tensor_reduce(eidf[:, :], past[:, :, :], AX_X, ALU.add))
                link(dve.tensor_scalar(eidf[:, :], eidf[:, :], float(E - 1), None, ALU.min))
                dve.tensor_scalar(slot_expert[:, half, :], eidf[:, :], float(-E), None, ALU.add)
                digit = [eidf[:, n:n + ROUND * ROUNDS].rearrange("p (k n) -> p k n", n=ROUND)[:, :, 0]
                         for n in range(DIGITS)]
                link(dve.scalar_tensor_tensor(packed[:, :], digit[-1], float(E), digit[-2], ALU.mult, ALU.add))
                for d in reversed(digit[:-2]):
                    link(dve.scalar_tensor_tensor(packed[:, :], packed[:, :], float(E), d, ALU.mult, ALU.add))
                dve.tensor_copy(turns[:, half, :], packed[:, :]).then_inc(routed, 1)

            def step(b, g, first, last):
                s = b * GROUPS + g
                ahead = (s + 2, b + (g + 2) // GROUPS, (g + 2) % GROUPS)
                more = not (last and g >= 2)
                if g == 1 and not first:
                    add_attention(b - 1)
                if at(b, g, PICK):
                    pick_best(0)
                if at(b, g, ROUTE[0]):
                    keep_ranks(0)
                if more:
                    maxima(*ahead, range(5))
                if not (first and g == 0):
                    norm(s - 1, b - (1 if g == 0 else 0), (g + 3) % GROUPS)
                if at(b, g, PICK):
                    pick_second(0)
                if at(b, g, STATS):
                    dve.wait_ge(stats_done, BATCH // HALVES)
                    row_stats(0, HTILES)
                if more:
                    maxima(*ahead, range(5, NSCORE))
                if g == 2 and not first:
                    batch_stats(b - 1)
                if at(b, g, RSTD):
                    invert(0, HTILES, 3)
                    normalise(0)
                    normalise(1)
                if at(b, g, min(TURN)):
                    normalise(2)
                    normalise(3)
                if at(b, g, ROUTE[0]):
                    rank_rows(0)
                if at(b, g, ROUTE[1]):
                    place_rows(0)
                if at(b, g, WEIGHTS):
                    weights(0)

            maxima(0, 0, 0, range(NSCORE))
            maxima(1, 0, 1, range(NSCORE))
            for g in range(GROUPS):
                step(0, g, True, False)
            with dve.Fori(1, STATIC0) as b:
                for g in range(GROUPS):
                    step(b, g, False, False)
            for b in range(STATIC0, BATCH):
                for g in range(GROUPS):
                    step(b, g, False, b == BATCH - 1)
            norm(STEPS - 1, BATCH - 1, GROUPS - 1)
            dve.wait_ge(stats_done, BATCH - 1)
            row_stats(HTILES, EARLY)
            invert(HTILES, EARLY, 4)
            normalise(4)
            add_attention(BATCH - 1)
            batch_stats(BATCH - 1)
            dve.wait_ge(stats_done, BATCH)
            row_stats(EARLY, TILES)
            normalise(5)
            normalise(6)
            invert(EARLY, TILES, 5)
            normalise(7)
            pick_best(1)
            pick_second(1)
            keep_ranks(1)

            def moe(half):
                def copy_w1(k, u, e):
                    k = half * (EVEN, ODD)[u] + k
                    at_least(dve, h_ready[u], k)
                    dve.tensor_copy(w1_t[:, u, :], w1_sb[:, bass.ds(e, 1), :].rearrange("p a f -> p (a f)"))\
                        .then_inc(w1_copied[u], 1)

                def relu(k, u, e):
                    k = half * (EVEN, ODD)[u] + k
                    dve.wait_ge(h_ready[u], k + 1)
                    at_least(dve, y_ready[u], k)
                    for c in range(FC // 2, FC):
                        c0 = (c - FC // 2) * P
                        last = dve.tensor_scalar(hT[:, u, c * P:(c + 1) * P], psT[:, 2 * u + 1, c0:c0 + P],
                                                 b1T[:, bass.ds(e * FC + c, 1)], 0.0, ALU.add, ALU.max)
                    last.then_inc(relu_dve[u], 1)

                def copy_y(k, u, e):
                    k = half * (EVEN, ODD)[u] + k
                    dve.wait_ge(y_ready[u], k + 1)
                    at_least(dve, y_stored[u], k * 16)
                    dve.tensor_tensor(y_t[:, u, :], ps_v[u][:, 0:D], b2_b[:, bass.ts(e, D)], ALU.add)\
                        .then_inc(y_copied[u], 1)

                def find_rows(k, n):
                    dve.wait_ge(xs_loaded[n], (-(-(SLOTS - n) // ROUND) * half + k + 1) * 16)
                    dve.scalar_tensor_tensor(y_row[:, n:n + 1], xs_t[:, n, BEST:XW],
                                             slot_expert[:, half, bass.ds(k * ROUND + n, 1)], xs_t[:, n, TOKEN:BEST],
                                             ALU.not_equal, ALU.add).then_inc(row_found, 1)

                es = experts(dve, half, 0)
                copy_w1(0, 0, es[0])
                copy_w1(0, 1, es[1])
                if half:
                    for u in range(2):
                        dve.wait_ge(y_stored[u], (EVEN, ODD)[u] * 16)
                find_rows(0, 0)
                find_rows(0, 1)
                relu(0, 0, es[0])
                copy_w1(1, 0, es[2])
                def body(k):
                    es = experts(dve, half, k)
                    for n in range(ROUND):
                        i = k * ROUND + n
                        if there(i + 1):
                            relu(k * 2 + (n + 1) // 2, (n + 1) % 2, es[n + 1])
                        if there(i + 3):
                            copy_w1(k * 2 + (n + 3) // 2, (n + 3) % 2, es[n + 3])
                        if there(i):
                            copy_y(k * 2 + n // 2, n % 2, es[n])
                        if there(i + 2):
                            find_rows(k + (n + 2) // ROUND, (n + 2) % ROUND)
                        if half == 0 and isinstance(k, int) and i < 3:
                            (rank_rows, place_rows, weights)[i](1)
                        if half == 1 and n in (1, 3) and not (isinstance(k, int) and k >= HTILES // 2):
                            combine(0, k * 2 + n // 2, None)

                turns_of(dve, body)

            def combine(half, t, batch):
                if batch is None:
                    if isinstance(t, int) and t == 0:
                        for b in range(BATCH // HALVES):
                            dve.wait_ge(results_loaded[b], 16)
                else:
                    dve.wait_ge(results_loaded[batch], 16)
                tile = half * HTILES + t
                xt = x_all[:, bass.ds(tile, 1), :].rearrange("p a d -> p (a d)")
                results = [yg[half][:, bass.ds(t, 1), k, :].rearrange("p a d -> p (a d)") for k in range(TOPK)]
                dve.scalar_tensor_tensor(xt, results[0], wgt[:, half, 0, bass.ds(t, 1)], xt, ALU.mult, ALU.add).then_inc(best_added, 1)
                dve.wait_ge(best_added, tile + 1)
                dve.scalar_tensor_tensor(xt, results[1], wgt[:, half, 1, bass.ds(t, 1)], xt, ALU.mult, ALU.add).then_inc(combined, 1)

            dve.wait_ge(moe_in, (1 + 2 * E) * 16)
            for half in range(HALVES):
                moe(half)
            for t in range(HTILES):
                combine(1, t, (HTILES + t) // CH)


_INS = ["L0_attn_x", "L0_attn_Wq", "L0_attn_Wk", "L0_attn_Wv", "L0_attn_Wo", "L0_attn_bo",
        "L0_ffn_gate_w", "L0_ffn_w1", "L0_ffn_b1", "L0_ffn_w2", "L0_ffn_b2"]
_OUTS = [((BATCH, T, D), "float32")]


def kernel(**inputs):
    import numpy as np
    import concourse.bacc as bacc
    from concourse.bass_utils import run_bass_kernel_spmd

    nc = bacc.Bacc("TRN2", target_bir_lowering=False, num_devices=1)
    arrays, args = {}, []
    for name in _INS:
        a = np.ascontiguousarray(inputs[name])
        arrays[f"in_{name}"] = a
        args.append(nc.dram_tensor(f"in_{name}", a.shape, mybir.dt.from_np(a.dtype), kind="ExternalInput").ap())
    for i, (shape, dtype) in enumerate(_OUTS):
        args.append(nc.dram_tensor(f"out_{i}", shape, mybir.dt.from_np(np.dtype(dtype)), kind="ExternalOutput").ap())
    layer(nc, *args)
    r = run_bass_kernel_spmd(nc, [arrays], core_ids=[0])
    return r.results[0]["out_0"]
```

```python
from contextlib import ExitStack

import concourse.bass as bass
from concourse import mybir

F32 = mybir.dt.float32
BF16 = mybir.dt.bfloat16
U32 = mybir.dt.uint32
I32 = mybir.dt.int32
ALU = mybir.AluOpType
ACT = mybir.ActivationFunctionType
AX_X = mybir.AxisListType.X

P = 128
BATCH, T, D = 8, 512, 128
HEADS = 16
HD = D // HEADS
CH = T // P
TILES = BATCH * CH
GROUPS = 4
GH = HEADS // GROUPS
STEPS = BATCH * GROUPS
PARTS = 3
PAIRS = PARTS * PARTS
QK_ROWS = 96
SHIFT0 = 96
SHIFTS = PARTS * GH
ST_ROWS = SHIFT0 + SHIFTS
VW = 32
SCALE = float(HD) ** -0.5
EPS = 1e-5
NEG = -3.0e38
E, F, TOPK = 8, 512, 2
FC = F // P
HALVES = 2
HTILES = TILES // HALVES
SLOTS = (HTILES * P * TOPK + E * (P - 1)) // P
EVEN, ODD = (SLOTS + 1) // 2, SLOTS // 2
TOKEN, BEST = D, D + 1
XW = D + 2
YROWS = HTILES * P * 2
ROUND = 4
ROUNDS = -(-SLOTS // ROUND)
AHEAD = 6
FULL = (SLOTS - AHEAD) // ROUND
DIGITS = ROUND + 3
SLOTS_UP = ROUNDS * ROUND + DIGITS

STATIC0 = BATCH // 2
STATS = (STATIC0, 3)
RSTD = (STATIC0 + 1, 0)
TURN = {(STATIC0 + 1, 1): (0, 1), (STATIC0 + 1, 2): (2, 3)}
GATE = (STATIC0 + 1, 3)
KEEP = (STATIC0 + 2, 0)
COUNT = (STATIC0 + 2, 1)
WEIGHTS = (STATIC0 + 3, 2)
SCATTER = {(STATIC0 + 3, 0): 3, (STATIC0 + 3, 1): 3, (STATIC0 + 3, 2): 3}
EARLY = (BATCH - 1) * CH

SCORE_TASKS = (
    [[(3, h, 0)] for h in range(GH)]
    + [[(2, h, 0), (0, h, 3 * P)] for h in range(GH)]
    + [[(1, h, 0), (1, h + 1, 2 * P)] for h in range(0, GH, 2)]
)
NSCORE = len(SCORE_TASKS)
PROB_TASKS = [(0, 0, 2), (0, 2, 2), (1, 0, 2), (1, 2, 2), (2, 0, 4), (3, 0, 4)]
NPROB = len(PROB_TASKS)
PT0 = [0, GH * 4 * P, GH * 7 * P, GH * 9 * P]
PT_COLS = GH * 10 * P


def at_least(eng, sem, n):
    if not isinstance(n, int) or n > 0:
        eng.wait_ge(sem, n)


def there(i):
    return not isinstance(i, int) or i < SLOTS


def at(b, g, step):
    return isinstance(b, int) and divmod(b * GROUPS + g, GROUPS) == step


def near(pair, u, distance):
    return pair + (u + distance) // 2, (u + distance) % 2


def is_batch(pair, u):
    return not isinstance(pair, int) or 0 <= pair * 2 + u < BATCH


def over_pairs(eng, body):
    body(0)
    with eng.Fori(1, BATCH // 2 - 1) as pair:
        body(pair)
    body(BATCH // 2 - 1)


def repeat(eng, n, body):
    body(0)
    with eng.Fori(1, n) as i:
        body(i)


def layer(nc, x, wq, wk, wv, wo, bo, gate_w, w1, b1, w2, b2, out):
    with ExitStack() as ctx:
        def sb(name, shape, dt=F32):
            return ctx.enter_context(nc.sbuf_tensor(name, shape, dt))

        def ps(name, shape):
            return ctx.enter_context(nc.psum_tensor(name, shape, F32))

        def sem(name):
            return ctx.enter_context(nc.semaphore(name))

        def sems(name, n):
            return [sem(f"{name}{i}") for i in range(n)]

        x_all = sb("x_all", [P, TILES, D])
        stats = sb("stats", [P, TILES, 6])
        mean = sb("mean", [P, TILES])
        rstd = sb("rstd", [P, TILES])
        lnt = sb("lnt", [P, 4, TILES])
        wq_sb = sb("wq_sb", [P, D])
        wk_sb = sb("wk_sb", [P, D])
        wv_sb = sb("wv_sb", [P, D])
        wo_sb = sb("wo_sb", [P, D])
        wqp = sb("wqp", [P, D])
        wkp = sb("wkp", [P, D])
        bo_b = sb("bo_b", [P, D])
        identf = sb("identf", [P, P])
        identb = sb("identb", [P, P], BF16)
        mask_qk = sb("mask_qk", [P, P], BF16)
        own = sb("own", [P, GH], BF16)
        xn = sb("xn", [P, 2, CH, D])
        xnT = sb("xnT", [P, 2, T])
        qrest = sb("qrest", [P, 2, T])
        krest = sb("krest", [P, 2, T])
        rows3T = sb("rows3T", [P, T])
        scoresT = sb("scoresT", [P, T])
        pad_row = sb("pad_row", [P, XW])
        qparts = sb("qparts", [P, 2, PARTS, T], BF16)
        kparts = sb("kparts", [P, 2, PARTS, T], BF16)
        v_all = sb("v_all", [P, TILES, D])
        Qs = sb("Qs", [P, GROUPS, GH, T], BF16)
        Ks = sb("Ks", [P, GROUPS, GH, T], BF16)
        Vs = sb("Vs", [P, GROUPS, CH, GH, VW])
        PT = sb("PT", [P, PT_COLS])
        nmax = sb("nmax", [P, 2, CH, GH])
        nrest = sb("nrest", [P, 2, CH, GH])
        nparts = sb("nparts", [P, 2, CH, PARTS, GH], BF16)
        shiftT = sb("shiftT", [SHIFTS, 2, T], BF16)
        Os = sb("Os", [P, 2, T])
        rsum = sb("rsum", [P, CH, GH])
        attn = sb("attn", [P, CH, D])
        w1_sb = sb("w1_sb", [P, E, F])
        w2_sb = sb("w2_sb", [P, E, FC, D])
        b2_b = sb("b2_b", [P, E * D])
        gate_rows = sb("gate_rows", [E, D])
        gateT = sb("gateT", [P, P // CH])
        b1_rows = sb("b1_rows", [E * FC, P])
        b1T = sb("b1T", [P, E * FC])
        xn2 = sb("xn2", [P, TILES, XW])
        tri = sb("tri", [P, P], BF16)
        onesb = sb("onesb", [P, P], BF16)
        ints = sb("ints", [P, E + HTILES + SLOTS_UP], I32)
        cst = sb("cst", [P, E + HTILES + SLOTS_UP])
        back = cst[:, 0:E]
        starts = cst[:, E:E + HTILES]
        slot_no = cst[:, E + HTILES:]
        resets = sb("resets", [P, E, HTILES])
        ones_e = sb("ones_e", [P, E])
        lg, rest, pr, oh1, oh2, rt = (sb(n, [P, HTILES, E]) for n in ("lg", "rest", "pr", "oh1", "oh2", "rt"))
        rmax, rz = sb("rmax", [P, HTILES]), sb("rz", [P, HTILES])
        picks = sb("picks", [P, E, HTILES], BF16)
        tot, inc, pos, rank = (sb(n, [P, E, HTILES]) for n in ("tot", "inc", "pos", "rank"))
        need = sb("need", [P, E, HTILES])
        nt, ends, base = (sb(n, [P, E]) for n in ("nt", "ends", "base"))
        past = sb("past", [P, SLOTS_UP, E])
        eidf = sb("eidf", [P, SLOTS_UP])
        slot_expert = sb("slot_expert", [P, HALVES, SLOTS_UP])
        packed = sb("packed", [P, ROUNDS])
        token2i = sb("token2i", [P, TILES + 1], I32)
        xs_t = sb("xs_t", [P, ROUND, XW])
        y_row = sb("y_row", [P, ROUND], I32)
        turns = sb("turns", [P, HALVES, ROUNDS], I32)
        dstf = sb("dstf", [P, HTILES])
        place = sb("place", [P, HALVES, TOPK, HTILES], I32)
        wgt = sb("wgt", [P, HALVES, TOPK, HTILES])
        xsT = Os[:, 0, 2 * D:4 * D].rearrange("p (u d) -> p u d", u=2)
        y_t = Os[:, 1, 0:2 * D].rearrange("p (u d) -> p u d", u=2)
        rowsT = [xn[:, 0, :, :].rearrange("p c d -> p (c d)"), xn[:, 1, :, :].rearrange("p c d -> p (c d)"),
                 xnT[:, 1, :], rows3T[:, :]]
        w1_t = qrest
        hT = krest
        yg = [v.rearrange("p (t k d) -> p t k d", t=HTILES, k=TOPK)
              for v in (v_all[:, :, :].rearrange("p t d -> p (t d)"), PT[:, 0:TILES * D])]
        xs_dram = [nc.dram_tensor(f"sorted_x{i}", [SLOTS * P, XW], F32, kind="Internal").ap() for i in range(HALVES)]
        sorted_y = nc.dram_tensor("sorted_y", [SLOTS * P, D], F32, kind="Internal").ap()
        token_y = nc.dram_tensor("token_y", [YROWS, D], F32, kind="Internal").ap()
        q_dram = nc.dram_tensor("q_parts", [BATCH, GROUPS, PARTS, HD * GH, T], BF16, kind="Internal").ap()
        k_dram = nc.dram_tensor("k_parts", [BATCH, PARTS, GROUPS, HD * GH, T], BF16, kind="Internal").ap()

        psS = ps("psS", [P, 2, 512])
        psT = ps("psT", [P, 4, 512])
        psO = ps("psO", [P, 512])
        psM = ps("psM", [P, 512])
        ps_v = [psO, psM]

        x_in, w_in, wo_in, gate_in = sems("x_in", BATCH), sem("w_in"), sem("wo_in"), sem("gate_in")
        wperm, consts, const_step = sem("wperm"), sem("consts"), sem("const_step")
        slots_set, rows_cleared = sem("slots_set"), sem("rows_cleared")
        ln = sem("ln")
        var_done, std_done = sem("var_done"), sem("std_done")
        xn_ready, xT_ready, xT_copied = sems("xn_ready", 2), sems("xT_ready", 2), sems("xT_copied", 2)
        qkv_ready, first_parts, q_rest, rests, second_parts, v_copied = (
            sems(n, 2) for n in ("qkv_ready", "first_parts", "q_rest", "rests", "second_parts", "v_copied"))
        qsplit_done, ksplit_done = sems("qsplit_done", 2), sems("ksplit_done", 2)
        q_stored, k_stored = sems("q_stored", 2), sems("k_stored", 2)
        xb_done = sem("xb_done")
        qk_loaded, shift_loaded = sems("qk_loaded", GROUPS), sems("shift_loaded", GROUPS)
        v_loaded = sem("v_loaded")
        scores_ready, scores_used = sems("scores_ready", 2), sems("scores_used", 2)
        shift_step, shift_split = sem("shift_step"), sems("shift_split", 2)
        shiftT_ready, shiftT_copied = sem("shiftT_ready"), sem("shiftT_copied")
        prob_ready, prob_done, masked = sems("prob_ready", 2), sems("prob_done", 2), sem("masked")
        pv_done = sems("pv_done", CH)
        heads_copied, headsT_ready, rsum_done, normed = (sem(n) for n in ("heads_copied", "headsT_ready", "rsum_done", "normed"))
        attnT_ready, attnT_copied, o_ready, x2_done = (sem(n) for n in ("attnT_ready", "attnT_copied", "o_ready", "x2_done"))
        gate_padded = sem("gate_padded")
        out_done, pool_turn, sp_turn = sem("out_done"), sem("pool_turn"), sem("sp_turn")
        moe_in, smallT, smallT_copied = sem("moe_in"), sem("smallT"), sem("smallT_copied")
        zeros_set, xs_cleared = sem("zeros_set"), sem("xs_cleared")
        iotas, sort_consts = sem("iotas"), sem("sort_consts")
        xn2_ready, xn2T_ready, xn2T_copied, scoresT_ready, scoresT_copied, logits_ready, logits_kept = (
            sem(n) for n in ("xn2_ready", "xn2T_ready", "xn2T_copied", "scoresT_ready", "scoresT_copied",
                             "logits_ready", "logits_kept"))
        stats_done = sem("stats_done")
        lg_done, exp_done, picks_done, ranks_ready, ranks_kept, routed = (
            sem(n) for n in ("lg_done", "exp_done", "picks_done", "ranks_ready", "ranks_kept", "routed"))
        scattered, combined = sems("scattered", HALVES), sem("combined")
        gathered, best_added = sems("gathered", ROUND), sem("best_added")
        results_loaded = sems("results_loaded", BATCH // HALVES)
        best_weighed, best_batches = sem("best_weighed"), sem("best_batches")
        placed = sem("placed")
        tokens_set, row_found = sem("tokens_set"), sem("row_found")
        xs_loaded = sems("xs_loaded", ROUND)
        xs_turned, xsT_copied, w1_copied, h_ready, relu_act, relu_dve, y_ready, y_copied, y_stored, y_scattered = (
            sems(n, 2) for n in ("xs_turned", "xsT_copied", "w1_copied", "h_ready",
                                 "relu_act", "relu_dve", "y_ready", "y_copied",
                                 "y_stored", "y_scattered"))

        QK_LOADS = (1 + PARTS) * 16
        Q_STORES, K_STORES = GROUPS * 16, 16
        CLEAR = 5
        CLEARS = HALVES * BATCH * 16

        def experts(eng, half, k):
            digits = eng.value_load(turns[0:1, half, bass.ds(k, 1)], min_val=0, max_val=E ** DIGITS - 1)
            return [digits // E ** n % E for n in range(DIGITS)]

        def turns_of(eng, body):
            repeat(eng, FULL, body)
            for k in range(FULL, ROUNDS):
                body(k)

        block = ctx.enter_context(nc.Block())

        @block.sync
        def _(sp):
            x_v = x.rearrange("b (c p) d -> b p c d", p=P)
            sp.dma_start(x_all[:, 0:CH, :], x_v[0]).then_inc(x_in[0], 16)
            for dst, src in ((wq_sb, wq), (wk_sb, wk), (wv_sb, wv)):
                sp.dma_start(dst[:, :], src).then_inc(w_in, 16)
            for b in range(1, BATCH):
                sp.dma_start(x_all[:, b * CH:(b + 1) * CH, :], x_v[b]).then_inc(x_in[b], 16)
            sp.dma_start(wo_sb[:, :], wo).then_inc(wo_in, 16)
            sp.dma_start(bo_b[:, :], bo.partition_broadcast(P)).then_inc(wo_in, 16)
            sp.dma_start(gate_rows[:, :], gate_w).then_inc(gate_in, 16)
            sp.dma_start(b1_rows[:, :], b1.rearrange("e (c p) -> (e c) p", p=P)).then_inc(gate_in, 16)
            sp.dma_start(b2_b[:, :], b2.rearrange("e d -> (e d)").partition_broadcast(P)).then_inc(moe_in, 16)

            def load_qk(b, g):
                sp.dma_start(Qs[0:PAIRS * HD, g, :, :].rearrange("r h t -> r (h t)"),
                             q_dram[b, g].rearrange("i (d h) t -> (i d) (h t)", h=GH).unsqueeze(0)
                             .to_broadcast([PARTS, PARTS * HD, GH * T])).then_inc(qk_loaded[g], 16)
                for a in range(PARTS):
                    sp.dma_start(Ks[a * PARTS * HD:(a + 1) * PARTS * HD, g, :, :].rearrange("r h t -> r (h t)"),
                                 k_dram[b, a, g].rearrange("(d h) t -> d (h t)", h=GH).unsqueeze(0)
                                 .to_broadcast([PARTS, HD, GH * T])).then_inc(qk_loaded[g], 16)

            def store_parts(pair, u):
                b = pair * 2 + u
                sp.wait_ge(qsplit_done[u], pair + 1)
                for g in range(GROUPS):
                    sp.dma_start(q_dram[b, g].rearrange("i r t -> r i t"),
                                 qparts[g * 32:(g + 1) * 32, u, :, :]).then_inc(q_stored[u], 16)
                sp.wait_ge(ksplit_done[u], pair + 1)
                sp.dma_start(k_dram[b].rearrange("i g r t -> (g r) i t"), kparts[:, u, :, :]).then_inc(k_stored[u], 16)

            store_parts(0, 0)
            store_parts(0, 1)
            sp.wait_ge(q_stored[0], Q_STORES)
            sp.wait_ge(k_stored[0], K_STORES)
            sp.wait_ge(slots_set, GROUPS)
            sp.wait_ge(rows_cleared, 2)
            for b in range(2, BATCH):
                if b - 2 < 2:
                    load_qk(0, b - 2)
                store_parts(b // 2, b % 2)
            for g in range(2, GROUPS):
                load_qk(0, g)
            for u in range(2):
                sp.wait_ge(q_stored[u], Q_STORES * BATCH // 2)
                sp.wait_ge(k_stored[u], K_STORES * BATCH // 2)

            def clear(half, slot, n):
                sp.dma_start(xs_dram[half].rearrange("(n p) d -> p n d", p=P)[:, bass.ds(slot, n), :],
                             pad_row[:, :].unsqueeze(1).to_broadcast([P, n, XW])).then_inc(xs_cleared, 16)

            sp.wait_ge(zeros_set, 1)
            sp.wait_ge(tokens_set, 1)
            for half in range(HALVES):
                clear(half, (BATCH - 1) * CLEAR, SLOTS - (BATCH - 1) * CLEAR)

            def load_shift(s, g):
                sp.wait_ge(shiftT_copied, s + 1)
                sp.dma_start(Qs[SHIFT0:SHIFT0 + SHIFTS, g, :, :],
                             shiftT[:, g % 2, :].unsqueeze(1).to_broadcast([SHIFTS, GH, T])).then_inc(shift_loaded[g], 16)

            def step(b, g, last):
                s = b * GROUPS + g
                if not (last and g == GROUPS - 1):
                    load_shift(s + 1, (g + 1) % GROUPS)
                if g == 0:
                    sp.dma_start(w1_sb[:, bass.ds(b, 1), :].rearrange("p a f -> p (a f)"), w1[b]).then_inc(moe_in, 16)
                if g == 1:
                    sp.dma_start(w2_sb[:, bass.ds(b, 1), :, :].rearrange("p a c d -> p (a c) d"),
                                 w2[b].rearrange("(c p) d -> p c d", p=P)).then_inc(moe_in, 16)
                if g >= 2 and not last:
                    clear(g - 2, b * CLEAR, CLEAR)
                if not last:
                    sp.wait_ge(prob_ready[1], (s + 1) * (NPROB // 2))
                    load_qk(b + 1, g)

            load_shift(0, 0)
            with sp.Fori(0, BATCH - 1) as b:
                for g in range(GROUPS):
                    step(b, g, False)
            for g in range(GROUPS):
                step(BATCH - 1, g, True)

            def load(half, k, n):
                u = n % 2
                if not (isinstance(k, int) and k == 0):
                    sp.wait_ge(xs_turned[u], half * (EVEN, ODD)[u] + k * 2 + n // 2 - 1)
                    sp.sem_inc(sp_turn, 1)
                    if half:
                        sp.wait_ge(row_found, k * ROUND + n - ROUND + 1)
                        sp.sem_inc(sp_turn, 1)
                sp.dma_start(xs_t[:, n, :], xs_dram[half][bass.ts(k * ROUND + n, P), :]).then_inc(xs_loaded[n], 16)

            def first_loads(half):
                sp.wait_ge(scattered[half], TOPK * HTILES * 16)
                for u in range(2):
                    at_least(sp, xs_turned[u], half * (EVEN, ODD)[u])
                for n in range(ROUND):
                    load(half, 0, n)

            def moe(half):
                for i in range(ROUND, AHEAD):
                    load(half, i // ROUND, i % ROUND)
                def body(k):
                    for n in range(ROUND):
                        if there(k * ROUND + n + AHEAD):
                            load(half, k + (n + AHEAD) // ROUND, (n + AHEAD) % ROUND)
                        if half == 0 and isinstance(k, int) and k * ROUND + n == SLOTS - 3:
                            first_loads(1)
                        if half == 0 and there(k * ROUND + n):
                            u = n % 2
                            sp.wait_ge(y_copied[u], k * 2 + n // 2 + 1)
                            sp.sem_inc(sp_turn, 1)
                            sp.dma_start(sorted_y[bass.ts(k * ROUND + n, P), :], y_t[:, u, :]).then_inc(y_stored[u], 16)

                turns_of(sp, body)

            o_v = out.rearrange("b (c p) d -> b p c d", p=P)
            def store_out(b):
                sp.wait_ge(combined, (b + 1) * CH)
                sp.dma_start(o_v[b], x_all[:, b * CH:(b + 1) * CH, :]).then_inc(out_done, 16)

            first_loads(0)
            moe(0)
            moe(1)
            for b in range(BATCH // HALVES):
                store_out(b)
            for u in range(2):
                sp.wait_ge(y_scattered[u], (EVEN, ODD)[u] * 16)
            for b in range(BATCH // HALVES):
                rows = token_y[b * CH * P * 2:(b + 1) * CH * P * 2, :].rearrange("(t p k) d -> p t (k d)", p=P, k=TOPK)
                sp.dma_start(yg[1][:, b * CH:(b + 1) * CH, :, :].rearrange("p t k d -> p t (k d)"), rows)\
                    .then_inc(results_loaded[b], 16)
            for b in range(BATCH // HALVES, BATCH):
                store_out(b)
            sp.wait_ge(out_done, 16 * BATCH)

        @block.gpsimd
        def _(pool):
            def own_wait():
                pool.sem_inc(pool_turn, 1)

            pool.memset(identf[:, :], 0.0).then_inc(const_step, 1)
            pool.memset(identb[:, :], 0.0).then_inc(const_step, 1)
            pool.memset(mask_qk[:, :], 0.0).then_inc(const_step, 1)
            pool.memset(own[:, :], 0.0).then_inc(const_step, 1)
            pool.wait_ge(const_step, 4)
            for m in (identf, identb):
                pool.affine_select(out=m[:, :], in_=m[:, :], compare_op=ALU.not_equal, fill=1.0, base=0,
                                   pattern=[[-1, P]], channel_multiplier=1).then_inc(consts, 1)
            pool.affine_select(out=mask_qk[:, :], in_=mask_qk[:, :], compare_op=ALU.is_ge, fill=NEG, base=0,
                               pattern=[[-1, P]], channel_multiplier=1).then_inc(consts, 1)
            for i in range(PARTS):
                pool.affine_select(out=own[:, :], in_=own[:, :], compare_op=ALU.not_equal, fill=1.0,
                                   base=-(SHIFT0 + i * GH), pattern=[[-1, GH]], channel_multiplier=1)\
                    .then_inc(const_step, 1)
                pool.wait_ge(const_step, 5 + i)
            pool.memset(Qs[64:96, :, :, :].rearrange("p g h t -> p (g h t)").bitcast(U32), 0).then_inc(rows_cleared, 1)
            pool.memset(Ks[64:96, :, :, :].rearrange("p g h t -> p (g h t)").bitcast(U32), 0).then_inc(rows_cleared, 1)
            pool.wait_ge(rows_cleared, 2)
            pool.memset(Vs[:, :, :, :, :], 0.0).then_inc(const_step, 1)
            pool.wait_ge(const_step, 8)
            pool.memset(Vs[:, :, :, :, HD:HD + 1], 1.0).then_inc(const_step, 1)

            pool.memset(gateT[:, :], 0.0).then_inc(gate_padded, 1)

            pool.memset(pad_row[:, 0:D], 0.0).then_inc(zeros_set, 1)
            pool.memset(tri[:, :], 0.0).then_inc(const_step, 1)
            pool.memset(resets[:, :, :], 1.0).then_inc(sort_consts, 1)
            pool.wait_ge(sort_consts, 1)
            pool.memset(resets[:, :, 0:1], 0.0).then_inc(sort_consts, 1)
            pool.memset(onesb[:, :], 1.0).then_inc(sort_consts, 1)
            pool.memset(ones_e[:, :], 1.0).then_inc(sort_consts, 1)
            pool.wait_ge(const_step, 10)
            pool.affine_select(out=tri[:, :], in_=tri[:, :], compare_op=ALU.is_ge, fill=1.0, base=0,
                               pattern=[[-1, P]], channel_multiplier=1).then_inc(sort_consts, 1)
            pool.iota(token2i[:, 0:TILES], pattern=[[0, HALVES], [2 * P, HTILES]], base=0, channel_multiplier=2).then_inc(iotas, 1)
            pool.iota(token2i[:, TILES:], pattern=[[0, 1]], base=2 * P * HTILES, channel_multiplier=2).then_inc(iotas, 1)
            pool.iota(ints[:, 0:E], pattern=[[1, E]], base=-E, channel_multiplier=0).then_inc(iotas, 1)
            pool.iota(ints[:, E:E + HTILES], pattern=[[P, HTILES]], base=0, channel_multiplier=0).then_inc(iotas, 1)
            pool.iota(ints[:, E + HTILES:], pattern=[[1, SLOTS_UP]], base=0, channel_multiplier=0).then_inc(iotas, 1)

            def third_k(pair, u):
                pool.wait_ge(second_parts[u], pair + 1)
                pool.tensor_tensor(kparts[:, u, 2, :], krest[:, u, :], kparts[:, u, 1, :], ALU.subtract)\
                    .then_inc(ksplit_done[u], 1)

            pool.wait_ge(wo_in, 2 * 16)
            def body(pair):
                for u in range(2):
                    if is_batch(*near(pair, u, -1)):
                        third_k(*near(pair, u, -1))
                    pool.wait_ge(xn_ready[u], pair + 1)
                    xs = x_all[:, bass.ts(pair * 2 + u, CH), :]
                    pool.tensor_tensor(xs, xs, bo_b[:, :].unsqueeze(1).to_broadcast([P, CH, D]), ALU.add)\
                        .then_inc(xb_done, 1)

            over_pairs(pool, body)
            third_k(BATCH // 2 - 1, 1)

            def load_v(b, g):
                own_wait()
                for c in range(CH):
                    last = pool.tensor_copy(Vs[:, g, c, :, 0:HD],
                                            v_all[:, b * CH + c, g * 32:(g + 1) * 32].rearrange("p (h d) -> p h d", d=HD))
                last.then_inc(v_loaded, 1)

            def mask(s, i):
                for slot in sorted({n % 2 for n, task in enumerate(PROB_TASKS) if task[0] == i}):
                    done = max(n // 2 for n, task in enumerate(PROB_TASKS) if task[0] == i and n % 2 == slot) + 1
                    pool.wait_ge(prob_done[slot], s * (NPROB // 2) + done)
                own_wait()
                cols = T - i * P
                square = PT[:, PT0[i]:PT0[i] + GH * cols].rearrange("p (h n) -> p h n", h=GH)[:, :, 0:P]
                pool.affine_select(out=square, in_=square, compare_op=ALU.is_ge, fill=0.0, base=0,
                                   pattern=[[0, GH], [1, P]], channel_multiplier=-1).then_inc(masked, 1)

            def split_shift(s, g):
                par = g % 2
                pool.wait_ge(scores_used[(NSCORE - 1) % 2], (s + 1) * (NSCORE // 2))
                at_least(pool, shiftT_ready, s - 1)
                own_wait()
                pool.tensor_copy(nparts[:, par, :, 0, :], nmax[:, par, :, :]).then_inc(shift_step, 1)
                pool.wait_ge(shift_step, s * 3 + 1)
                pool.tensor_tensor(nrest[:, par, :, :], nmax[:, par, :, :], nparts[:, par, :, 0, :], ALU.subtract)\
                    .then_inc(shift_step, 1)
                pool.wait_ge(shift_step, s * 3 + 2)
                own_wait()
                pool.tensor_copy(nparts[:, par, :, 1, :], nrest[:, par, :, :]).then_inc(shift_step, 1)
                pool.wait_ge(shift_step, s * 3 + 3)
                pool.tensor_tensor(nparts[:, par, :, 2, :], nrest[:, par, :, :], nparts[:, par, :, 1, :], ALU.subtract)\
                    .then_inc(shift_split[par], 1)

            def scatter(half, number):
                t, k = number // TOPK, number % TOPK
                pool.indirect_dma_start(
                    out=xs_dram[half], out_offset=bass.IndirectOffsetOnAxis(ap=place[:, half, k, t:t + 1], axis=0),
                    in_=xn2[:, half * HTILES + t, :], in_offset=None).then_inc(scattered[half], 16)

            sent = [0]
            def step(b, g, first, last):
                s = b * GROUPS + g
                early = SCATTER.get((b, g), 0) if isinstance(b, int) else 0
                if early and not sent[0]:
                    pool.wait_ge(placed, TOPK)
                    pool.wait_ge(xs_cleared, CLEARS)
                mask(s, 0)
                if not (first and g == 0) and not (last and g > 0):
                    pool.wait_ge(pv_done[CH - 1], s)
                    load_v(b + (g + 3) // GROUPS, (g + 3) % GROUPS)
                for i in range(1, CH):
                    for _ in range(early // (CH - 1) + (i <= early % (CH - 1))):
                        scatter(0, sent[0])
                        sent[0] += 1
                    mask(s, i)
                if not (last and g >= 2):
                    split_shift(s + 2, (g + 2) % GROUPS)

            pool.wait_ge(const_step, 9)
            pool.wait_ge(v_copied[0], 1)
            for g in range(GROUPS):
                load_v(0, g)
            for u in range(2):
                pool.wait_ge(v_copied[u], BATCH // 2)
            split_shift(0, 0)
            split_shift(1, 1)
            for g in range(GROUPS):
                step(0, g, True, False)
            with pool.Fori(1, BATCH - 1) as b:
                for g in range(GROUPS):
                    step(b, g, False, False)
            for g in range(GROUPS):
                step(BATCH - 1, g, False, True)

            def gather(number):
                t, k = number // TOPK, number % TOPK
                pool.indirect_dma_start(
                    out=yg[0][:, t, k, :], out_offset=None, in_=sorted_y,
                    in_offset=bass.IndirectOffsetOnAxis(ap=place[:, 0, k, t:t + 1], axis=0))\
                    .then_inc(gathered[number % ROUND], 16)

            def store_y(k, n):
                u = n % 2
                pool.wait_ge(y_copied[u], (EVEN, ODD)[u] + k * 2 + n // 2 + 1)
                pool.indirect_dma_start(
                    out=token_y, out_offset=bass.IndirectOffsetOnAxis(ap=y_row[:, n:n + 1], axis=0),
                    in_=y_t[:, u, :], in_offset=None, bounds_check=YROWS - 1, oob_is_err=False).then_inc(y_scattered[u], 16)

            for number in range(sent[0], TOPK * HTILES):
                scatter(0, number)
            pool.wait_ge(placed, HALVES * TOPK)
            for number in range(TOPK * HTILES):
                scatter(1, number)
            for u in range(2):
                pool.wait_ge(y_stored[u], (EVEN, ODD)[u] * 16)
            for k in range(ROUNDS):
                for n in range(ROUND):
                    if there(k * ROUND + n):
                        store_y(k, n)
                    if k * ROUND + n < TOPK * HTILES:
                        gather(k * ROUND + n)
            for b in range(BATCH // HALVES):
                pool.wait_ge(best_weighed, b + 1)
                xs = x_all[:, HTILES + b * CH:HTILES + (b + 1) * CH, :]
                pool.tensor_tensor(xs, xs, yg[1][:, b * CH:(b + 1) * CH, 0, :], ALU.add).then_inc(best_batches, 1)

        @block.scalar
        def _(act):
            act.wait_ge(const_step, 7)
            for g in range(GROUPS // 2):
                act.activation(Ks[96:128, g, :, :], own[96:128, :].unsqueeze(2).to_broadcast([32, GH, T]), ACT.Copy)\
                    .then_inc(slots_set, 1)

            def root(t0, t1, n):
                act.wait_ge(var_done, n)
                act.activation(rstd[:, t0:t1], lnt[:, 3, t0:t1], ACT.Sqrt).then_inc(std_done, 1)

            def copy_xn(pair, u):
                act.wait_ge(xT_ready[u], pair + 1)
                at_least(act, qkv_ready[u], pair)
                act.activation(xnT[:, u, :], psS[:, u, :], ACT.Copy).then_inc(xT_copied[u], 1)

            def round_rests(pair, u):
                act.wait_ge(q_rest[u], pair + 1)
                act.activation(qparts[:, u, 1, :], qrest[:, u, :], ACT.Copy)
                act.wait_ge(rests[u], pair + 1)
                act.activation(kparts[:, u, 1, :], krest[:, u, :], ACT.Copy).then_inc(second_parts[u], 1)

            root(0, 2 * CH, 1)
            copy_xn(0, 0)
            def body(pair):
                for u in range(2):
                    if isinstance(pair, int) and (pair, u) == (0, 1):
                        root(2 * CH, TILES, 2)
                    if is_batch(*near(pair, u, 1)):
                        copy_xn(*near(pair, u, 1))
                    if is_batch(*near(pair, u, -1)):
                        round_rests(*near(pair, u, -1))
                    act.wait_ge(qkv_ready[u], pair + 1)
                    at_least(act, q_stored[u], pair * Q_STORES)
                    at_least(act, k_stored[u], pair * K_STORES)
                    act.activation(qparts[:, u, 0, :], psT[:, 2 * u, :], ACT.Copy, scale=SCALE)
                    act.activation(kparts[:, u, 0, :], psT[:, 2 * u + 1, :], ACT.Copy).then_inc(first_parts[u], 1)
                    act.activation(v_all[:, bass.ts(pair * 2 + u, CH), :].rearrange("p c d -> p (c d)"), ps_v[u][:, :], ACT.Copy)\
                        .then_inc(v_copied[u], 1)

            over_pairs(act, body)
            round_rests(BATCH // 2 - 1, 1)
            act.wait_ge(smallT, 2)
            act.wait_ge(gate_padded, 1)
            act.activation(gateT[:, 0:E], psS[:, 0, 0:E], ACT.Copy).then_inc(smallT_copied, 1)
            act.activation(b1T[:, :], psS[:, 0, E:E + E * FC], ACT.Copy).then_inc(smallT_copied, 1)

            def exps(s, n):
                i, h0, nh = PROB_TASKS[n]
                slot, cols = n % 2, T - i * P
                act.wait_ge(prob_ready[slot], s * (NPROB // 2) + n // 2 + 1)
                at_least(act, pv_done[i], s)
                src = psT[:, 2 * slot:2 * slot + 2, 0:cols] if i < 2 else \
                    psT[:, 2 * slot:2 * slot + 2, :].rearrange("p a n -> p (a n)")[:, 0:nh * cols]
                dst = PT[:, PT0[i] + h0 * cols:PT0[i] + (h0 + nh) * cols]
                if i == 1:
                    dst = dst.rearrange("p (a n) -> p a n", a=nh)
                elif i == 0:
                    src = src.rearrange("p a n -> p (a n)")
                act.activation(dst, src, ACT.Exp).then_inc(prob_done[slot], 1)

            def copy_heads(s, g):
                act.wait_ge(pv_done[CH - 1], s + 1)
                at_least(act, headsT_ready, s - 1)
                act.activation(Os[:, g % 2, :], psO[:, :], ACT.Copy).then_inc(heads_copied, 1)

            def copy_shift(s, b, g):
                act.wait_ge(shiftT_ready, s + 1)
                if b is not None:
                    act.wait_ge(shift_loaded[(g + 2) % GROUPS], (b + 1) * 16)
                act.activation(shiftT[:, g % 2, :], psM[0:SHIFTS, 0:T // 2].bitcast(BF16), ACT.Copy)\
                    .then_inc(shiftT_copied, 1)

            def copy_attention(b):
                act.wait_ge(attnT_ready, b + 1)
                at_least(act, o_ready, b)
                act.activation(xnT[:, 0, :], psM[:, :], ACT.Copy).then_inc(attnT_copied, 1)

            def copy_rows(b, bank):
                act.wait_ge(xn2T_ready, b + 1)
                at_least(act, scoresT_ready, b // (BATCH // HALVES))
                act.activation(rowsT[b % (BATCH // HALVES)], bank, ACT.Copy).then_inc(xn2T_copied, 1)

            def copy_scores(half, bank):
                act.wait_ge(scoresT_ready, half + 1)
                at_least(act, logits_ready, half)
                act.activation(scoresT[:, :], bank, ACT.Copy).then_inc(scoresT_copied, 1)

            def exp_logits(half):
                act.wait_ge(lg_done, half + 1)
                act.activation(pr[:, :, :], lg[:, :, :], ACT.Exp).then_inc(exp_done, 1)

            def step(b, g, first, last):
                s = b * GROUPS + g
                exps(s, 0)
                exps(s, 1)
                if not (first and g == 0):
                    copy_heads(s - 1, (g + 3) % GROUPS)
                if not (last and g == GROUPS - 1):
                    before = None if first and g == 0 else b - (1 if g == 0 else 0)
                    copy_shift(s + 1, before, (g + 1) % GROUPS)
                if at(b, g, RSTD):
                    root(0, HTILES, 3)
                if at(b, g, WEIGHTS):
                    exp_logits(0)
                for n in range(2, NPROB - 1):
                    exps(s, n)
                turned = isinstance(b, int) and TURN.get((b, g))
                if g == 0 and not first:
                    copy_attention(b - 1)
                if turned:
                    copy_rows(turned[0], psM[:, :])
                if at(b, g, GATE):
                    copy_scores(0, psM[:, :])
                exps(s, NPROB - 1)
                if turned:
                    copy_rows(turned[1], psM[:, :])

            copy_shift(0, None, 0)
            for g in range(GROUPS):
                step(0, g, True, False)
            with act.Fori(1, STATIC0) as b:
                for g in range(GROUPS):
                    step(b, g, False, False)
            for b in range(STATIC0, BATCH):
                for g in range(GROUPS):
                    step(b, g, False, b == BATCH - 1)
            copy_heads(STEPS - 1, GROUPS - 1)
            root(HTILES, EARLY, 4)
            copy_attention(BATCH - 1)
            copy_rows(4, psT[:, 0, :])
            copy_rows(5, psT[:, 1, :])
            root(EARLY, TILES, 5)
            copy_rows(6, psT[:, 2, :])
            copy_rows(7, psT[:, 3, :])
            copy_scores(1, psS[:, 0, :])
            exp_logits(1)

            def moe(half):
                def copy_xs(k, u):
                    k = half * (EVEN, ODD)[u] + k
                    act.wait_ge(xs_turned[u], k + 1)
                    at_least(act, h_ready[u], k)
                    act.activation(xsT[:, u, :], psS[:, u, 0:P], ACT.Copy).then_inc(xsT_copied[u], 1)

                def copy_w1(k, u, e):
                    k = half * (EVEN, ODD)[u] + k
                    at_least(act, h_ready[u], k)
                    act.activation(w1_t[:, u, :], w1_sb[:, bass.ds(e, 1), :].rearrange("p a f -> p (a f)"), ACT.Copy)\
                        .then_inc(w1_copied[u], 1)

                def relu(k, u, e):
                    k = half * (EVEN, ODD)[u] + k
                    act.wait_ge(h_ready[u], k + 1)
                    at_least(act, y_ready[u], k)
                    for c in range(FC // 2):
                        last = act.activation(hT[:, u, c * P:(c + 1) * P], psT[:, 2 * u, c * P:(c + 1) * P], ACT.Relu,
                                              bias=b1T[:, bass.ds(e * FC + c, 1)])
                    last.then_inc(relu_act[u], 1)

                act.wait_ge(routed, half + 1)
                es = experts(act, half, 0)
                for u in range(2):
                    copy_w1(0, u, es[u])
                for i in range(3):
                    copy_xs(i // 2, i % 2)
                relu(0, 0, es[0])
                copy_w1(1, 0, es[2])
                def body(k):
                    es = experts(act, half, k)
                    for n in range(ROUND):
                        i = k * ROUND + n
                        if there(i + 1):
                            relu(k * 2 + (n + 1) // 2, (n + 1) % 2, es[n + 1])
                        if there(i + 3):
                            copy_xs(k * 2 + (n + 3) // 2, (n + 3) % 2)
                            copy_w1(k * 2 + (n + 3) // 2, (n + 3) % 2, es[n + 3])

                turns_of(act, body)

            act.wait_ge(moe_in, (1 + 2 * E) * 16)
            for half in range(HALVES):
                moe(half)
            for b in range(BATCH // HALVES):
                act.wait_ge(results_loaded[b], 16)
                for t in range(b * CH, (b + 1) * CH):
                    last = act.activation(yg[1][:, t, 0, :], yg[1][:, t, 0, :], ACT.Copy, scale=wgt[:, 1, 0, t:t + 1])
                last.then_inc(best_weighed, 1)

        @block.tensor
        def _(pe):
            def turn_xn(pair, u):
                pe.wait_ge(xn_ready[u], pair + 1)
                at_least(pe, xT_copied[u], pair)
                for c in range(CH):
                    last = pe.transpose(psS[:, u, c * P:(c + 1) * P], xn[:, u, c, :], identf[:, :])
                last.then_inc(xT_ready[u], 1)

            pe.wait_ge(consts, 3)
            turn_xn(0, 0)
            pe.wait_ge(wperm, 2)
            pe.wait_ge(w_in, 3 * 16)
            def body(pair):
                for u in range(2):
                    if is_batch(*near(pair, u, 1)):
                        turn_xn(*near(pair, u, 1))
                    pe.wait_ge(xT_copied[u], pair + 1)
                    at_least(pe, rests[u], pair)
                    at_least(pe, v_copied[u], pair)
                    pe.matmul(psT[:, 2 * u, :], wqp[:, :], xnT[:, u, :], start=True, stop=True)
                    pe.matmul(psT[:, 2 * u + 1, :], wkp[:, :], xnT[:, u, :], start=True, stop=True)
                    for c in range(CH):
                        last = pe.matmul(ps_v[u][:, c * P:(c + 1) * P], xnT[:, u, c * P:(c + 1) * P], wv_sb[:, :],
                                         start=True, stop=True)
                    last.then_inc(qkv_ready[u], 1)

            over_pairs(pe, body)

            for u in range(2):
                pe.wait_ge(v_copied[u], BATCH // 2)
                pe.wait_ge(rests[u], BATCH // 2)
            pe.wait_ge(gate_in, 2 * 16)
            pe.wait_ge(wo_in, 2 * 16)
            pe.wait_ge(sort_consts, 5)
            pe.transpose(psS[:, 0, 0:E], gate_rows[:, :], identf[0:E, 0:E]).then_inc(smallT, 1)
            pe.transpose(psS[:, 0, E:E + E * FC], b1_rows[:, :], identf[0:E * FC, 0:E * FC]).then_inc(smallT, 1)
            pe.wait_ge(smallT_copied, 2)

            def scores(s, b, g, a):
                slot = a % 2
                at_least(pe, scores_used[slot], s * (NSCORE // 2) + a // 2)
                if a == 0:
                    pe.wait_ge(qk_loaded[g], (b + 1) * QK_LOADS)
                for j, h, c0 in SCORE_TASKS[a]:
                    n = (j + 1) * P
                    pe.matmul(psS[:, slot, c0:c0 + n], Qs[0:QK_ROWS, g, h, j * P:n], Ks[0:QK_ROWS, g, h, 0:n],
                              start=True, stop=False)
                    last = pe.matmul(psS[:, slot, c0 + n - P:c0 + n], identb[:, :], mask_qk[:, :], start=False, stop=True)
                last.then_inc(scores_ready[slot], 1)

            def probs(s, b, g, n):
                i, h0, nh = PROB_TASKS[n]
                slot, cols = n % 2, T - i * P
                at_least(pe, prob_done[slot], s * (NPROB // 2) + n // 2)
                if n == 0:
                    pe.wait_ge(shift_loaded[g], (b + 1) * 16)
                for k in range(nh):
                    h = h0 + k
                    bank, c0 = (k, 0) if i < 2 else (k * cols // 512, k * cols % 512)
                    reg = psT[:, 2 * slot + bank, c0:c0 + cols]
                    last = pe.matmul(reg, Ks[0:ST_ROWS, g, h, i * P:(i + 1) * P], Qs[0:ST_ROWS, g, h, i * P:T],
                                     start=True, stop=True)
                last.then_inc(prob_ready[slot], 1)

            def weigh(s, g, i):
                pe.wait_ge(masked, s * CH + i + 1)
                if i == 0:
                    at_least(pe, heads_copied, s)
                    pe.wait_ge(v_loaded, s + 1)
                cols = T - i * P
                for h in range(GH):
                    c0 = PT0[i] + h * cols
                    last = pe.matmul(psO[h * VW:(h + 1) * VW, i * P:T], Vs[:, g, i, h, :], PT[:, c0:c0 + cols],
                                     start=(i == 0), stop=(i == CH - 1))
                last.then_inc(pv_done[i], 1)

            def turn_shift(s, b, g):
                pe.wait_ge(shift_split[g % 2], b * 2 + g // 2 + 1)
                at_least(pe, normed, s - 2)
                for j in range(CH):
                    last = pe.transpose(psM[0:SHIFTS, j * P // 2:(j + 1) * P // 2].bitcast(BF16),
                                        nparts[:, g % 2, j, :, :].rearrange("p i h -> p (i h)"), identb[:, :])
                last.then_inc(shiftT_ready, 1)

            def turn_heads(s, g, copied):
                pe.wait_ge(heads_copied, s + 1)
                at_least(pe, normed, s)
                pe.wait_ge(shiftT_copied, copied)
                for j in range(CH):
                    last = pe.transpose(psM[:, j * P:(j + 1) * P], Os[:, g % 2, j * P:(j + 1) * P], identf[:, :])
                last.then_inc(headsT_ready, 1)

            def turn_attention(b):
                pe.wait_ge(normed, (b + 1) * GROUPS)
                for c in range(CH):
                    last = pe.transpose(psM[:, c * P:(c + 1) * P], attn[:, c, :], identf[:, :])
                last.then_inc(attnT_ready, 1)

            def project(b):
                pe.wait_ge(attnT_copied, b + 1)
                for c in range(CH):
                    last = pe.matmul(psM[:, c * P:(c + 1) * P], xnT[:, 0, c * P:(c + 1) * P], wo_sb[:, :],
                                     start=True, stop=True)
                last.then_inc(o_ready, 1)

            def turn_rows(b, bank):
                pe.wait_ge(xn2_ready, b + 1)
                for c in range(CH):
                    last = pe.transpose(bank[:, c * P:(c + 1) * P], xn2[:, b * CH + c, 0:D], identf[:, :])
                last.then_inc(xn2T_ready, 1)

            def score_experts(half, bank):
                pe.wait_ge(xn2T_copied, (half + 1) * (BATCH // HALVES))
                for i, rows in enumerate(rowsT):
                    last = pe.matmul(bank[i * 32:(i + 1) * 32, :], gateT[:, :], rows, start=True, stop=True)
                last.then_inc(scoresT_ready, 1)

            def turn_scores(half):
                pe.wait_ge(scoresT_copied, half + 1)
                for c in range(CH):
                    last = pe.transpose(psM[:, c * P:(c + 1) * P], scoresT[:, c * P:(c + 1) * P], identf[:, :])
                last.then_inc(logits_ready, 1)

            def count_rows(half):
                pe.wait_ge(picks_done, half + 1)
                pk = picks[:, :, :].rearrange("p e t -> p (e t)")
                pe.matmul(psM[:, 0:E * HTILES], tri[:, :], pk, start=True, stop=True)
                pe.matmul(psM[:, E * HTILES:2 * E * HTILES], onesb[:, :], pk, start=True, stop=True).then_inc(ranks_ready, 1)

            def step(b, g, first, last):
                s = b * GROUPS + g
                ahead = (s + 2, b + (g + 2) // GROUPS, (g + 2) % GROUPS)
                more = not (last and g >= 2)
                before = not (first and g == 0)
                nxt = not (last and g == GROUPS - 1)
                turned = isinstance(b, int) and TURN.get((b, g))

                def sc(*tasks):
                    if more:
                        for a in tasks:
                            scores(*ahead, a)

                probs(s, b, g, 0)
                sc(0)
                if before:
                    weigh(s - 1, (g + 3) % GROUPS, 3)
                probs(s, b, g, 1)
                sc(1)
                if g == 1 and not first:
                    pe.wait_ge(x2_done, b)
                for step_before, batches in TURN.items():
                    if at(b, g - 1, step_before):
                        pe.wait_ge(xn2T_copied, batches[1] + 1)
                if at(b, g - 1, GATE):
                    pe.wait_ge(logits_kept, 1)
                if at(b, g - 1, COUNT):
                    pe.wait_ge(ranks_kept, 1)
                if nxt:
                    turn_shift(s + 1, b + (g + 1) // GROUPS, (g + 1) % GROUPS)
                sc(2)
                probs(s, b, g, 2)
                sc(3)
                probs(s, b, g, 3)
                sc(4)
                weigh(s, g, 0)
                if before:
                    turn_heads(s - 1, (g + 3) % GROUPS, s + 2 if nxt else s + 1)
                probs(s, b, g, 4)
                sc(5)
                weigh(s, g, 1)
                if g == 0 and not first:
                    turn_attention(b - 1)
                if turned:
                    pe.wait_ge(normed, s)
                    turn_rows(turned[0], psM[:, :])
                if at(b, g, GATE):
                    pe.wait_ge(normed, s)
                    score_experts(0, psM[:, :])
                sc(6)
                probs(s, b, g, 5)
                sc(7)
                weigh(s, g, 2)
                sc(8)
                if g == 0 and not first:
                    project(b - 1)
                if turned:
                    pe.wait_ge(xn2T_copied, turned[0] + 1)
                    turn_rows(turned[1], psM[:, :])
                if at(b, g, GATE):
                    turn_scores(0)
                if at(b, g, COUNT):
                    pe.wait_ge(normed, s)
                    count_rows(0)
                sc(9)

            for a in range(NSCORE):
                scores(0, 0, 0, a)
            for a in range(NSCORE):
                scores(1, 0, 1, a)
                if a == 2:
                    turn_shift(0, 0, 0)
            for g in range(GROUPS):
                step(0, g, True, False)
            with pe.Fori(1, STATIC0) as b:
                for g in range(GROUPS):
                    step(b, g, False, False)
            for b in range(STATIC0, BATCH):
                for g in range(GROUPS):
                    step(b, g, False, b == BATCH - 1)
            weigh(STEPS - 1, GROUPS - 1, 3)
            turn_heads(STEPS - 1, GROUPS - 1, STEPS)
            turn_attention(BATCH - 1)
            turn_rows(4, psT[:, 0, :])
            project(BATCH - 1)
            turn_rows(5, psT[:, 1, :])
            turn_rows(6, psT[:, 2, :])
            turn_rows(7, psT[:, 3, :])
            score_experts(1, psS[:, 0, :])
            pe.wait_ge(x2_done, BATCH)
            turn_scores(1)
            pe.wait_ge(logits_kept, 2)
            count_rows(1)
            pe.wait_ge(ranks_kept, HALVES)

            def moe(half):
                def turn_xs(k, n):
                    u = n % 2
                    pe.wait_ge(xs_loaded[n], (-(-(SLOTS - n) // ROUND) * half + k + 1) * 16)
                    at_least(pe, xsT_copied[u], half * (EVEN, ODD)[u] + k * 2 + n // 2)
                    pe.transpose(psS[:, u, 0:P], xs_t[:, n, 0:D], identf[:, :]).then_inc(xs_turned[u], 1)

                def expand(k, u):
                    k = half * (EVEN, ODD)[u] + k
                    pe.wait_ge(xsT_copied[u], k + 1)
                    pe.wait_ge(w1_copied[u], k + 1)
                    at_least(pe, relu_act[u], k)
                    at_least(pe, relu_dve[u], k)
                    for c in range(FC):
                        bank, c0 = 2 * u + c // (FC // 2), c % (FC // 2) * P
                        last = pe.matmul(psT[:, bank, c0:c0 + P], w1_t[:, u, c * P:(c + 1) * P], xsT[:, u, :],
                                         start=True, stop=True)
                    last.then_inc(h_ready[u], 1)

                def contract(k, u, e):
                    k = half * (EVEN, ODD)[u] + k
                    pe.wait_ge(relu_act[u], k + 1)
                    pe.wait_ge(relu_dve[u], k + 1)
                    at_least(pe, y_copied[u], k)
                    for c in range(FC):
                        last = pe.matmul(ps_v[u][:, 0:D], hT[:, u, c * P:(c + 1) * P],
                                         w2_sb[:, bass.ds(e, 1), c, :].rearrange("p a d -> p (a d)"),
                                         start=(c == 0), stop=(c == FC - 1))
                    last.then_inc(y_ready[u], 1)

                pe.wait_ge(routed, half + 1)
                for i in range(3):
                    turn_xs(0, i)
                expand(0, 0)
                def body(k):
                    es = experts(pe, half, k)
                    for n in range(ROUND):
                        i = k * ROUND + n
                        if there(i + 1):
                            expand(k * 2 + (n + 1) // 2, (n + 1) % 2)
                        if there(i):
                            contract(k * 2 + n // 2, n % 2, es[n])
                        if there(i + 3):
                            turn_xs(k + (n + 3) // ROUND, (n + 3) % ROUND)

                turns_of(pe, body)

            pe.wait_ge(moe_in, (1 + 2 * E) * 16)
            for half in range(HALVES):
                moe(half)

        @block.vector
        def _(dve):
            links = [0]

            def link(ins):
                links[0] += 1
                ins.then_inc(ln, 1)
                dve.wait_ge(ln, links[0])

            def row_stats(t0, t1):
                st, m = stats[:, t0:t1, :], mean[:, t0:t1]
                diff, sq, both, var = (lnt[:, i, t0:t1] for i in range(4))
                link(dve.tensor_tensor(diff, st[:, :, 1], st[:, :, 4], ALU.subtract))
                dve.tensor_tensor(m, st[:, :, 1], st[:, :, 4], ALU.add)
                link(dve.tensor_tensor(sq, diff, diff, ALU.mult))
                link(dve.tensor_tensor(both, st[:, :, 2], st[:, :, 5], ALU.add))
                link(dve.tensor_scalar(sq, sq, 0.25, EPS, ALU.mult, ALU.add))
                link(dve.tensor_scalar(m, m, 0.5, None, ALU.mult))
                dve.scalar_tensor_tensor(var, both, 1.0 / D, sq, ALU.mult, ALU.add).then_inc(var_done, 1)

            def invert(t0, t1, n):
                dve.wait_ge(std_done, n)
                link(dve.reciprocal(rstd[:, t0:t1], rstd[:, t0:t1]))

            dve.wait_ge(const_step, 7)
            for g in range(GROUPS // 2, GROUPS):
                dve.tensor_copy(Ks[96:128, g, :, :], own[96:128, :].unsqueeze(2).to_broadcast([32, GH, T])).then_inc(slots_set, 1)

            def x_stats(batches):
                for b in batches:
                    dve.wait_ge(x_in[b], 16)
                    for t in range(b * CH, (b + 1) * CH):
                        last = dve.bn_stats(stats[:, t, :], x_all[:, t, :])
                link(last)
                row_stats(batches[0] * CH, (batches[-1] + 1) * CH)

            def first_norm(pair, u):
                b = pair * 2 + u
                at_least(dve, xT_ready[u], pair)
                for c in range(CH):
                    t = b * CH + c
                    last = dve.tensor_scalar(xn[:, u, c, :], x_all[:, t, :], mean[:, bass.ds(t, 1)],
                                             rstd[:, bass.ds(t, 1)], ALU.subtract, ALU.mult)
                last.then_inc(xn_ready[u], 1)

            def third_q(pair, u):
                dve.wait_ge(second_parts[u], pair + 1)
                dve.tensor_tensor(qparts[:, u, 2, :], qrest[:, u, :], qparts[:, u, 1, :], ALU.subtract)\
                    .then_inc(qsplit_done[u], 1)

            x_stats([0, 1])
            invert(0, 2 * CH, 1)
            first_norm(0, 0)
            dve.wait_ge(w_in, 3 * 16)
            for dst, src in ((wqp, wq_sb), (wkp, wk_sb)):
                dve.tensor_copy(dst[:, :].rearrange("p (g d h) -> p g d h", g=GROUPS, h=GH),
                                src[:, :].rearrange("p (g h d) -> p g d h", g=GROUPS, h=GH)).then_inc(wperm, 1)
            first_norm(0, 1)
            x_stats(range(2, BATCH))

            def body(pair):
                for u in range(2):
                    start = isinstance(pair, int) and (pair, u) == (0, 0)
                    if is_batch(*near(pair, u, 2)) and not start:
                        first_norm(*near(pair, u, 2))
                    if is_batch(*near(pair, u, -1)):
                        third_q(*near(pair, u, -1))
                    dve.wait_ge(first_parts[u], pair + 1)
                    at_least(dve, ksplit_done[u], pair)
                    dve.scalar_tensor_tensor(qrest[:, u, :], psT[:, 2 * u, :], SCALE, qparts[:, u, 0, :], ALU.mult, ALU.subtract)\
                        .then_inc(q_rest[u], 1)
                    dve.tensor_tensor(krest[:, u, :], psT[:, 2 * u + 1, :], kparts[:, u, 0, :], ALU.subtract)\
                        .then_inc(rests[u], 1)
                    if start:
                        invert(2 * CH, TILES, 2)
                        first_norm(1, 0)

            over_pairs(dve, body)
            third_q(BATCH // 2 - 1, 1)
            dve.wait_ge(xb_done, BATCH)
            dve.wait_ge(iotas, 5)
            dve.wait_ge(sort_consts, 5)
            link(dve.tensor_copy(cst[:, :], ints[:, :]))
            dve.tensor_copy(xn2[:, :, TOKEN], token2i[:, 0:TILES])
            dve.memset(pad_row[:, BEST:], 1.0)
            dve.tensor_copy(pad_row[:, TOKEN:BEST], token2i[:, TILES:]).then_inc(tokens_set, 1)

            def maxima(s, b, g, tasks):
                par = g % 2
                for a in tasks:
                    slot = a % 2
                    if a == 0:
                        at_least(dve, shift_split[par], b * 2 + g // 2)
                    dve.wait_ge(scores_ready[slot], s * (NSCORE // 2) + a // 2 + 1)
                    if SCORE_TASKS[a][0][0] == 1:
                        h = SCORE_TASKS[a][0][1]
                        last = dve.tensor_reduce(nmax[:, par, 1, h:h + 2],
                                                 psS[:, slot, :].rearrange("p (h n) -> p h n", h=2),
                                                 AX_X, ALU.max, negate=True)
                    else:
                        for j, h, c0 in SCORE_TASKS[a]:
                            last = dve.tensor_reduce(nmax[:, par, j, h:h + 1], psS[:, slot, c0:c0 + (j + 1) * P],
                                                     AX_X, ALU.max, negate=True)
                    last.then_inc(scores_used[slot], 1)

            def norm(s, b, g):
                dve.wait_ge(headsT_ready, s + 1)
                o = psM[:, :].rearrange("p (j h v) -> p j h v", j=CH, h=GH)
                dve.reciprocal(rsum[:, :, :], o[:, :, :, HD]).then_inc(rsum_done, 1)
                dve.wait_ge(rsum_done, s + 1)
                if g == 0:
                    at_least(dve, attnT_ready, b)
                dst = attn[:, :, g * 32:(g + 1) * 32].rearrange("p j (h d) -> p j h d", h=GH)
                dve.tensor_tensor(dst, o[:, :, :, 0:HD], rsum[:, :, :].unsqueeze(3).to_broadcast([P, CH, GH, HD]),
                                  ALU.mult).then_inc(normed, 1)

            def add_attention(b):
                dve.wait_ge(o_ready, b + 1)
                xs = x_all[:, bass.ts(b, CH), :]
                dve.tensor_tensor(xs, psM[:, :].rearrange("p (c d) -> p c d", c=CH), xs, ALU.add).then_inc(x2_done, 1)

            def batch_stats(b):
                dve.wait_ge(x2_done, b + 1)
                for c in range(CH):
                    t = b * CH + c
                    last = dve.bn_stats(stats[:, bass.ds(t, 1), :].rearrange("p a s -> p (a s)"), x_all[:, t, :])
                last.then_inc(stats_done, 1)

            def normalise(b):
                for t in range(b * CH, (b + 1) * CH):
                    last = dve.tensor_scalar(xn2[:, t, 0:D], x_all[:, t, :], mean[:, t:t + 1], rstd[:, t:t + 1],
                                             ALU.subtract, ALU.mult)
                last.then_inc(xn2_ready, 1)

            def keep_logits(half):
                dve.wait_ge(logits_ready, half + 1)
                dve.tensor_copy(lg[:, :, :].rearrange("p (b c) e -> p b c e", c=CH),
                                psM[:, :].rearrange("p (c b e) -> p b c e", c=CH, b=BATCH // HALVES)[:, :, :, 0:E])\
                    .then_inc(logits_kept, 1)
                dve.wait_ge(logits_kept, half + 1)

            def wide(v, n=E):
                return v.unsqueeze(2).to_broadcast([P, v.shape[1], n])

            def across(v, n=HTILES):
                return v.unsqueeze(1).to_broadcast([P, n, v.shape[1]])

            def best_score(half):
                keep_logits(half)
                link(dve.tensor_reduce(rmax[:, :], lg[:, :, :], AX_X, ALU.max))
                dve.tensor_tensor(lg[:, :, :], lg[:, :, :], wide(rmax[:, :]), ALU.subtract).then_inc(lg_done, 1)
                dve.wait_ge(lg_done, half + 1)

            def best_expert(half):
                link(dve.tensor_scalar(rt[:, :, :], lg[:, :, :], 0.0, None, ALU.is_equal))
                pick_first(oh1)
                dve.tensor_copy(xn2[:, half * HTILES:(half + 1) * HTILES, BEST], rz[:, :])

            def second_score(half):
                link(dve.scalar_tensor_tensor(rest[:, :, :], oh1[:, :, :], NEG, lg[:, :, :], ALU.mult, ALU.add))
                link(dve.tensor_reduce(rmax[:, :], rest[:, :, :], AX_X, ALU.max))

            def second_expert(half):
                link(dve.tensor_tensor(rt[:, :, :], rest[:, :, :], wide(rmax[:, :]), ALU.is_equal))
                pick_first(oh2)
                dve.tensor_tensor(picks[:, :, :].rearrange("p e t -> p t e"), oh1[:, :, :], oh2[:, :, :], ALU.add)\
                    .then_inc(picks_done, 1)

            def pick_first(oh):
                link(dve.tensor_tensor(rt[:, :, :], rt[:, :, :], across(back), ALU.mult))
                link(dve.tensor_reduce(rz[:, :], rt[:, :, :], AX_X, ALU.min))
                link(dve.tensor_tensor(oh[:, :, :], across(back), wide(rz[:, :]), ALU.is_equal))

            def keep_ranks(half):
                dve.wait_ge(ranks_ready, half + 1)
                dve.tensor_copy(rank[:, :, :].rearrange("p e t -> p (e t)"), psM[:, 0:E * HTILES])
                last = dve.tensor_copy(tot[:, :, :].rearrange("p e t -> p (e t)"), psM[:, E * HTILES:2 * E * HTILES])
                last.then_inc(ranks_kept, 1)
                dve.wait_ge(ranks_kept, half + 1)

            def weights(half):
                dve.wait_ge(exp_done, half + 1)
                link(dve.tensor_reduce(rz[:, :], pr[:, :, :], AX_X, ALU.add))
                link(dve.reciprocal(rz[:, :], rz[:, :]))
                for k, oh in enumerate((oh1, oh2)):
                    link(dve.tensor_tensor(rt[:, :, :], oh[:, :, :], pr[:, :, :], ALU.mult))
                    link(dve.tensor_reduce(rmax[:, :], rt[:, :, :], AX_X, ALU.add))
                    link(dve.tensor_tensor(wgt[:, half, k, :], rmax[:, :], rz[:, :], ALU.mult))

            def rank_rows(half):
                flat = [v[:, :, :].rearrange("p e t -> p (e t)") for v in (tot, inc, resets)]
                link(dve.tensor_tensor_scan(flat[1], flat[2], flat[0], 0.0, ALU.mult, ALU.add))
                link(dve.tensor_tensor(need[:, :, :], wide(inc[:, :, HTILES - 1], HTILES), across(starts, E), ALU.is_gt))
                link(dve.tensor_reduce(nt[:, :], need[:, :, :], AX_X, ALU.add))
                link(dve.tensor_tensor_scan(ends[:, :], ones_e[:, :], nt[:, :], 0.0, ALU.mult, ALU.add))
                link(dve.tensor_tensor(base[:, :], ends[:, :], nt[:, :], ALU.subtract))
                link(dve.tensor_scalar(base[:, :], base[:, :], float(P), None, ALU.mult))

            def ranks_to_places(half):
                link(dve.tensor_tensor(inc[:, :, :], inc[:, :, :], tot[:, :, :], ALU.subtract))
                link(dve.tensor_tensor(pos[:, :, :], rank[:, :, :], inc[:, :, :], ALU.add))
                link(dve.tensor_tensor(pos[:, :, :], pos[:, :, :], wide(base[:, :], HTILES), ALU.add))

            def place_rows(half, k):
                link(dve.tensor_tensor(rt[:, :, :], (oh1, oh2)[k][:, :, :], pos[:, :, :].rearrange("p e t -> p t e"), ALU.mult))
                link(dve.tensor_reduce(dstf[:, :], rt[:, :, :], AX_X, ALU.add))
                dve.tensor_copy(place[:, half, k, :], dstf[:, :]).then_inc(placed, 1)
                dve.wait_ge(placed, half * TOPK + k + 1)

            def find_experts(half):
                link(dve.tensor_tensor(past[:, :, :], wide(slot_no), across(ends[:, :], SLOTS_UP), ALU.is_ge))
                link(dve.tensor_reduce(eidf[:, :], past[:, :, :], AX_X, ALU.add))
                link(dve.tensor_scalar(eidf[:, :], eidf[:, :], float(E - 1), None, ALU.min))
                dve.tensor_scalar(slot_expert[:, half, :], eidf[:, :], float(-E), None, ALU.add)

            def pack_experts(half):
                digit = [eidf[:, n:n + ROUND * ROUNDS].rearrange("p (k n) -> p k n", n=ROUND)[:, :, 0]
                         for n in range(DIGITS)]
                link(dve.scalar_tensor_tensor(packed[:, :], digit[-1], float(E), digit[-2], ALU.mult, ALU.add))
                for d in reversed(digit[:-2]):
                    link(dve.scalar_tensor_tensor(packed[:, :], packed[:, :], float(E), d, ALU.mult, ALU.add))
                dve.tensor_copy(turns[:, half, :], packed[:, :]).then_inc(routed, 1)

            def step(b, g, first, last):
                s = b * GROUPS + g
                ahead = (s + 2, b + (g + 2) // GROUPS, (g + 2) % GROUPS)
                more = not (last and g >= 2)
                if g == 1 and not first:
                    add_attention(b - 1)
                if at(b, g, KEEP):
                    best_score(0)
                if at(b, g - 1, COUNT):
                    keep_ranks(0)
                if more:
                    maxima(*ahead, range(3))
                if at(b, g, (STATIC0 + 2, 1)):
                    second_score(0)
                if at(b, g, (STATIC0 + 2, 2)):
                    rank_rows(0)
                if at(b, g, (STATIC0 + 2, 3)):
                    place_rows(0, 0)
                if at(b, g, (STATIC0 + 3, 0)):
                    find_experts(0)
                if more:
                    maxima(*ahead, range(3, 5))
                if not (first and g == 0):
                    norm(s - 1, b - (1 if g == 0 else 0), (g + 3) % GROUPS)
                if at(b, g, STATS):
                    dve.wait_ge(stats_done, BATCH // HALVES)
                    row_stats(0, HTILES)
                if at(b, g, RSTD):
                    invert(0, HTILES, 3)
                    normalise(0)
                if at(b, g, min(TURN)):
                    normalise(2)
                if at(b, g, KEEP):
                    best_expert(0)
                if at(b, g, (STATIC0 + 2, 1)):
                    second_expert(0)
                if more:
                    maxima(*ahead, range(5, 8))
                if at(b, g, RSTD):
                    normalise(1)
                if at(b, g, min(TURN)):
                    normalise(3)
                if at(b, g, (STATIC0 + 2, 2)):
                    ranks_to_places(0)
                if at(b, g, (STATIC0 + 2, 3)):
                    place_rows(0, 1)
                if at(b, g, (STATIC0 + 3, 0)):
                    pack_experts(0)
                if more:
                    maxima(*ahead, range(8, NSCORE))
                if g == 2 and not first:
                    batch_stats(b - 1)
                    if last:
                        dve.wait_ge(stats_done, BATCH - 1)
                        row_stats(HTILES, EARLY)
                if at(b, g, WEIGHTS):
                    weights(0)

            maxima(0, 0, 0, range(NSCORE))
            maxima(1, 0, 1, range(NSCORE))
            for g in range(GROUPS):
                step(0, g, True, False)
            with dve.Fori(1, STATIC0) as b:
                for g in range(GROUPS):
                    step(b, g, False, False)
            for b in range(STATIC0, BATCH):
                for g in range(GROUPS):
                    step(b, g, False, b == BATCH - 1)
            norm(STEPS - 1, BATCH - 1, GROUPS - 1)
            invert(HTILES, EARLY, 4)
            normalise(4)
            normalise(5)
            add_attention(BATCH - 1)
            batch_stats(BATCH - 1)
            dve.wait_ge(stats_done, BATCH)
            row_stats(EARLY, TILES)
            normalise(6)
            invert(EARLY, TILES, 5)
            normalise(7)
            best_score(1)
            best_expert(1)
            second_score(1)
            second_expert(1)
            keep_ranks(1)
            rank_rows(1)
            ranks_to_places(1)
            for k in range(TOPK):
                place_rows(1, k)
            find_experts(1)
            pack_experts(1)

            def moe(half):
                def relu(k, u, e):
                    k = half * (EVEN, ODD)[u] + k
                    dve.wait_ge(h_ready[u], k + 1)
                    at_least(dve, y_ready[u], k)
                    for c in range(FC // 2, FC):
                        c0 = (c - FC // 2) * P
                        last = dve.tensor_scalar(hT[:, u, c * P:(c + 1) * P], psT[:, 2 * u + 1, c0:c0 + P],
                                                 b1T[:, bass.ds(e * FC + c, 1)], 0.0, ALU.add, ALU.max)
                    last.then_inc(relu_dve[u], 1)

                def copy_y(k, u, e):
                    dve.wait_ge(y_ready[u], half * (EVEN, ODD)[u] + k + 1)
                    if half == 0:
                        at_least(dve, y_stored[u], k * 16)
                    elif isinstance(k, int) and k == 0:
                        dve.wait_ge(y_stored[u], (EVEN, ODD)[u] * 16)
                    else:
                        dve.wait_ge(y_scattered[u], k * 16)
                    dve.tensor_tensor(y_t[:, u, :], ps_v[u][:, 0:D], b2_b[:, bass.ts(e, D)], ALU.add)\
                        .then_inc(y_copied[u], 1)

                def find_rows(k, n):
                    dve.wait_ge(xs_loaded[n], (-(-(SLOTS - n) // ROUND) + k + 1) * 16)
                    dve.scalar_tensor_tensor(y_row[:, n:n + 1], xs_t[:, n, BEST:XW],
                                             slot_expert[:, 1, bass.ds(k * ROUND + n, 1)], xs_t[:, n, TOKEN:BEST],
                                             ALU.not_equal, ALU.add).then_inc(row_found, 1)

                es = experts(dve, half, 0)
                if half:
                    find_rows(0, 0)
                    find_rows(0, 1)
                relu(0, 0, es[0])
                def body(k):
                    es = experts(dve, half, k)
                    sums = half == 1 and not (isinstance(k, int) and not 1 <= k <= HTILES // 2)
                    for n in range(ROUND):
                        i = k * ROUND + n
                        if there(i + 1):
                            relu(k * 2 + (n + 1) // 2, (n + 1) % 2, es[n + 1])
                        if sums:
                            dve.wait_ge(gathered[n], k * 16)
                        if there(i):
                            copy_y(k * 2 + n // 2, n % 2, es[n])
                        if half and there(i + 2):
                            find_rows(k + (n + 2) // ROUND, (n + 2) % ROUND)
                        if half == 0 and isinstance(k, int) and i == 2:
                            weights(1)
                        if sums and n in (1, 3):
                            combine(0, k * 2 - 2 + n // 2)

                turns_of(dve, body)

            def combine(half, t):
                tile = half * HTILES + t
                xt = x_all[:, bass.ds(tile, 1), :].rearrange("p a d -> p (a d)")
                results = [yg[half][:, bass.ds(t, 1), k, :].rearrange("p a d -> p (a d)") for k in range(TOPK)]
                dve.scalar_tensor_tensor(xt, results[0], wgt[:, half, 0, bass.ds(t, 1)], xt, ALU.mult, ALU.add).then_inc(best_added, 1)
                dve.wait_ge(best_added, tile + 1)
                dve.scalar_tensor_tensor(xt, results[1], wgt[:, half, 1, bass.ds(t, 1)], xt, ALU.mult, ALU.add).then_inc(combined, 1)

            dve.wait_ge(moe_in, (1 + 2 * E) * 16)
            for half in range(HALVES):
                moe(half)
            for b in range(BATCH // HALVES):
                dve.wait_ge(best_batches, b + 1)
                for t in range(b * CH, (b + 1) * CH):
                    xt = x_all[:, HTILES + t, :]
                    dve.scalar_tensor_tensor(xt, yg[1][:, t, 1, :], wgt[:, 1, 1, t:t + 1], xt, ALU.mult, ALU.add)\
                        .then_inc(combined, 1)


_INS = ["L0_attn_x", "L0_attn_Wq", "L0_attn_Wk", "L0_attn_Wv", "L0_attn_Wo", "L0_attn_bo",
        "L0_ffn_gate_w", "L0_ffn_w1", "L0_ffn_b1", "L0_ffn_w2", "L0_ffn_b2"]
_OUTS = [((BATCH, T, D), "float32")]


def kernel(**inputs):
    import numpy as np
    import concourse.bacc as bacc
    from concourse.bass_utils import run_bass_kernel_spmd

    nc = bacc.Bacc("TRN2", target_bir_lowering=False, num_devices=1)
    arrays, args = {}, []
    for name in _INS:
        a = np.ascontiguousarray(inputs[name])
        arrays[f"in_{name}"] = a
        args.append(nc.dram_tensor(f"in_{name}", a.shape, mybir.dt.from_np(a.dtype), kind="ExternalInput").ap())
    for i, (shape, dtype) in enumerate(_OUTS):
        args.append(nc.dram_tensor(f"out_{i}", shape, mybir.dt.from_np(np.dtype(dtype)), kind="ExternalOutput").ap())
    layer(nc, *args)
    r = run_bass_kernel_spmd(nc, [arrays], core_ids=[0])
    return r.results[0]["out_0"]
```
